# Optimizing a Trainium2 kernel written in Bass

```python
import numpy as np
import jax
import jax.numpy as jnp

def _softmax(x, axis=-1):
    return jax.nn.softmax(x, axis=axis)

def _gelu(x):
    return jax.nn.gelu(x, approximate=True)

def _silu(x):
    return jax.nn.silu(x)

def _sigmoid(x):
    return jax.nn.sigmoid(x)

def _layernorm(x, axis=-1, eps=1e-05):
    m = jnp.mean(x, axis=axis, keepdims=True)
    v = jnp.var(x, axis=axis, keepdims=True)
    return (x - m) / jnp.sqrt(v + eps)

def _scatter_add(tgt, idx, src, axis=0):
    return tgt.at[idx].add(src)

def _segment_sum(src, seg, n):
    return jax.ops.segment_sum(src, seg, n)
kernel_name = 'mk_gps_d2_gnn_r16_a771d1'

def setup_inputs(seed: int=0):
    np.random.seed(seed)
    _w = jnp.asarray

    def _rec_inputs():
        import jax
        import jax.numpy as jnp
        _gk = jax.random.key(seed)
        x = -6.415e-05 + 1 * jax.random.normal(jax.random.fold_in(_gk, 1), (625, 1024), jnp.float32)
        src = jax.random.randint(jax.random.fold_in(_gk, 2), (20000,), 0, 625, jnp.int32)
        dst = jnp.minimum((625 * jax.random.uniform(jax.random.fold_in(_gk, 3), (20000,)) ** 2.0).astype(jnp.int32), 9999)
        _o = jnp.argsort(dst, stable=True)
        src = src[_o]
        dst = dst[_o]
        edge_type_8 = jax.random.randint(jax.random.fold_in(_gk, 12), (20000,), 0, 8, jnp.int32)
        return (x, src, dst, edge_type_8)
    x, src, dst, edge_type_8 = _rec_inputs()

    def _L0_gnn_setup():
        import jax, jax.numpy as jnp
        import numpy as np
        N, D, R, E = (625, 1024, 8, 5000)

        def _rgcn(x, edge_index, edge_type, weight, root, bias):
            src, dst = (edge_index[0], edge_index[1])
            msgs = x[src]
            out = x @ root + bias
            n = x.shape[0]
            for r in range(weight.shape[0]):
                mask = (edge_type == r).astype(x.dtype)
                sums = jax.ops.segment_sum(msgs * mask[:, None], dst, num_segments=n)
                cnt = jax.ops.segment_sum(mask, dst, num_segments=n)
                mean = sums / jnp.maximum(cnt, 1.0)[:, None]
                out = out + mean @ weight[r]
            return out
        key = jax.random.key(seed)
        ks = jax.random.split(key, 8)
        s = 1.0 / np.sqrt(D)
        x = jax.random.normal(ks[0], (N, D), dtype=jnp.float32)
        edge_index = jax.random.randint(ks[1], (2, E), 0, N, dtype=jnp.int64)
        edge_type = jax.random.randint(ks[2], (E,), 0, R, dtype=jnp.int64)
        weight = jax.random.normal(ks[3], (R, D, D), dtype=jnp.float32) * s
        root = jax.random.normal(ks[4], (D, D), dtype=jnp.float32) * s
        bias = jnp.zeros((D,), dtype=jnp.float32)
        w_gate = jax.random.normal(ks[5], (2 * D, D), dtype=jnp.float32) * (1.0 / np.sqrt(2 * D))
        b_gate = jnp.zeros((D,), dtype=jnp.float32)
        return {'x': x, 'edge_index': edge_index, 'edge_type': edge_type, 'weight': weight, 'root': root, 'bias': bias, 'w_gate': w_gate, 'b_gate': b_gate}
    _L0_gnn_all = _L0_gnn_setup()
    _L0_gnn_in = {k: v for k, v in _L0_gnn_all.items() if k in ('weight', 'root', 'bias', 'w_gate', 'b_gate')}
    del _L0_gnn_all

    def _L0_mix_setup():
        import jax, jax.numpy as jnp
        import numpy as np
        NUM_HEADS = 16
        D_MODEL = 1024
        HEAD_DIM = D_MODEL // NUM_HEADS
        EPS = 1e-06

        def _feature_map(x):
            return jax.nn.elu(x) + 1.0
        key = jax.random.key(seed)
        ks = jax.random.split(key, 9)
        B, S, D = (4, 512, D_MODEL)
        scale = 1.0 / np.sqrt(D)
        inputs_q = jax.random.normal(ks[0], (B, S, D), dtype=jnp.float32)
        Wq = jax.random.normal(ks[1], (D, D), dtype=jnp.float32) * scale
        Wk = jax.random.normal(ks[2], (D, D), dtype=jnp.float32) * scale
        Wv = jax.random.normal(ks[3], (D, D), dtype=jnp.float32) * scale
        Wo = jax.random.normal(ks[4], (D, D), dtype=jnp.float32) * scale
        bq = jnp.zeros((D,), jnp.float32)
        bk = jnp.zeros((D,), jnp.float32)
        bv = jnp.zeros((D,), jnp.float32)
        bo = jnp.zeros((D,), jnp.float32)
        return {'inputs_q': inputs_q, 'Wq': Wq, 'bq': bq, 'Wk': Wk, 'bk': bk, 'Wv': Wv, 'bv': bv, 'Wo': Wo, 'bo': bo}
    _L0_mix_all = _L0_mix_setup()
    _L0_mix_in = {k: v for k, v in _L0_mix_all.items() if k in ('Wq', 'bq', 'Wk', 'bk', 'Wv', 'bv', 'Wo', 'bo')}
    del _L0_mix_all

    def _L0_ffn_setup():
        import jax, jax.numpy as jnp
        import numpy as np
        D = 1024
        LW = 16
        DEPTH = 8
        NN = 2 ** DEPTH - 1
        NL = 2 ** DEPTH
        B, S = (2, 1024)

        def _fff(x, nw, nb, w1, b1, w2, b2, act):
            node = jnp.zeros(x.shape[:2], dtype=jnp.int32)
            for _ in range(DEPTH):
                logit = jnp.einsum('bsd,bsd->bs', x, nw[node]) + nb[node]
                node = 2 * node + 1 + (logit > 0).astype(jnp.int32)
            leaf = node - NN
            h = act(jnp.einsum('bsd,bsdl->bsl', x, w1[leaf]) + b1[leaf])
            return jnp.einsum('bsl,bsld->bsd', h, w2[leaf]) + b2[leaf]

        def _forward(x, q_nw, q_nb, q_w1, q_b1, q_w2, q_b2, k_nw, k_nb, k_w1, k_b1, k_w2, k_b2, v_nw, v_nb, v_w1, v_b1, v_w2, v_b2, f_nw, f_nb, f_w1, f_b1, f_w2, f_b2):
            mu = jnp.mean(x, -1, keepdims=True)
            sd = jnp.std(x, -1, ddof=1, keepdims=True)
            xn = (x - mu) / jnp.sqrt(sd + 1e-05)
            relu = jax.nn.relu
            q = _fff(xn, q_nw, q_nb, q_w1, q_b1, q_w2, q_b2, relu)
            k = _fff(xn, k_nw, k_nb, k_w1, k_b1, k_w2, k_b2, relu)
            v = _fff(xn, v_nw, v_nb, v_w1, v_b1, v_w2, v_b2, relu)
            att = jax.nn.softmax(jnp.einsum('bqd,bkd->bqk', q, k) / jnp.sqrt(jnp.float32(D)), axis=-1)
            y = xn + jnp.einsum('bqk,bkd->bqd', att, v)
            gelu = lambda t: jax.nn.gelu(t, approximate=False)
            return y + _fff(y, f_nw, f_nb, f_w1, f_b1, f_w2, f_b2, gelu)

        def _make_fff_params(key, scale_in, scale_leaf):
            ks = jax.random.split(key, 4)
            nw = jax.random.normal(ks[0], (NN, D), jnp.float32) * scale_in
            nb = jnp.zeros((NN,), jnp.float32)
            w1 = jax.random.normal(ks[1], (NL, D, LW), jnp.float32) * scale_in
            b1 = jax.random.normal(ks[2], (NL, LW), jnp.float32) * 0.01
            w2 = jax.random.normal(ks[3], (NL, LW, D), jnp.float32) * scale_leaf
            b2 = jnp.zeros((NL, D), jnp.float32)
            return (nw, nb, w1, b1, w2, b2)
        key = jax.random.key(seed)
        kx, kq, kk, kv, kf = jax.random.split(key, 5)
        s_in = 1.0 / np.sqrt(D)
        s_lf = 1.0 / np.sqrt(LW)
        inp = {'x': jax.random.normal(kx, (B, S, D), jnp.float32)}
        for name, kk_ in (('q', kq), ('k', kk), ('v', kv), ('f', kf)):
            nw, nb, w1, b1, w2, b2 = _make_fff_params(kk_, s_in, s_lf)
            inp.update({f'{name}_nw': nw, f'{name}_nb': nb, f'{name}_w1': w1, f'{name}_b1': b1, f'{name}_w2': w2, f'{name}_b2': b2})
        return inp
    _L0_ffn_all = _L0_ffn_setup()
    _L0_ffn_in = {k: v for k, v in _L0_ffn_all.items() if k in ('q_nw', 'q_nb', 'q_w1', 'q_b1', 'q_w2', 'q_b2', 'k_nw', 'k_nb', 'k_w1', 'k_b1', 'k_w2', 'k_b2', 'v_nw', 'v_nb', 'v_w1', 'v_b1', 'v_w2', 'v_b2', 'f_nw', 'f_nb', 'f_w1', 'f_b1', 'f_w2', 'f_b2')}
    del _L0_ffn_all

    def _L1_gnn_setup():
        import jax, jax.numpy as jnp
        import numpy as np
        N = 1250
        E = 20000
        D_IN = 1024
        D_OUT = 1024
        key = jax.random.key(seed)
        k1, k2, k3, k4 = jax.random.split(key, 4)
        x = jax.random.normal(k1, (N, D_IN), dtype=jnp.float32)
        edge_index = jax.random.randint(k2, (2, E), 0, N, dtype=jnp.int64)
        W = jax.random.normal(k3, (D_OUT, D_IN), dtype=jnp.float32) * (1.0 / np.sqrt(D_IN))
        b = jax.random.normal(k4, (D_OUT,), dtype=jnp.float32) * 0.01
        return {'x': x, 'edge_index': edge_index, 'W': W, 'b': b}
    _L1_gnn_all = _L1_gnn_setup()
    _L1_gnn_in = {k: v for k, v in _L1_gnn_all.items() if k in ('W', 'b')}
    del _L1_gnn_all

    def _L1_mix_setup():
        import jax, jax.numpy as jnp
        import numpy as np
        B, S, E, H = (4, 256, 1024, 16)
        D = E // H

        def _xavier(key, out_f, in_f):
            lim = float(np.sqrt(6.0 / (in_f + out_f)))
            return jax.random.uniform(key, (out_f, in_f), jnp.float32, -lim, lim)

        def _feature_map(t):
            return jax.nn.elu(t) + 1.0
        key = jax.random.key(seed)
        ks = jax.random.split(key, 9)
        x = jax.random.normal(ks[0], (B, S, E), jnp.float32)
        Wq = _xavier(ks[1], E, E)
        Wk = _xavier(ks[2], E, E)
        Wv = _xavier(ks[3], E, E)
        Wo = _xavier(ks[4], E, E)
        bq = jnp.zeros((E,), jnp.float32)
        bk = jnp.zeros((E,), jnp.float32)
        bv = jnp.zeros((E,), jnp.float32)
        bo = jnp.zeros((E,), jnp.float32)
        return {'x': x, 'Wq': Wq, 'bq': bq, 'Wk': Wk, 'bk': bk, 'Wv': Wv, 'bv': bv, 'Wo': Wo, 'bo': bo}
    _L1_mix_all = _L1_mix_setup()
    _L1_mix_in = {k: v for k, v in _L1_mix_all.items() if k in ('Wq', 'bq', 'Wk', 'bk', 'Wv', 'bv', 'Wo', 'bo')}
    del _L1_mix_all

    def _L1_ffn_setup():
        import jax, jax.numpy as jnp
        import numpy as np
        EPS = 1e-05

        def _ln(x, g, b):
            mu = jnp.mean(x, axis=-1, keepdims=True)
            var = jnp.mean(jnp.square(x - mu), axis=-1, keepdims=True)
            return (x - mu) * jax.lax.rsqrt(var + EPS) * g + b

        def _forward(x, index_b, index_t, sw1, sb1, sw2, sb2, sw3, sb3, s_ln_g, s_ln_b, sg_w, sg_b, eg_w, eg_b, exp_bias, ew1, eb1, ew2, eb2, ew3, eb3, sel_ln_g, sel_ln_b):
            x1 = jnp.einsum('btd,hd->bth', x, sw1) + sb1
            x2 = jnp.einsum('btd,hd->bth', x, sw2) + sb2
            sh = _ln(jax.nn.silu(x1) * x2, s_ln_g, s_ln_b)
            shared_out = jnp.einsum('bth,dh->btd', sh, sw3) + sb3
            x_moe = x[index_b, index_t]
            shared_scores = jax.nn.sigmoid(x_moe @ sg_w.T + sg_b)
            expert_scores = jax.nn.sigmoid(x_moe @ eg_w.T + eg_b)
            top1_idx = jnp.argmax(expert_scores + exp_bias, axis=-1)
            top1_score = jnp.take_along_axis(expert_scores, top1_idx[:, None], axis=-1)
            weights = jax.nn.softmax(jnp.concatenate([shared_scores, top1_score], axis=-1), axis=-1)
            shared_w, expert_w = (weights[:, 0], weights[:, 1])
            shared_moe_out = shared_out[index_b, index_t] * shared_w[:, None]
            h1 = jnp.einsum('md,ehd->meh', x_moe, ew1) + eb1
            h2 = jnp.einsum('md,ehd->meh', x_moe, ew2) + eb2
            z = _ln(jax.nn.silu(h1) * h2, sel_ln_g, sel_ln_b)
            out_all = jnp.einsum('meh,edh->med', z, ew3) + eb3
            expert_out = jnp.take_along_axis(out_all, top1_idx[:, None, None], axis=1)[:, 0]
            expert_moe_out = expert_out * expert_w[:, None]
            final_out = shared_out.at[index_b, index_t].set(shared_moe_out + expert_moe_out)
            return final_out
        B, T, D, E, H, M = (2, 128, 1024, 8, 512, 128)
        key = jax.random.key(seed)
        ks = jax.random.split(key, 24)
        s = 0.02
        inp = {}
        inp['x'] = jax.random.normal(ks[0], (B, T, D), jnp.float32)
        flat = jnp.arange(M, dtype=jnp.int32) * 2
        inp['index_b'] = flat // T
        inp['index_t'] = flat % T
        inp['sw1'] = jax.random.normal(ks[1], (H, D), jnp.float32) * s
        inp['sb1'] = jnp.zeros((H,), jnp.float32)
        inp['sw2'] = jax.random.normal(ks[2], (H, D), jnp.float32) * s
        inp['sb2'] = jnp.zeros((H,), jnp.float32)
        inp['sw3'] = jax.random.normal(ks[3], (D, H), jnp.float32) * s
        inp['sb3'] = jnp.zeros((D,), jnp.float32)
        inp['s_ln_g'] = jnp.ones((H,), jnp.float32)
        inp['s_ln_b'] = jnp.zeros((H,), jnp.float32)
        inp['sg_w'] = jax.random.normal(ks[4], (1, D), jnp.float32) * s
        inp['sg_b'] = jnp.zeros((1,), jnp.float32)
        inp['eg_w'] = jax.random.normal(ks[5], (E, D), jnp.float32) * s
        inp['eg_b'] = jnp.zeros((E,), jnp.float32)
        inp['exp_bias'] = jnp.zeros((E,), jnp.float32)
        inp['ew1'] = jax.random.normal(ks[6], (E, H, D), jnp.float32) * s
        inp['eb1'] = jnp.zeros((E, H), jnp.float32)
        inp['ew2'] = jax.random.normal(ks[7], (E, H, D), jnp.float32) * s
        inp['eb2'] = jnp.zeros((E, H), jnp.float32)
        inp['ew3'] = jax.random.normal(ks[8], (E, D, H), jnp.float32) * s
        inp['eb3'] = jnp.zeros((E, D), jnp.float32)
        inp['sel_ln_g'] = jnp.ones((H,), jnp.float32)
        inp['sel_ln_b'] = jnp.zeros((H,), jnp.float32)
        return inp
    _L1_ffn_all = _L1_ffn_setup()
    _L1_ffn_in = {k: v for k, v in _L1_ffn_all.items() if k in ('index_b', 'index_t', 'sw1', 'sb1', 'sw2', 'sb2', 'sw3', 'sb3', 's_ln_g', 's_ln_b', 'sg_w', 'sg_b', 'eg_w', 'eg_b', 'exp_bias', 'ew1', 'eb1', 'ew2', 'eb2', 'ew3', 'eb3', 'sel_ln_g', 'sel_ln_b')}
    del _L1_ffn_all
    return {'x': x, 'src': src, 'dst': dst, 'edge_type_8': edge_type_8, 'L0_gnn_weight': _L0_gnn_in['weight'], 'L0_gnn_root': _L0_gnn_in['root'], 'L0_gnn_bias': _L0_gnn_in['bias'], 'L0_gnn_w_gate': _L0_gnn_in['w_gate'], 'L0_gnn_b_gate': _L0_gnn_in['b_gate'], 'L0_mix_Wq': _L0_mix_in['Wq'], 'L0_mix_bq': _L0_mix_in['bq'], 'L0_mix_Wk': _L0_mix_in['Wk'], 'L0_mix_bk': _L0_mix_in['bk'], 'L0_mix_Wv': _L0_mix_in['Wv'], 'L0_mix_bv': _L0_mix_in['bv'], 'L0_mix_Wo': _L0_mix_in['Wo'], 'L0_mix_bo': _L0_mix_in['bo'], 'L0_ffn_q_nw': _L0_ffn_in['q_nw'], 'L0_ffn_q_nb': _L0_ffn_in['q_nb'], 'L0_ffn_q_w1': _L0_ffn_in['q_w1'], 'L0_ffn_q_b1': _L0_ffn_in['q_b1'], 'L0_ffn_q_w2': _L0_ffn_in['q_w2'], 'L0_ffn_q_b2': _L0_ffn_in['q_b2'], 'L0_ffn_k_nw': _L0_ffn_in['k_nw'], 'L0_ffn_k_nb': _L0_ffn_in['k_nb'], 'L0_ffn_k_w1': _L0_ffn_in['k_w1'], 'L0_ffn_k_b1': _L0_ffn_in['k_b1'], 'L0_ffn_k_w2': _L0_ffn_in['k_w2'], 'L0_ffn_k_b2': _L0_ffn_in['k_b2'], 'L0_ffn_v_nw': _L0_ffn_in['v_nw'], 'L0_ffn_v_nb': _L0_ffn_in['v_nb'], 'L0_ffn_v_w1': _L0_ffn_in['v_w1'], 'L0_ffn_v_b1': _L0_ffn_in['v_b1'], 'L0_ffn_v_w2': _L0_ffn_in['v_w2'], 'L0_ffn_v_b2': _L0_ffn_in['v_b2'], 'L0_ffn_f_nw': _L0_ffn_in['f_nw'], 'L0_ffn_f_nb': _L0_ffn_in['f_nb'], 'L0_ffn_f_w1': _L0_ffn_in['f_w1'], 'L0_ffn_f_b1': _L0_ffn_in['f_b1'], 'L0_ffn_f_w2': _L0_ffn_in['f_w2'], 'L0_ffn_f_b2': _L0_ffn_in['f_b2'], 'L1_gnn_W': _L1_gnn_in['W'], 'L1_gnn_b': _L1_gnn_in['b'], 'L1_mix_Wq': _L1_mix_in['Wq'], 'L1_mix_bq': _L1_mix_in['bq'], 'L1_mix_Wk': _L1_mix_in['Wk'], 'L1_mix_bk': _L1_mix_in['bk'], 'L1_mix_Wv': _L1_mix_in['Wv'], 'L1_mix_bv': _L1_mix_in['bv'], 'L1_mix_Wo': _L1_mix_in['Wo'], 'L1_mix_bo': _L1_mix_in['bo'], 'L1_ffn_index_b': _L1_ffn_in['index_b'], 'L1_ffn_index_t': _L1_ffn_in['index_t'], 'L1_ffn_sw1': _L1_ffn_in['sw1'], 'L1_ffn_sb1': _L1_ffn_in['sb1'], 'L1_ffn_sw2': _L1_ffn_in['sw2'], 'L1_ffn_sb2': _L1_ffn_in['sb2'], 'L1_ffn_sw3': _L1_ffn_in['sw3'], 'L1_ffn_sb3': _L1_ffn_in['sb3'], 'L1_ffn_s_ln_g': _L1_ffn_in['s_ln_g'], 'L1_ffn_s_ln_b': _L1_ffn_in['s_ln_b'], 'L1_ffn_sg_w': _L1_ffn_in['sg_w'], 'L1_ffn_sg_b': _L1_ffn_in['sg_b'], 'L1_ffn_eg_w': _L1_ffn_in['eg_w'], 'L1_ffn_eg_b': _L1_ffn_in['eg_b'], 'L1_ffn_exp_bias': _L1_ffn_in['exp_bias'], 'L1_ffn_ew1': _L1_ffn_in['ew1'], 'L1_ffn_eb1': _L1_ffn_in['eb1'], 'L1_ffn_ew2': _L1_ffn_in['ew2'], 'L1_ffn_eb2': _L1_ffn_in['eb2'], 'L1_ffn_ew3': _L1_ffn_in['ew3'], 'L1_ffn_eb3': _L1_ffn_in['eb3'], 'L1_ffn_sel_ln_g': _L1_ffn_in['sel_ln_g'], 'L1_ffn_sel_ln_b': _L1_ffn_in['sel_ln_b']}

def reference(x, src, dst, edge_type_8, L0_gnn_weight, L0_gnn_root, L0_gnn_bias, L0_gnn_w_gate, L0_gnn_b_gate, L0_mix_Wq, L0_mix_bq, L0_mix_Wk, L0_mix_bk, L0_mix_Wv, L0_mix_bv, L0_mix_Wo, L0_mix_bo, L0_ffn_q_nw, L0_ffn_q_nb, L0_ffn_q_w1, L0_ffn_q_b1, L0_ffn_q_w2, L0_ffn_q_b2, L0_ffn_k_nw, L0_ffn_k_nb, L0_ffn_k_w1, L0_ffn_k_b1, L0_ffn_k_w2, L0_ffn_k_b2, L0_ffn_v_nw, L0_ffn_v_nb, L0_ffn_v_w1, L0_ffn_v_b1, L0_ffn_v_w2, L0_ffn_v_b2, L0_ffn_f_nw, L0_ffn_f_nb, L0_ffn_f_w1, L0_ffn_f_b1, L0_ffn_f_w2, L0_ffn_f_b2, L1_gnn_W, L1_gnn_b, L1_mix_Wq, L1_mix_bq, L1_mix_Wk, L1_mix_bk, L1_mix_Wv, L1_mix_bv, L1_mix_Wo, L1_mix_bo, L1_ffn_index_b, L1_ffn_index_t, L1_ffn_sw1, L1_ffn_sb1, L1_ffn_sw2, L1_ffn_sb2, L1_ffn_sw3, L1_ffn_sb3, L1_ffn_s_ln_g, L1_ffn_s_ln_b, L1_ffn_sg_w, L1_ffn_sg_b, L1_ffn_eg_w, L1_ffn_eg_b, L1_ffn_exp_bias, L1_ffn_ew1, L1_ffn_eb1, L1_ffn_ew2, L1_ffn_eb2, L1_ffn_ew3, L1_ffn_eb3, L1_ffn_sel_ln_g, L1_ffn_sel_ln_b):
    import jax
    import jax.numpy as jnp

    def _L0_gnn_ref(x, edge_index, edge_type, weight, root, bias, w_gate, b_gate):
        import jax, jax.numpy as jnp
        import numpy as np
        N, D, R, E = (625, 1024, 8, 5000)

        def _rgcn(x, edge_index, edge_type, weight, root, bias):
            src, dst = (edge_index[0], edge_index[1])
            msgs = x[src]
            out = x @ root + bias
            n = x.shape[0]
            for r in range(weight.shape[0]):
                mask = (edge_type == r).astype(x.dtype)
                sums = jax.ops.segment_sum(msgs * mask[:, None], dst, num_segments=n)
                cnt = jax.ops.segment_sum(mask, dst, num_segments=n)
                mean = sums / jnp.maximum(cnt, 1.0)[:, None]
                out = out + mean @ weight[r]
            return out
        u = _rgcn(x, edge_index, edge_type, weight, root, bias)
        z = jnp.concatenate([u, x], axis=1) @ w_gate + b_gate
        h = jnp.tanh(u) * z + x * (1.0 - z)
        return h

    def _L0_mix_ref(inputs_q, Wq, bq, Wk, bk, Wv, bv, Wo, bo):
        import jax, jax.numpy as jnp
        import numpy as np
        NUM_HEADS = 16
        D_MODEL = 1024
        HEAD_DIM = D_MODEL // NUM_HEADS
        EPS = 1e-06

        def _feature_map(x):
            return jax.nn.elu(x) + 1.0
        B, S, D = inputs_q.shape
        H, Dh = (NUM_HEADS, HEAD_DIM)
        q = (inputs_q @ Wq + bq).reshape(B, S, H, Dh)
        k = (inputs_q @ Wk + bk).reshape(B, S, H, Dh)
        v = (inputs_q @ Wv + bv).reshape(B, S, H, Dh)
        q = _feature_map(q)
        k = _feature_map(k)
        kv = jnp.einsum('bkhd,bkhm->bhdm', k, v)
        out = jnp.einsum('bqhd,bhdm->bqhm', q, kv)
        normalizer = jnp.einsum('bqhd,bkhd->bqh', q, k)
        normalizer = jnp.maximum(normalizer, EPS)
        out = out / normalizer[..., None]
        out = out.reshape(B, S, D)
        return out @ Wo + bo

    def _L0_ffn_ref(x, q_nw, q_nb, q_w1, q_b1, q_w2, q_b2, k_nw, k_nb, k_w1, k_b1, k_w2, k_b2, v_nw, v_nb, v_w1, v_b1, v_w2, v_b2, f_nw, f_nb, f_w1, f_b1, f_w2, f_b2):
        import jax, jax.numpy as jnp
        import numpy as np
        D = 1024
        LW = 16
        DEPTH = 8
        NN = 2 ** DEPTH - 1
        NL = 2 ** DEPTH
        B, S = (2, 1024)

        def _fff(x, nw, nb, w1, b1, w2, b2, act):
            node = jnp.zeros(x.shape[:2], dtype=jnp.int32)
            for _ in range(DEPTH):
                logit = jnp.einsum('bsd,bsd->bs', x, nw[node]) + nb[node]
                node = 2 * node + 1 + (logit > 0).astype(jnp.int32)
            leaf = node - NN
            h = act(jnp.einsum('bsd,bsdl->bsl', x, w1[leaf]) + b1[leaf])
            return jnp.einsum('bsl,bsld->bsd', h, w2[leaf]) + b2[leaf]

        def _forward(x, q_nw, q_nb, q_w1, q_b1, q_w2, q_b2, k_nw, k_nb, k_w1, k_b1, k_w2, k_b2, v_nw, v_nb, v_w1, v_b1, v_w2, v_b2, f_nw, f_nb, f_w1, f_b1, f_w2, f_b2):
            mu = jnp.mean(x, -1, keepdims=True)
            sd = jnp.std(x, -1, ddof=1, keepdims=True)
            xn = (x - mu) / jnp.sqrt(sd + 1e-05)
            relu = jax.nn.relu
            q = _fff(xn, q_nw, q_nb, q_w1, q_b1, q_w2, q_b2, relu)
            k = _fff(xn, k_nw, k_nb, k_w1, k_b1, k_w2, k_b2, relu)
            v = _fff(xn, v_nw, v_nb, v_w1, v_b1, v_w2, v_b2, relu)
            att = jax.nn.softmax(jnp.einsum('bqd,bkd->bqk', q, k) / jnp.sqrt(jnp.float32(D)), axis=-1)
            y = xn + jnp.einsum('bqk,bkd->bqd', att, v)
            gelu = lambda t: jax.nn.gelu(t, approximate=False)
            return y + _fff(y, f_nw, f_nb, f_w1, f_b1, f_w2, f_b2, gelu)

        def _make_fff_params(key, scale_in, scale_leaf):
            ks = jax.random.split(key, 4)
            nw = jax.random.normal(ks[0], (NN, D), jnp.float32) * scale_in
            nb = jnp.zeros((NN,), jnp.float32)
            w1 = jax.random.normal(ks[1], (NL, D, LW), jnp.float32) * scale_in
            b1 = jax.random.normal(ks[2], (NL, LW), jnp.float32) * 0.01
            w2 = jax.random.normal(ks[3], (NL, LW, D), jnp.float32) * scale_leaf
            b2 = jnp.zeros((NL, D), jnp.float32)
            return (nw, nb, w1, b1, w2, b2)
        return _forward(x, q_nw, q_nb, q_w1, q_b1, q_w2, q_b2, k_nw, k_nb, k_w1, k_b1, k_w2, k_b2, v_nw, v_nb, v_w1, v_b1, v_w2, v_b2, f_nw, f_nb, f_w1, f_b1, f_w2, f_b2)

    def _L1_gnn_ref(x, edge_index, W, b):
        import jax, jax.numpy as jnp
        import numpy as np
        N = 1250
        E = 20000
        D_IN = 1024
        D_OUT = 1024
        num_nodes = x.shape[0]
        self_idx = jnp.arange(num_nodes, dtype=edge_index.dtype)
        ei = jnp.concatenate([edge_index, jnp.stack([self_idx, self_idx], axis=0)], axis=1)
        row, col = (ei[0], ei[1])
        h = jnp.einsum('nd,od->no', x, W) + b
        deg = jnp.zeros((num_nodes,), dtype=h.dtype).at[row].add(1.0)
        deg_inv_sqrt = deg ** (-0.5)
        norm = deg_inv_sqrt[row] * deg_inv_sqrt[col]
        msg = norm[:, None] * h[col]
        out = jax.ops.segment_sum(msg, row, num_segments=num_nodes)
        return out

    def _L1_mix_ref(x, Wq, bq, Wk, bk, Wv, bv, Wo, bo):
        import jax, jax.numpy as jnp
        import numpy as np
        B, S, E, H = (4, 256, 1024, 16)
        D = E // H

        def _xavier(key, out_f, in_f):
            lim = float(np.sqrt(6.0 / (in_f + out_f)))
            return jax.random.uniform(key, (out_f, in_f), jnp.float32, -lim, lim)

        def _feature_map(t):
            return jax.nn.elu(t) + 1.0
        b, s, _ = x.shape
        Q = (x @ Wq.T + bq).reshape(b, s, H, D)
        K = (x @ Wk.T + bk).reshape(b, s, H, D)
        V = (x @ Wv.T + bv).reshape(b, s, H, D)
        Q = _feature_map(Q)
        K = _feature_map(K)
        KV = jnp.einsum('bshd,bshe->bhde', K, V)
        K_sum = K.sum(axis=1)
        Z = 1.0 / (jnp.einsum('bshd,bhd->bsh', Q, K_sum) + 1e-06)
        out = jnp.einsum('bshd,bhde,bsh->bshe', Q, KV, Z)
        out = out.reshape(b, s, E)
        out = out @ Wo.T + bo
        return out

    def _L1_ffn_ref(x, index_b, index_t, sw1, sb1, sw2, sb2, sw3, sb3, s_ln_g, s_ln_b, sg_w, sg_b, eg_w, eg_b, exp_bias, ew1, eb1, ew2, eb2, ew3, eb3, sel_ln_g, sel_ln_b):
        import jax, jax.numpy as jnp
        import numpy as np
        EPS = 1e-05

        def _ln(x, g, b):
            mu = jnp.mean(x, axis=-1, keepdims=True)
            var = jnp.mean(jnp.square(x - mu), axis=-1, keepdims=True)
            return (x - mu) * jax.lax.rsqrt(var + EPS) * g + b

        def _forward(x, index_b, index_t, sw1, sb1, sw2, sb2, sw3, sb3, s_ln_g, s_ln_b, sg_w, sg_b, eg_w, eg_b, exp_bias, ew1, eb1, ew2, eb2, ew3, eb3, sel_ln_g, sel_ln_b):
            x1 = jnp.einsum('btd,hd->bth', x, sw1) + sb1
            x2 = jnp.einsum('btd,hd->bth', x, sw2) + sb2
            sh = _ln(jax.nn.silu(x1) * x2, s_ln_g, s_ln_b)
            shared_out = jnp.einsum('bth,dh->btd', sh, sw3) + sb3
            x_moe = x[index_b, index_t]
            shared_scores = jax.nn.sigmoid(x_moe @ sg_w.T + sg_b)
            expert_scores = jax.nn.sigmoid(x_moe @ eg_w.T + eg_b)
            top1_idx = jnp.argmax(expert_scores + exp_bias, axis=-1)
            top1_score = jnp.take_along_axis(expert_scores, top1_idx[:, None], axis=-1)
            weights = jax.nn.softmax(jnp.concatenate([shared_scores, top1_score], axis=-1), axis=-1)
            shared_w, expert_w = (weights[:, 0], weights[:, 1])
            shared_moe_out = shared_out[index_b, index_t] * shared_w[:, None]
            h1 = jnp.einsum('md,ehd->meh', x_moe, ew1) + eb1
            h2 = jnp.einsum('md,ehd->meh', x_moe, ew2) + eb2
            z = _ln(jax.nn.silu(h1) * h2, sel_ln_g, sel_ln_b)
            out_all = jnp.einsum('meh,edh->med', z, ew3) + eb3
            expert_out = jnp.take_along_axis(out_all, top1_idx[:, None, None], axis=1)[:, 0]
            expert_moe_out = expert_out * expert_w[:, None]
            final_out = shared_out.at[index_b, index_t].set(shared_moe_out + expert_moe_out)
            return final_out
        return _forward(x, index_b, index_t, sw1, sb1, sw2, sb2, sw3, sb3, s_ln_g, s_ln_b, sg_w, sg_b, eg_w, eg_b, exp_bias, ew1, eb1, ew2, eb2, ew3, eb3, sel_ln_g, sel_ln_b)
    edge_index = jnp.stack([src, dst])
    xn = _layernorm(x, axis=-1)
    x = x + _L0_gnn_ref(xn, edge_index, edge_type_8, L0_gnn_weight, L0_gnn_root, L0_gnn_bias, L0_gnn_w_gate, L0_gnn_b_gate) + _L0_mix_ref(xn[None], L0_mix_Wq, L0_mix_bq, L0_mix_Wk, L0_mix_bk, L0_mix_Wv, L0_mix_bv, L0_mix_Wo, L0_mix_bo)[0]
    x = x + _L0_ffn_ref(_layernorm(x, axis=-1)[None], L0_ffn_q_nw, L0_ffn_q_nb, L0_ffn_q_w1, L0_ffn_q_b1, L0_ffn_q_w2, L0_ffn_q_b2, L0_ffn_k_nw, L0_ffn_k_nb, L0_ffn_k_w1, L0_ffn_k_b1, L0_ffn_k_w2, L0_ffn_k_b2, L0_ffn_v_nw, L0_ffn_v_nb, L0_ffn_v_w1, L0_ffn_v_b1, L0_ffn_v_w2, L0_ffn_v_b2, L0_ffn_f_nw, L0_ffn_f_nb, L0_ffn_f_w1, L0_ffn_f_b1, L0_ffn_f_w2, L0_ffn_f_b2)[0]
    xn = _layernorm(x, axis=-1)
    x = x + _L1_gnn_ref(xn, edge_index, L1_gnn_W, L1_gnn_b) + _L1_mix_ref(xn[None], L1_mix_Wq, L1_mix_bq, L1_mix_Wk, L1_mix_bk, L1_mix_Wv, L1_mix_bv, L1_mix_Wo, L1_mix_bo)[0]
    x = x + _L1_ffn_ref(_layernorm(x, axis=-1)[None], L1_ffn_index_b, L1_ffn_index_t, L1_ffn_sw1, L1_ffn_sb1, L1_ffn_sw2, L1_ffn_sb2, L1_ffn_sw3, L1_ffn_sb3, L1_ffn_s_ln_g, L1_ffn_s_ln_b, L1_ffn_sg_w, L1_ffn_sg_b, L1_ffn_eg_w, L1_ffn_eg_b, L1_ffn_exp_bias, L1_ffn_ew1, L1_ffn_eb1, L1_ffn_ew2, L1_ffn_eb2, L1_ffn_ew3, L1_ffn_eb3, L1_ffn_sel_ln_g, L1_ffn_sel_ln_b)[0]
    return x

_drawn_inputs = setup_inputs


def setup_inputs(seed=0):
    import zlib

    import numpy as np

    out = dict(_drawn_inputs(seed))
    spreads = {'L0_gnn_bias': (0.0, 0.1),
     'L0_gnn_b_gate': (0.0, 0.1),
     'L0_mix_bq': (0.0, 2.0),
     'L0_mix_bk': (0.0, 2.0),
     'L0_mix_bv': (0.0, 0.1),
     'L0_mix_bo': (0.0, 0.1),
     'L0_ffn_q_nb': (0.0, 0.297),
     'L0_ffn_q_b2': (0.0, 0.746),
     'L0_ffn_k_nb': (0.0, 0.1),
     'L0_ffn_k_b2': (0.0, 0.617),
     'L0_ffn_v_nb': (0.0, 0.1),
     'L0_ffn_v_b2': (0.0, 0.1),
     'L0_ffn_f_nb': (0.0, 0.1),
     'L0_ffn_f_b2': (0.0, 0.311),
     'L1_mix_bq': (0.0, 2.0),
     'L1_mix_bk': (0.0, 2.0),
     'L1_mix_bv': (0.0, 0.308),
     'L1_mix_bo': (0.0, 0.307),
     'L1_ffn_sb1': (0.0, 0.574),
     'L1_ffn_sb2': (0.0, 0.394),
     'L1_ffn_sb3': (0.0, 0.325),
     'L1_ffn_s_ln_g': (1.0, 0.6),
     'L1_ffn_s_ln_b': (0.0, 0.721),
     'L1_ffn_eg_b': (0.0, 2.0),
     'L1_ffn_exp_bias': (0.0, 0.355),
     'L1_ffn_eb1': (0.0, 2.0),
     'L1_ffn_eb2': (0.0, 2.0),
     'L1_ffn_eb3': (0.0, 0.8),
     'L1_ffn_sel_ln_g': (1.0, 0.6),
     'L1_ffn_sel_ln_b': (0.0, 0.8)}
    factors = {'L0_mix_Wq': 8.0,
     'L0_mix_Wk': 5.314,
     'L0_ffn_q_b1': 22.965,
     'L0_ffn_k_b1': 8.0,
     'L0_ffn_v_b1': 8.0,
     'L0_ffn_f_b1': 33.817,
     'L1_gnn_b': 23.43,
     'L1_mix_Wq': 144.677,
     'L1_mix_Wk': 133.491,
     'L1_mix_Wv': 3.376,
     'L1_ffn_sg_w': 66.643,
     'L1_ffn_eg_w': 3.755,
     'L1_ffn_ew1': 2.983,
     'L1_ffn_ew2': 2.856,
     'L1_ffn_ew3': 2.823}
    for name, (base, spread) in spreads.items():
        noise = np.random.default_rng([zlib.crc32(name.encode()), seed]).standard_normal(out[name].shape)
        drawn = base * np.exp(spread * noise) if base else spread * noise
        out[name] = jnp.asarray(drawn.astype(out[name].dtype))
    for name, factor in factors.items():
        out[name] = (out[name] * factor).astype(out[name].dtype)
    return out
```

```python
from contextlib import ExitStack

import concourse.bass as bass
from concourse import mybir

F32 = mybir.dt.float32
F32R = mybir.dt.float32r
F16 = mybir.dt.float16
I32 = mybir.dt.int32
U32 = mybir.dt.uint32
ALU = mybir.AluOpType
ACT = mybir.ActivationFunctionType
AX = mybir.AxisListType


class Step:

    def __init__(self, engine, emit, after, sem=None, value=0):
        self.engine, self.emit, self.after = engine, emit, after
        self.sem, self.value, self.wanted = sem, value, sem is not None
        self.own = False


def flat(after):
    out = []
    for a in after:
        if isinstance(a, Step):
            out.append(a)
        elif a is not None:
            out += flat(a)
    return out


class Queues:

    ENGINES = ("tensor", "scalar", "vector", "gpsimd", "sync")

    def __init__(self, nc, ctx):
        self.nc, self.ctx = nc, ctx
        self.steps = {e: [] for e in self.ENGINES}
        self.counter = {e: ctx.enter_context(nc.semaphore(f"done_{e}")) for e in self.ENGINES}
        self.last = {}
        self.pooled = None

    def add(self, engine, emit, after):
        step = Step(engine, emit, flat(after))
        for a in step.after:
            a.wanted = True
        self.steps[engine].append(step)
        return step

    def pe(self, emit, *after):
        return self.add("tensor", emit, after)

    def act(self, emit, *after):
        return self.add("scalar", emit, after)

    def dve(self, emit, *after):
        return self.add("vector", emit, after)

    def pool(self, emit, *after):
        self.pooled = self.add("gpsimd", emit, (after, self.pooled))
        return self.pooled

    def sp(self, emit, *after):
        return self.add("sync", emit, after)

    def sem(self, name):
        return self.ctx.enter_context(self.nc.semaphore(name))

    def dma(self, engine, sem, emit, *after):
        before = self.last.get(sem.name)
        step = Step(engine, emit, flat(after) + ([before] if before else []), sem, 16 + (before.value if before else 0))
        for a in step.after:
            a.wanted = True
        self.last[sem.name] = step
        self.steps[engine].append(step)
        return step

    def emit_all(self):
        self.sp(lambda e: e.nop(), list(self.last.values()))
        for e in self.ENGINES:
            n = 0
            for s in self.steps[e]:
                if s.sem is None and s.wanted:
                    n += 1
                    s.sem, s.value = self.counter[e], n
        with self.nc.Block() as block:
            for e in self.ENGINES:
                self.emit_engine(block, e)

    def emit_engine(self, block, e):
        def run(engine):
            seen = {}
            for s in self.steps[e]:
                for a in s.after:
                    if seen.get(a.sem.name, 0) < a.value:
                        engine.wait_ge(a.sem, a.value)
                        seen[a.sem.name] = a.value
                last = s.emit(engine)
                if s.wanted and not s.own:
                    last.then_inc(s.sem, 16 if s.sem.name != self.counter[e].name else 1)

        {"tensor": block.tensor, "scalar": block.scalar, "vector": block.vector,
         "gpsimd": block.gpsimd, "sync": block.sync}[e](run)

N, D, TT, PT = 625, 1024, 5, 125
NP, NH = 628, 314
EPS = 1e-5


def gps_layers(nc, A, out):
    ctx = ExitStack()
    with ctx:
        q = Queues(nc, ctx)
        pe, act, dve, pool, sp, dma = q.pe, q.act, q.dve, q.pool, q.sp, q.dma

        C0 = 16512
        RL0 = C0 + 12288
        NRING, NHIGH = 14, 6
        HI0 = RL0 + NRING * 4096
        R0 = HI0 + NHIGH * 4096
        LENT = HI0 - 3 * 4096
        TOP = 229344

        def size_of(shape, dt):
            n = 1
            for s in shape[1:]:
                n *= s
            return n * (2 if dt == F16 else 4)

        def at(name, shape, dt, offset):
            assert offset + size_of(shape, dt) <= TOP, (name, offset + size_of(shape, dt) - TOP)
            return nc.alloc_sbuf_tensor_at(name, shape, dt, offset=offset)

        here = [C0]

        def const(name, shape, dt):
            o = here[0]
            here[0] += (size_of(shape, dt) + 31) // 32 * 32
            assert here[0] <= RL0, name
            return nc.alloc_sbuf_tensor_at(name, shape, dt, offset=o)

        PS = ctx.enter_context(nc.psum_tensor("PS", [128, 4096], F32))

        def bank(i, n=1):
            return PS[:, i * 512:(i + n) * 512]

        freed = [[] for _ in range(8)]

        def free(b, n, *steps):
            for i in range(b, b + n):
                freed[i] = list(steps)

        def scratch(name, shape, dt=F32):
            return nc.dram_tensor(name, shape, dt, kind="Internal").ap()

        ident = const("ident", [128, 128], F32)
        iota16 = const("iota16", [128, 640], F16)
        ones16 = const("ones16", [128, 128], F16)
        zeros16 = const("zeros16", [128, 512], F16)
        bdmask = const("bdmask", [128, 130], F32)
        rstd = const("rstd", [PT, TT], F32)
        lnst = const("lnst", [PT, TT, 2, 6], F32)
        lnmv = const("lnmv", [PT, TT, 2], F32)
        lnt = const("lnt", [PT, 8, TT], F32)
        ii = at("iota_int", [128, 640], I32, R0 + 81024)

        io = pool(lambda e: e.iota(ii[:, 0:128], [[1, 128]], base=0, channel_multiplier=-1))
        ident_ok = dve(lambda e: e.tensor_scalar(ident[:, :], ii[:, 0:128], 0.0, None, op0=ALU.is_equal), io)
        io2 = pool(lambda e: e.iota(ii[:, :], [[1, 640]], base=0, channel_multiplier=0), ident_ok)
        iota_ok = dve(lambda e: e.tensor_copy(iota16[:, :], ii[:, :]), io2)
        ones_ok = pool(lambda e: e.memset(ones16[:, :], 1.0))
        zeros_ok = pool(lambda e: e.memset(zeros16[:, :], 0.0))

        def fill(ap, value, *after):
            if ap.dtype == F32R:
                ap = ap.bitcast(F32)
            return pool(lambda e: e.memset(ap, value), *after)

        m0 = fill(bdmask[:, :], 0.0)
        bd_ok = [fill(bdmask[0:64, 0:64], 1.0, m0), fill(bdmask[64:128, 64:128], 1.0, m0),
                 fill(bdmask[0:64, 128:129], 1.0, m0), fill(bdmask[64:128, 129:130], 1.0, m0)]

        RAW = [at(f"raw{i}", [128, 1024], F32, RL0 + 4096 * i) for i in range(NRING)]
        LOW = [at(f"low{i}", [128, 1024], F32R, RL0 + 4096 * i) for i in range(NRING)]
        HIGH = [at(f"high{i}", [128, 1024], F32R, HI0 + 4096 * i) for i in range(NHIGH)]
        RAWS = [q.sem(f"raw_sem{i}") for i in range(NRING)]

        class Stream:

            def __init__(self, places):
                self.src, self.loaded, self.high, self.low, self.used = [], [], [], [], []
                self.order = list(places)
                self.place = []
                self.tenant = {}
                self.limit = 1 << 30
                self.ahead = NHIGH
                self.guard = {}
                self.raw_guard = {}
                self.subtract = dve
                self.pooled = ()

            def declare(self, ap, parts=4):
                w = ap.shape[-1] // parts
                self.src += [ap[:, j * w:(j + 1) * w] for j in range(parts)]
                self.load()
                return list(range(len(self.src) - parts, len(self.src)))

            def grow(self, places, *after):
                self.order = list(places) + self.order
                for p in places:
                    self.raw_guard[p] = after
                self.load()

            def drop(self, places):
                self.dropped = list(places)
                for p in places:
                    self.order.remove(p)

            def lent(self):
                return [self.used[self.tenant[p]] for p in self.dropped]

            def load(self):
                while len(self.loaded) < len(self.src) and self.tenant.get(self.order[0], -1) < len(self.used):
                    self.load_one()

            def load_one(self):
                i, p = len(self.loaded), self.order.pop(0)
                raw, src = RAW[p], self.src[i]
                before = self.used[self.tenant[p]] if p in self.tenant else None
                self.loaded.append(dma("sync", RAWS[p], lambda e: e.dma_start(raw[:, 0:src.shape[-1]], src),
                                       before, self.raw_guard.pop(p, None)))
                self.tenant[p] = i
                self.place.append(p)
                self.order.append(p)

            def split_one(self):
                i = len(self.high)
                w = self.src[i].shape[-1]
                raw, low, high = RAW[self.place[i]], LOW[self.place[i]], HIGH[i % NHIGH]
                h = act(lambda e: e.activation(high[:, 0:w], raw[:, 0:w], ACT.Copy),
                        self.loaded[i], self.used[i - NHIGH] if i >= NHIGH else None, self.guard.pop(i % NHIGH, None))
                self.high.append(h)
                on = pool if i % 4 in self.pooled else self.subtract
                self.low.append(on(lambda e: e.tensor_tensor(low[:, 0:w], raw[:, 0:w], high[:, 0:w], ALU.subtract), h))

            def split(self, n=1):
                for _ in range(n):
                    if len(self.high) < min(self.limit, len(self.place)) and len(self.high) - len(self.used) < self.ahead:
                        self.split_one()

            def ready(self, i):
                while len(self.high) <= i:
                    self.split_one()
                return [self.high[i], self.low[i]]

            def pair(self, i):
                return HIGH[i % NHIGH], LOW[self.place[i]]

            def release(self, i, step):
                assert len(self.used) == i
                self.used.append(step)
                self.load()

        W = Stream([*range(7), 12, 13])

        def rsqrt(v, r, w, h, *after):
            b = dve(lambda e: e.tensor_scalar(w.bitcast(I32), v.bitcast(I32), 1, None, op0=ALU.arith_shift_right), *after)
            m = dve(lambda e: e.tensor_scalar(h, v, -0.5, None, op0=ALU.mult), *after)
            b = dve(lambda e, b=b: e.tensor_scalar(r.bitcast(I32), w.bitcast(I32), -1.0, float(0x5F3759DF), op0=ALU.mult, op1=ALU.add), b)
            for _ in range(3):
                if v.shape[-1] == 1:
                    b = dve(lambda e: e.scalar_tensor_tensor(w, r, r, h, op0=ALU.mult, op1=ALU.mult), b, m)
                else:
                    b = dve(lambda e: e.tensor_tensor(w, r, r, ALU.mult), b)
                    b = dve(lambda e: e.tensor_tensor(w, w, h, ALU.mult), b, m)
                b = dve(lambda e: e.scalar_tensor_tensor(r, w, 1.5, r, op0=ALU.add, op1=ALU.mult), b)
            return b

        def moments(a, b, x, after):
            last = []
            for t in range(a, b):
                for h in range(2):
                    last.append(dve(lambda e, t=t, h=h: e.bn_stats(lnst[:, t, h, :], x[:, t, 512 * h:512 * h + 512]), after[t]))
            for t in range(a, b):
                last.append(dve(lambda e, t=t: e.bn_aggr(lnmv[:, t, :], lnst[:, t, :, :].rearrange("p a b -> p (a b)")), last[2 * (t - a):2 * (t - a) + 2]))
            return last

        def ln_stats(a, b, x, after):
            d = dve(lambda e: e.tensor_scalar(lnt[:, 0, a:b], lnmv[:, a:b, 1], EPS, None, op0=ALU.add), moments(a, b, x, after))
            return rsqrt(lnt[:, 0, a:b], rstd[:, a:b], lnt[:, 1, a:b], lnt[:, 5, a:b], d)

        def normalize(t, dst, x, scale, *after):
            return dve(lambda e: e.tensor_scalar(dst, x, lnmv[:, t, 0:1], scale[:, t:t + 1],
                                                 op0=ALU.subtract, op1=ALU.mult), *after)

        def cols(t):
            return slice(t * PT, (t + 1) * PT)

        def transpose_tile(t, x, hi, lo, b, *after):
            ps = bank(b, 2).rearrange("p (k c) -> p k c", k=8)[:, :, 0:PT]

            def emit(e):
                for k in range(8):
                    ins = e.transpose(ps[:, k, :], x[:, k * 128:(k + 1) * 128], ident[0:PT, 0:PT])
                return ins
            a = pe(emit, ident_ok, freed[b], freed[b + 1], *after)
            h = act(lambda e: e.activation(hi[:, :, cols(t)], ps, ACT.Copy), a)
            l = dve(lambda e: e.tensor_tensor(lo[:, :, cols(t)], ps, hi[:, :, cols(t)], ALU.subtract), h)
            free(b, 2, h, l)
            return [h, l]

        def rows(dst, xh, xl, xs, part, kts, first, last, *after):
            wh, wl = W.pair(part)

            def emit(e):
                for j, kt in enumerate(kts):
                    c = slice(512 * j, 512 * j + 512)
                    e.matmul(dst, xh[:, kt, xs], wh[:, c], start=first and j == 0, stop=False)
                    e.matmul(dst, xh[:, kt, xs], wl[:, c], start=False, stop=False)
                    ins = e.matmul(dst, xl[:, kt, xs], wh[:, c], start=False, stop=last and j == len(kts) - 1)
                return ins
            return pe(emit, W.ready(part), *after)

        def rows_tile(t, parts, xh, xl, b, ready, first=True, last=True, done=None):
            for j, part in enumerate(parts):
                s = rows(bank(b)[0:PT, :], xh, xl, cols(t), part, (2 * j, 2 * j + 1),
                         first and j == 0, last and j == 3, freed[b] if first else None, ready)
                if done is None and t == TT - 1:
                    W.release(part, s)
            return s

        XTH = at("xt_high", [128, 8, NP], F32R, R0)
        XTL = at("xt_low", [128, 8, NP], F32R, R0 + 20096)
        P1 = R0 + 40192
        SPARE = RL0 + 7 * 4096
        XN = at("x_rows", [PT, TT, D], F32, P1)

        xsem = [q.sem(f"x_sem{t}") for t in range(TT)]
        xload = [dma("sync", xsem[t], lambda e, t=t: e.dma_start(XN[:, t, :], A["x"][t * PT:(t + 1) * PT, :])) for t in range(TT)]

        EI0 = at("edges0", [128, 3, 128], I32, P1 + 59904)
        EI1 = at("edges1", [36, 3, 128], I32, P1 + 61440)
        esem = [q.sem("e_sem0"), q.sem("e_sem1")]
        eload = [dma("scalar", esem[0], lambda e: e.dma_start(EI0[:, :, :], A["edges"][0:128])),
                 dma("scalar", esem[1], lambda e: e.dma_start(EI1[:, :, :], A["edges"][128:164]))]

        NB, LOOK = 40, 4
        tidi = at("e_tidi", [128, 2], I32, P1 + 66432)
        bsti = at("e_bsti", [128, NB], I32, P1 + 66624)
        tgt = const("target_id", [64, 10], F32)
        tgti = const("target_int", [64, 10], I32)
        ti = pool(lambda e: e.iota(tidi[:, :], [[128, 2]], base=0, channel_multiplier=1))
        bi = pool(lambda e: e.iota(bsti[:, :], [[128, NB]], base=0, channel_multiplier=0))
        gi = pool(lambda e: e.iota(tgti[:, :], [[64, 10]], base=0, channel_multiplier=1))

        Wk = [W.declare(A["L0_mix_Wk"][h]) for h in range(2)]
        Wv = [W.declare(A["L0_mix_Wv"][h]) for h in range(2)]
        Wroot = [W.declare(A["L0_gnn_root"][h]) for h in range(2)]
        Wq = [W.declare(A["L0_mix_Wq"][h]) for h in range(2)]
        Wo = [W.declare(A["L0_mix_Wo"][h]) for h in range(2)]
        Wrel = [[W.declare(A["L0_gnn_weight"][r, h]) for h in range(2)] for r in range(8)]
        Wgate = []
        for h in range(2):
            Wgate.append([W.declare(A["L0_gnn_w_gate"][1, h]), W.declare(A["L0_gnn_w_gate"][0, h])])
        FF = ("k", "q", "v", "f")
        Wnode = {"kqv": [W.declare(A["L0_ffn_kq_nw"]), W.declare(A["L0_ffn_v_nw"], 2)]}
        Wf1, Wf2 = {}, {}

        def declare_units(units):
            for n in range(len(units) + 1):
                if n < len(units):
                    Wf1[units[n]] = W.declare(A[f"L0_ffn_{units[n][0]}_w1"][units[n][1]])
                if n:
                    Wf2[units[n - 1]] = W.declare(A[f"L0_ffn_{units[n - 1][0]}_w2"][units[n - 1][1]])

        units = [(f, g) for f in "kqv" for g in range(8)]
        declare_units(units)
        Wnode["f"] = [W.declare(A["L0_ffn_f_nw"], 2)]
        declare_units([("f", g) for g in range(8)])
        Wgnn, Wk1 = [], []
        for h in range(2):
            Wgnn.append(W.declare(A["L1_gnn_W"][h]))
            Wk1.append(W.declare(A["L1_mix_Wk"][h]))
        Wv1 = [W.declare(A["L1_mix_Wv"][h]) for h in range(2)]
        Wq_of, Wo_of = [{"L0_mix": w0, "L1_mix": [W.declare(A[f"L1_mix_W{n}"][h]) for h in range(2)]} for n, w0 in (("q", Wq), ("o", Wo))]
        Ws1, Ws2 = W.declare(A["L1_ffn_sw1"]), W.declare(A["L1_ffn_sw2"])
        Ws3, We = [], [[], [], []]
        for x in range(9):
            if x < 8:
                We[0].append(W.declare(A["L1_ffn_ew1"][x]))
                We[1].append(W.declare(A["L1_ffn_ew2"][x]))
            if x:
                We[2].append([W.declare(A["L1_ffn_ew3"][x - 1, h], 2) for h in range(2)])
            if x in (3, 7):
                Ws3.append(W.declare(A["L1_ffn_sw3"][x // 4], 2))

        adj = scratch("adjacency", [PT, TT, 8, 640])
        cntd = scratch("counts", [5120])
        STG = [at(f"a_stage{i}", [PT, TT, 8, 64], F32, P1 + 41280 + 10240 * i) for i in range(2)]
        TA = [at(f"at_stage{i}", [64, TT, PT], F32, P1 + 61760 + 2528 * i) for i in range(2)]
        ALLC = [at(f"a_sum{i}", [PT, TT, 64], F32, P1 + 66816 + 1280 * i) for i in range(3)]
        TMP = [at(f"tmp{i}", [PT, 512], F32, P1 + 70688 + 2048 * i) for i in range(2)]
        OHS = at("one_src", [128, 9, 640], F16, SPARE)
        OHK = at("one_key", [128, 9, 128], F16, SPARE + 11520)
        EC = at("e_bucket", [128, 2, LOOK, 2], F32, SPARE + 15136)
        BKV = [at(f"bias_kv{i}", [PT, 512], F32, SPARE + 15200 + 2048 * i) for i in range(2)]
        CST = [at(f"c_stage{i}", [1, 256], F32, P1 + 75424 + 1024 * i) for i in range(2)]
        KN = at("k_rows", [PT, TT, D], F32, P1)
        VN = at("v_rows", [PT, TT, 8, 130], F32, P1 + 20480)

        bias_sem = [q.sem(f"bias_sem{i}") for i in range(3)]
        bias_n = [0]

        def bias_rows(tile, name, *after):
            bias_n[0] += 1
            src = A[name] if isinstance(name, str) else name
            return dma("gpsimd", bias_sem[bias_n[0] % 3], lambda e: e.dma_start(tile, src.partition_broadcast(tile.shape[0])), *after)

        tmp_free = [None, None]

        def keys_tile(dst, b, i, bias, *after):
            w = TMP[i][:, :]
            a = dve(lambda e: e.tensor_tensor(dst, bank(b)[0:PT, :], bias, ALU.add), *after)
            free(b, 1, a)
            m = act(lambda e: e.activation(w, dst, ACT.Relu, scale=-1.0), a, tmp_free[i])
            x = act(lambda e: e.activation(w, w, ACT.Exp, scale=-1.0), m)
            r = act(lambda e: e.activation(dst, dst, ACT.Relu), m)
            s = pool(lambda e: e.tensor_tensor(dst, dst, w, ALU.add), x, r)
            tmp_free[i] = s
            return s

        def values_tile(h, t, b, bias, *after):
            v = dve(lambda e: e.tensor_tensor(VN[:, t, 4 * h:4 * h + 4, 0:128], bank(b)[0:PT, :].rearrange("p (a c) -> p a c", a=4),
                                              bias.rearrange("p (a c) -> p a c", a=4), ALU.add), *after)
            free(b, 1, v)
            return v

        bias_kv = {("k", h): bias_rows(BKV[h][:, :], A["L0_mix_bk"][512 * h:512 * h + 512]) for h in range(2)}
        ones_v = dve(lambda e: e.memset(VN[:, :, :, 128:130], 1.0), iota_ok)
        k_done, v_done, late = [], [], []

        rootd = scratch("x_root", [N, D])
        rsem = [q.sem(f"root_sem{i}") for i in range(2)]
        root_stored = []

        def root_tile(h, t, b, i, s):
            a = act(lambda e: e.activation(TMP[i][:, :], bank(b)[0:PT, :], ACT.Copy), s, tmp_free[i])
            free(b, 1, a)
            tmp_free[i] = dma("scalar", rsem[i], lambda e: e.dma_start(rootd[t * PT:(t + 1) * PT, 512 * h:512 * h + 512], TMP[i][:, :]), a)
            root_stored.append(tmp_free[i])

        def fill_halves():
            n = 0
            for of, w in (("k", Wk), ("v", Wv), ("root", Wroot)):
                for h in range(2):
                    if of == "v":
                        bias_kv["v", h] = bias_rows(BKV[h][:, :], A["L0_mix_bv"][512 * h:512 * h + 512], k_done)
                    for t in range(TT):
                        b = 4 + n % 2
                        for j, part in enumerate(w[h]):
                            s = rows(bank(b)[0:PT, :], XTH, XTL, cols(t), part, (2 * j, 2 * j + 1), j == 0, j == 3, freed[b] if j == 0 else None, xt_ok[t])
                            if t == TT - 1:
                                W.release(part, s)
                            if j == 1:
                                W.split()
                                yield
                        sl = slice(512 * h, 512 * h + 512)
                        if of == "k":
                            late.append(lambda h=h, t=t, b=b, n=n, sl=sl, s=s: k_done.append(keys_tile(KN[:, t, sl], b, n % 2, BKV[h][:, :], s, bias_kv["k", h])))
                        elif of == "root":
                            late.append(lambda h=h, t=t, b=b, n=n, s=s: root_tile(h, t, b, n % 2, s))
                        else:
                            late.append(lambda h=h, t=t, b=b, s=s: v_done.append(values_tile(h, t, b, BKV[h][:, :], s, bias_kv["v", h], ones_v)))
                        n += 1
                        W.split()
                        yield

        W.subtract = pool
        pads = [fill(XTH[:, :, N:NP], 0.0), fill(XTL[:, :, N:NP], 0.0)]
        xt_ok = []
        filler = fill_halves()

        def fill_gap(n=1):
            for _ in range(n):
                next(filler, None)

        def finish_late():
            while late:
                late.pop(0)()

        stats = ln_stats(0, 2, XN, xload)
        normal = [normalize(t, XN[:, t, :], XN[:, t, :], rstd, stats) for t in range(2)]
        stats = ln_stats(2, 5, XN, xload)
        for t in range(2):
            xt_ok.append(transpose_tile(t, XN[:, t, :], XTH, XTL, (6, 0, 2)[t % 3], normal[t]))
        normal += [normalize(t, XN[:, t, :], XN[:, t, :], rstd, stats) for t in range(2, 5)]
        fill_gap(2)
        for t in range(2, 5):
            xt_ok.append(transpose_tile(t, XN[:, t, :], XTH, XTL, (6, 0, 2)[t % 3], normal[t]))
        fill_gap(2)
        ESF = at("e_src", [128, 2, 128], F32, P1 + 62976)
        EKF = at("e_key", [128, 2, 128], F32, P1 + 64000)
        E2 = at("e_cols", [128, 164, 2], F32, SPARE + 13824)
        kmin = at("e_kmin", [128, 2], F32, P1 + 66336)
        kmax = at("e_kmax", [128, 2], F32, P1 + 66368)
        tid = at("e_tid", [128, 2], F32, P1 + 66400)
        bst = at("e_bst", [128, NB], F32, P1 + 66464)
        em = at("e_m", [128, 2, 2, NB], F32, P1 + 66784)
        lohi = at("e_lohi", [NB, 2], F32, P1 + 67424)
        lohr = at("e_lohr", [1, 4, NB], F32, P1 + 67456)
        bnd = at("e_bnd", [1, 4 * NB], I32, P1 + 74784)
        many = const("many", [1, 2], F32)
        manyi = const("many_int", [1, 1], I32)

        EI = [EI0, EI1]
        NE = [128, 36]
        mt = const("sel_tmp", [128, 24], F32)

        def sel(i, n=1):
            return mt[:, i:i + n]

        m_own = dve(lambda e: e.tensor_scalar(sel(10), tidi[:, 0:1], 700.0, None, op0=ALU.add), ti)
        tgt_ok = dve(lambda e: e.tensor_copy(tgt[:, :], tgti[:, :]), gi)
        tf = dve(lambda e: e.tensor_copy(tid[:, :], tidi[:, :]), ti)
        bf = dve(lambda e: e.tensor_copy(bst[:, :], bsti[:, :]), bi)
        lo_hi = []
        edge_cols = []
        for h in range(2):
            def halves(h=h, n=NE[h], E=EI[h]):
                s = dve(lambda e: e.tensor_copy(ESF[0:n, h, :], E[:, 0, :]), eload[h])
                k = dve(lambda e: e.scalar_tensor_tensor(EKF[0:n, h, :], E[:, 1, :], 8.0, E[:, 2, :], op0=ALU.mult, op1=ALU.add), eload[h])
                a = dve(lambda e: e.tensor_reduce(kmin[0:n, h:h + 1], EKF[0:n, h, :], axis=AX.X, op=ALU.min), k)
                b = dve(lambda e: e.tensor_reduce(kmax[0:n, h:h + 1], EKF[0:n, h, :], axis=AX.X, op=ALU.max), k)
                c = dve(lambda e: e.tensor_scalar(em[0:n, h, 0, :], bst[0:n, :], kmax[0:n, h:h + 1], None, op0=ALU.is_le), b, bf)
                d = dve(lambda e: e.tensor_scalar(em[0:n, h, 1, :], bst[0:n, :], 127.0, kmin[0:n, h:h + 1], op0=ALU.add, op1=ALU.is_ge), a, bf)
                f = dve(lambda e: e.tensor_tensor(em[0:n, h, 1, :], em[0:n, h, 0, :], em[0:n, h, 1, :], ALU.mult), c, d)
                g = dve(lambda e: e.tensor_scalar(kmin[0:n, h:h + 1], tid[0:n, h:h + 1], -512.0, None, op0=ALU.add), tf, d)
                i = dve(lambda e: e.tensor_scalar(em[0:n, h, 0, :], em[0:n, h, 1, :], kmin[0:n, h:h + 1], 512.0, op0=ALU.mult, op1=ALU.add), f, g)
                j = dve(lambda e: e.tensor_scalar(kmax[0:n, h:h + 1], tid[0:n, h:h + 1], 1.0, None, op0=ALU.add), tf, c)
                l = dve(lambda e: e.tensor_scalar(em[0:n, h, 1, :], em[0:n, h, 1, :], kmax[0:n, h:h + 1], None, op0=ALU.mult), j, i)
                lo_hi.append(pe(lambda e: e.transpose(bank(0)[0:NB, h * 128:h * 128 + n], em[0:n, h, 0, :], ident[0:n, 0:n]), i, ident_ok, [freed[j] for j in range(4)]))
                lo_hi.append(pe(lambda e: e.transpose(bank(1)[0:NB, h * 128:h * 128 + n], em[0:n, h, 1, :], ident[0:n, 0:n]), l, ident_ok))
                edge_cols.append(pe(lambda e: e.transpose(bank(2)[:, h * 128:h * 128 + n], ESF[0:n, h, :], ident[0:n, 0:n]), s))
                edge_cols.append(pe(lambda e: e.transpose(bank(3)[:, h * 128:h * 128 + n], EKF[0:n, h, :], ident[0:n, 0:n]), k))
            halves()
            finish_late()
            fill_gap(2)
        c0 = act(lambda e: e.activation(E2[:, :, 0], bank(2)[:, 0:164], ACT.Copy), edge_cols)
        c1 = act(lambda e: e.activation(E2[:, :, 1], bank(3)[:, 0:164], ACT.Copy), edge_cols)
        edges_ok = [c0, c1]
        a = dve(lambda e: e.tensor_reduce(lohi[:, 0:1], bank(0)[0:NB, 0:164], axis=AX.X, op=ALU.min), lo_hi)
        b = dve(lambda e: e.tensor_reduce(lohi[:, 1:2], bank(1)[0:NB, 0:164], axis=AX.X, op=ALU.max), lo_hi)
        t0 = pe(lambda e: e.transpose(bank(6)[0:1, 0:NB], lohi[:, 0:1], ident[0:NB, 0:NB]), a, freed[6])
        t1 = pe(lambda e: e.transpose(bank(6)[0:1, NB:2 * NB], lohi[:, 1:2], ident[0:NB, 0:NB]), b)
        fill_gap(2)
        finish_late()
        lo = dve(lambda e: e.tensor_scalar(lohr[:, 0, :], bank(6)[0:1, 0:NB], 164.0 - LOOK, None, op0=ALU.min), t0, t1)
        c = dve(lambda e: e.tensor_scalar(lohr[:, 1, :], lohr[:, 0, :], float(LOOK), None, op0=ALU.add), lo)
        d = dve(lambda e: e.tensor_tensor(lohr[:, 2, :], lohr[:, 1, :], bank(6)[0:1, NB:2 * NB], ALU.max), c)
        f = dve(lambda e: e.tensor_tensor(lohr[:, 3, :], lohr[:, 2, :], lohr[:, 1, :], ALU.subtract), d)
        g = dve(lambda e: e.tensor_reduce(many[:, 0:1], lohr[:, 3, :], axis=AX.X, op=ALU.max), f)
        many_ok = dve(lambda e: e.tensor_scalar(manyi[:, :], many[:, 0:1], 31.0 - LOOK, None, op0=ALU.is_gt), g)
        edges_done = [edges_ok, many_ok]
        bounds_ok = dve(lambda e: e.tensor_copy(bnd[:, :].rearrange("o (g w b) -> o w g b", g=10, w=4), lohr[:, :, :].rearrange("o w (g b) -> o w g b", b=4)), f)
        free(0, 1, a)
        free(1, 1, b)
        free(2, 1, c0)
        free(3, 1, c1)
        free(6, 1, lo, d)

        made, taken = [[q.sem(f"one_{n}{j}") for j in range(4)] for n in ("made", "taken")]
        asem = [q.sem(f"a_sem{i}") for i in range(2)]
        csem = [q.sem(f"c_sem{i}") for i in range(2)]
        regs = {}

        def register(e, name):
            if (e.engine, name) not in regs:
                regs[e.engine, name] = e.alloc_register(f"{e.engine.name}_{name}")
            return regs[e.engine, name]

        def bounds_of(e, g):
            r = [register(e, f"bound{i}") for i in range(16)]
            e.load(r, bnd[0:1, 16 * g:16 * g + 16])
            return r

        bounds = {}

        def load_bounds(add, g):
            def emit(e):
                bounds[e.engine] = bounds_of(e, g)
            return add(emit, bounds_ok)

        looked = []

        def edge_columns(b):
            def emit(e):
                lowest = e.snap(bounds[e.engine][b % 4], min_val=0, max_val=164 - LOOK)
                return e.tensor_copy(EC[:, b % 2, :, :], E2[:, bass.ds(lowest, LOOK), :])
            return dve(emit, edges_ok)

        def one_hot(e, i, b, src, key):
            e.tensor_scalar(OHS[:, i, 0:626], iota16[:, 0:626], src, None, op0=ALU.is_equal)
            return e.tensor_scalar(OHK[:, i, :], iota16[:, 0:128], 128.0 * b, key, op0=ALU.add, op1=ALU.is_equal)

        def one_hots(b, columns_ok):
            made_ok = []
            for k in range(LOOK):
                n = LOOK * b + k
                made_ok.append(dve(lambda e, k=k, n=n: one_hot(e, n % 5, b, EC[:, b % 2, k, 0:1], EC[:, b % 2, k, 1:2]), columns_ok, iota_ok, looked[n - 5] if n >= 5 else None))

            def past(e):
                r = bounds[e.engine]
                it = register(e, "round")
                with e.If_ne(r[12 + b % 4], 0):
                    with e.Fori(r[4 + b % 4], r[8 + b % 4], 4) as i:
                        e.reg_add(it, it, 1)
                        for j in range(4):
                            e.wait_ge(taken[j], it)
                            one_hot(e, 5 + j, b, E2[:, bass.ds(i + j, 1), 0], E2[:, bass.ds(i + j, 1), 1]).then_inc(made[j], 1)
            dve(past)
            return made_ok

        def count(b, s, made_ok):
            ps = bank(2 * s, 2)

            def look(e, i, first, last):
                for m in range(TT):
                    e.matmul(ps[0:PT, 128 * m:128 * m + 128], OHS[:, i, cols(m)], OHK[:, i, :], start=first and m in (0, 4), stop=last, skip_group_check=True)
                return e.matmul(ps[:, 640:768], ones16[:, :], OHK[:, i, :], start=False, stop=last, skip_group_check=True)
            for k in range(LOOK):
                n = LOOK * b + k
                looked.append(pe(lambda e, n=n, k=k: look(e, n % 5, k == 0, k == LOOK - 1), made_ok[k], ones_ok, freed[2 * s] if k == 0 else None, freed[2 * s + 1] if k == 0 else None))

            def past(e):
                r = bounds[e.engine]
                it = register(e, "round")
                with e.If_ne(r[12 + b % 4], 0):
                    with e.Fori(0, r[12 + b % 4], 4):
                        e.reg_add(it, it, 1)
                        for j in range(4):
                            e.wait_ge(made[j], it)
                            look(e, 5 + j, False, True).then_inc(taken[j], 1)
                return e.matmul(ps[0:PT, 0:8], zeros16[:, 0:PT], zeros16[:, 0:8], start=False, stop=True, skip_group_check=True)
            return pe(past, zeros_ok)

        def start_rounds(add, credit):
            def emit(e):
                e.reg_mov(register(e, "round"), 0)
                if credit:
                    for j in range(4):
                        e.sem_inc(taken[j], 1)
            return add(emit)
        start_rounds(dve, False)
        start_rounds(pe, True)
        edges_done.append(bounds_ok)
        stg_free = [edges_done, edges_done]
        stored, cnt_stored, summed, sum_free, evac, at_stored, degrees = [], [], [], [None] * 3, [], [], []
        adjt = scratch("adjacency_sum", [640, N])
        tas = [q.sem(f"ta_sem{i}") for i in range(2)]
        dis = const("rsqrt_degree", [PT, TT], F32)
        deg = const("degree", [PT, 2, TT], F32)
        deg_ok = dve(lambda e: e.memset(deg[:, 0, :], 1.0))

        def sum_kinds(c):
            stg, total = STG[c % 2], ALLC[c % 3][:, :, :]
            a = pool(lambda e: e.tensor_tensor(total, stg[:, :, 0, :], stg[:, :, 1, :], ALU.add), evac[c], sum_free[c % 3], edges_done)
            for r in range(2, 8):
                a = pool(lambda e, r=r: e.tensor_tensor(total, total, stg[:, :, r, :], ALU.add), a)
            summed.append(a)
            stg_free[c % 2] = [stg_free[c % 2], a]

        def turn_sum(c):
            ps = bank(6, 2).rearrange("p (m c) -> p m c", c=128)[0:64, 0:TT, 0:PT]
            i = c % 2

            def emit(e):
                for m in range(TT):
                    ins = e.transpose(ps[:, m, :], ALLC[c % 3][:, m, :], ident[0:PT, 0:PT])
                return ins
            a = pe(emit, summed[c], freed[6], freed[7])
            d = dve(lambda e: e.tensor_reduce(deg[:, 1, :], ALLC[c % 3][:, :, :], axis=AX.X, op=ALU.add), summed[c], degrees[-1] if degrees else deg_ok)
            degrees.append(dve(lambda e: e.tensor_tensor(deg[:, 0, :], deg[:, 0, :], deg[:, 1, :], ALU.add), d))
            b = dve(lambda e: e.scalar_tensor_tensor(TA[i][:, :, :], iota16[0:64, 0:N].rearrange("p (m c) -> p m c", m=TT), tgt[:, c:c + 1], ps,
                                                     op0=ALU.is_equal, op1=ALU.add), a, tgt_ok, edges_done, at_stored[c - 2] if c > 1 else None)
            free(6, 2, b)
            sum_free[c % 3] = [a, d]
            at_stored.append(dma("sync", tas[i], lambda e: e.dma_start(adjt[64 * c:64 * c + 64, :], TA[i][:, :, :].rearrange("p m c -> p (m c)")), b))

        load_bounds(dve, 0)
        columns_ok = edge_columns(0)
        for b in range(NB):
            if b % 4 == 0:
                load_bounds(pe, b // 4)
            made_ok = one_hots(b, columns_ok)
            if b + 1 < NB:
                if b % 4 == 3:
                    load_bounds(dve, b // 4 + 1)
                columns_ok = edge_columns(b + 1)
            p = count(b, b % 2, made_ok)
            c, j = b // 4, b % 4
            if j == 0:
                evac.append([])

            def copy_out(b=b, p=p, c=c, j=j, stg=STG[c % 2], cst=CST[b // 2 % 2]):
                ps = bank(2 * (b % 2), 2)
                x = act(lambda e: e.activation(stg[:, :, :, 16 * j:16 * j + 16], ps[0:PT, 0:640].rearrange("p (m d r) -> p m r d", m=TT, d=16), ACT.Copy),
                        p, stg_free[c % 2] if j == 0 else None)
                y = act(lambda e: e.activation(cst[0:1, 128 * (b % 2):128 * (b % 2) + 128], ps[0:1, 640:768], ACT.Copy), p, cnt_stored[-2:-1] if b % 2 == 0 else None)
                free(2 * (b % 2), 2, x, y)
                evac[c].extend([x, y])
            copy_out()
            if b % 2:
                cnt_stored.append(dma("scalar", csem[b // 2 % 2], lambda e, b=b: e.dma_start(cntd[128 * b - 128:128 * b + 128].unsqueeze(0), CST[b // 2 % 2][:, :]), evac[c][-4:]))
            if j == 3:
                def store(c=c, stg=STG[c % 2]):
                    stored.append(dma("scalar", asem[c % 2], lambda e: e.dma_start(adj.rearrange("p m r d -> p (m r) d")[:, :, 64 * c:64 * c + 64], stg[:, :, :, :].rearrange("p m r d -> p (m r) d")), evac[c]))
                    stg_free[c % 2] = [stored[-1]]
                store()
                sum_kinds(c)
            if j == 2 and c >= 2:
                turn_sum(c - 2)
            finish_late()
            fill_gap()
        while next(filler, True) is None:
            finish_late()
        finish_late()
        turn_sum(8)
        turn_sum(9)
        dis_ok = rsqrt(deg[:, 0, :], dis[:, :], lnt[:, 6, :], lnt[:, 7, :], degrees[-1])
        W.subtract = dve
        mi = const("sel_int", [128, 2], I32)
        tokm = const("sel_token", [128, 1], U32)
        eqm = at("sel_equal", [128, 128], F32, P1 + 75776)
        eqi = at("sel_order", [128, 128], I32, P1 + 75776)
        low = at("sel_lower", [128, 128], F32, P1 + 76288)
        rev8 = const("sel_rev", [128, 8], F32)

        ml = dma("scalar", q.sem("sel_sem"), lambda e: e.dma_start(mi[:, :], A["L1_ffn_index"]))
        m_low = pool(lambda e: e.iota(eqi[:, :], [[1, 128]], base=0, channel_multiplier=-1), k_done)
        m_low = dve(lambda e: e.tensor_scalar(low[:, :], eqi[:, :], 0.0, None, op0=ALU.is_lt), m_low)
        rev_ok = dve(lambda e: e.tensor_scalar(rev8[:, :], iota16[:, 0:8], -1.0, 8.0, op0=ALU.mult, op1=ALU.add), iota_ok)
        m = dve(lambda e: e.tensor_copy(sel(0, 2), mi[:, :]), ml)
        m = dve(lambda e: e.tensor_scalar(sel(2, 2), sel(0, 2), 0.0, None, op0=ALU.is_lt), m)
        m = dve(lambda e: e.tensor_tensor(sel(0), sel(0), sel(2), ALU.add), m)
        m = dve(lambda e: e.scalar_tensor_tensor(sel(1), sel(3), float(N), sel(1), op0=ALU.mult, op1=ALU.add), m)
        m = dve(lambda e: e.tensor_scalar(sel(4), sel(1), 0.0, float(N - 1), op0=ALU.max, op1=ALU.min), m)
        tokm_ok = dve(lambda e: e.tensor_copy(tokm[:, :], sel(4)), m)
        m = dve(lambda e: e.tensor_tensor(sel(5), sel(4), sel(1), ALU.is_equal), tokm_ok)
        m = dve(lambda e: e.scalar_tensor_tensor(sel(5), sel(0), 0.0, sel(5), op0=ALU.is_equal, op1=ALU.mult), m)
        m = dve(lambda e: e.tensor_tensor(sel(6), sel(4), sel(10), ALU.subtract), m, m_own)
        m = dve(lambda e: e.scalar_tensor_tensor(sel(6), sel(6), sel(5), sel(10), op0=ALU.mult, op1=ALU.add), m)
        m = dve(lambda e: e.tensor_copy(eqm[:, :], sel(6).to_broadcast([128, 128])), m, m_low)

        def kept_places(m):
            m = pe(lambda e: e.transpose(bank(5)[:, 0:128], eqm[:, :], ident[:, :]), m, ident_ok, freed[5])
            m = dve(lambda e: e.scalar_tensor_tensor(eqm[:, :], bank(5)[:, 0:128], sel(6), low[:, :], op0=ALU.is_equal, op1=ALU.mult), m, m_low)
            free(5, 1, m)
            m = dve(lambda e: e.tensor_reduce(sel(7), eqm[:, :], axis=AX.X, op=ALU.max), m)
            return dve(lambda e: e.tensor_scalar(sel(7), sel(7), -1.0, 1.0, op0=ALU.mult, op1=ALU.add), m)

        def columns(b, xh, xl, mb, part, first, last, *after):
            wh, wl = W.pair(part)

            def emit(e):
                for j in range(2):
                    kt = 2 * (part % 4) + j
                    c = slice(512 * j + 128 * mb, 512 * j + 128 * mb + 128)
                    for n, (w, x) in enumerate(((wh, xh), (wh, xl), (wl, xh))):
                        for h in range(2):
                            ins = e.matmul(bank(b + h)[:, 0:NH], w[:, c], x[:, kt, NH * h:NH * h + NH],
                                           start=first and j == 0 and n == 0, stop=last and j == 1 and n == 2)
                return ins
            return pe(emit, W.ready(part), *after)

        def mixer(p, XH, XL, x_ok, base, k_done, v_done, before, denominator, finish):
            QT = at(f"q_cols_{p}", [128, 8, NP], F32, base + 20800)
            KV = at(f"kv_{p}", [128, 8, 130], F32, base + 40896)
            tmp = [at(f"q_tmp{i}_{p}", [128, 2, NH], F32, base + 45056 + 2528 * i) for i in range(2)]
            BQ = const(f"bias_q_{p}", [128, 8], F32)
            AO = [at(f"ao{i}_{p}", [PT, D], F32, base + 45056 + 4096 * i) for i in range(2)]
            nrm = [const(f"norm{i}_{p}", [PT, 8], F32) for i in range(2)]
            bq_ok = dma("gpsimd", q.sem(f"bq_{p}"), lambda e: e.dma_start(BQ[:, :], A[f"{p}_bq"]))
            q_done = []
            tmp_free = [before, before]
            for h in range(2):
                for mb in range(4):
                    def queries(h=h, mb=mb, m=4 * h + mb):
                        b, i = 2 * (m % 2), m % 2
                        for j, part in enumerate(Wq_of[p][h]):
                            s = columns(b, XH, XL, mb, part, j == 0, j == 3, freed[b], freed[b + 1], x_ok)
                            if mb == 3:
                                W.release(part, s)
                        W.split()
                        ps = bank(b, 2).rearrange("p (a c) -> p a c", a=2)[:, :, 0:NH]
                        qt = QT[:, m, :].rearrange("p (a c) -> p a c", a=2)
                        r = act(lambda e: e.activation(qt, ps, ACT.Relu, bias=BQ[:, m:m + 1]), s, bq_ok, before)
                        n = dve(lambda e: e.tensor_scalar(tmp[i][:, :, :], ps, BQ[:, m:m + 1], 0.0, op0=ALU.add, op1=ALU.min), s, bq_ok, r, tmp_free[i])
                        x = act(lambda e: e.activation(tmp[i][:, :, :], tmp[i][:, :, :], ACT.Exp), n)
                        d = dve(lambda e: e.tensor_tensor(qt, qt, tmp[i][:, :, :], ALU.add), x, r)
                        free(b, 2, r, n)
                        tmp_free[i] = d
                        q_done.append(d)
                    queries()

            kvp = bank(4, 4).rearrange("p (a c) -> p a c", a=8)

            def outer(e):
                for a in range(8):
                    for t in range(TT):
                        ins = e.matmul(kvp[:, a, 0:130], KN[:, t, 128 * a:128 * a + 128], VN[:, t, a, :], start=t == 0, stop=t == TT - 1)
                return ins
            o = pe(outer, k_done, v_done, [freed[i] for i in range(4, 8)])
            kv_ok = dve(lambda e: e.tensor_tensor(KV[:, :, :], kvp[:, :, 0:130], bdmask[:, :].unsqueeze(1).to_broadcast([128, 8, 130]), ALU.mult), o, bd_ok, before)
            free(4, 4, kv_ok)

            OH = at(f"ao_high_{p}", [128, 8, NP], F32R, base - 20480)
            OL = at(f"ao_low_{p}", [128, 8, NP], F32R, base - 20480 + 20096)
            ao_free, ao_ok = [None, None], []
            heads_done[p] = []
            for t in range(TT):
                halves = []
                for g in range(2):
                    def heads(t=t, g=g, b=2 * g):
                        ps = bank(b, 2).rearrange("p (a c) -> p a c", a=4)

                        def emit(e):
                            for a in range(4):
                                ins = e.matmul(ps[0:PT, a, 0:130], QT[:, 4 * g + a, cols(t)], KV[:, 4 * g + a, :], start=True, stop=True)
                            return ins
                        s = pe(emit, q_done, kv_ok, freed[b], freed[b + 1])
                        n = nrm[g][:, :].rearrange("p (a c) -> p a c", a=4)
                        m = dve(lambda e: e.tensor_scalar(n, ps[0:PT, :, 128:130], 1e-6, None, op0=denominator), s, ao_free[t % 2])
                        r = dve(lambda e: e.reciprocal(nrm[g][:, :], nrm[g][:, :]), m)
                        d = dve(lambda e: e.tensor_tensor(AO[t % 2][:, 512 * g:512 * g + 512].rearrange("p (a c d) -> p a c d", a=4, c=2),
                                                          ps[0:PT, :, 0:128].rearrange("p a (c d) -> p a c d", c=2),
                                                          n.unsqueeze(3).to_broadcast([PT, 4, 2, 64]), ALU.mult), r)
                        free(b, 2, m, d)
                        halves.append(d)
                        heads_done[p].append(d)
                    heads()
                ao_free[t % 2] = halves
                if t:
                    ao_ok.append(transpose_tile(t - 1, AO[(t - 1) % 2][:, :], OH, OL, 4 + 2 * (t % 2), ao_free[(t - 1) % 2], kv_ok))
            ao_ok.append(transpose_tile(4, AO[0][:, :], OH, OL, 4, ao_free[0], kv_ok))
            for t in range(TT):
                ao_free[t % 2] = ao_free[t % 2] + ao_ok[t]
            for h in range(2):
                for t in range(TT):
                    b = (5 * h + t) % 4
                    s = rows_tile(t, Wo_of[p][h], OH, OL, b, ao_ok[t])
                    W.split(4 if t == TT - 1 else 1)
                    finish(h, t, b, s)
            return ao_ok

        heads_done = {}
        acc = scratch("x_mixed", [N, D])
        XB = at("x_base", [PT, TT, D], F32, P1 + 41280)
        BO = at("bias_o", [PT, 512], F32, P1 + 73728)
        bos = q.sem("bo_sem")
        xbs = [q.sem(f"xb_sem{t}") for t in range(TT)]
        abs_ = [q.sem(f"ab_sem{i}") for i in range(3)]
        lnx = const("x_twice", [PT, 2, TT], F32)
        acc_stored, xb_ok = [], {}

        def mixed_base():
            a = dve(lambda e: e.tensor_scalar(lnx[:, 0, :], rstd[:, :], 1.0, None, op0=ALU.add))
            b = dve(lambda e: e.scalar_tensor_tensor(lnx[:, 1, :], lnmv[:, :, 0], -1.0, rstd[:, :], op0=ALU.mult, op1=ALU.mult))
            n, o = {}, None
            for h in range(2):
                o = dma("sync", bos, lambda e, h=h: e.dma_start(BO[:, :], A["L0_mix_bo"][512 * h:512 * h + 512].partition_broadcast(PT)), counted, list(xb_ok.values()))
                for t in range(TT):
                    def tile(h=h, t=t, x=XB[:, t, :], sl=slice(512 * h, 512 * h + 512)):
                        if h == 0:
                            l = dma("scalar", xbs[t], lambda e: e.dma_start(x, A["x"][t * PT:(t + 1) * PT, :]), heads_done["L0_mix"])
                            n[t] = act(lambda e: e.activation(x, x, ACT.Identity, bias=lnx[:, 1, t:t + 1], scale=lnx[:, 0, t:t + 1]), l, a, b)
                        xb_ok[t, h] = pool(lambda e: e.tensor_tensor(x[:, sl], x[:, sl], BO[:, :], ALU.add), n[t], o)
                    tile()

        def add_mixed(h, t, b, s):
            i = (5 * h + t) % 3
            sl = slice(512 * h, 512 * h + 512)
            if not xb_ok:
                mixed_base()
            d = dve(lambda e: e.tensor_tensor(XB[:, t, sl], XB[:, t, sl], bank(b)[0:PT, :], ALU.add), xb_ok[t, h], s)
            free(b, 1, d)
            acc_stored.append(dma("sync", abs_[i], lambda e: e.dma_start(acc[t * PT:(t + 1) * PT, sl], XB[:, t, sl]), d))

        counted = [stored, cnt_stored, at_stored, dis_ok, evac, summed, degrees, k_done, v_done, root_stored]
        W.grow(range(7, 12), counted)
        mixed = mixer("L0_mix", XTH, XTL, [xt_ok, pads], P1 + 20480, k_done, [v_done, ones_v], counted, ALU.max, add_mixed)
        kept_ok = kept_places(m)

        U = at("u_rows", [PT, TT, D], F32, P1)
        AR = [at(f"a_kind{i}", [PT, TT, NP], F32R, P1 + 20480 + 12576 * i) for i in range(2)]
        Y0 = P1 + 45632
        YH = [at(f"y_high{i}", [PT, 512], F32R, Y0 + 4096 * i) for i in range(8)]
        YL = [at(f"y_low{i}", [PT, 512], F32R, Y0 + 4096 * i + 2048) for i in range(8)]
        BR = at("bias_root", [PT, D], F32, Y0 + 7 * 4096)
        rc = const("one_over_count", [PT, TT, 8], F32)
        arsem = [q.sem(f"ar_sem{i}") for i in range(2)]

        done_mix = [acc_stored, mixed, kept_ok]
        cl = dma("gpsimd", q.sem("cnt_sem"), lambda e: e.dma_start(rc[:, :, :], cntd[0:5000].rearrange("(j p r) -> p j r", p=PT, r=8)), cnt_stored)
        c1 = dve(lambda e: e.tensor_scalar(rc[:, :, :], rc[:, :, :], 1.0, None, op0=ALU.max), cl)
        rc_ok = dve(lambda e: e.reciprocal(rc[:, :, :], rc[:, :, :]), c1)
        br_ok = dma("sync", q.sem("br_sem"), lambda e: e.dma_start(BR[:, :], A["L0_gnn_bias"].partition_broadcast(PT)), done_mix)
        u_done = {}
        usem = [q.sem(f"u_sem{t}") for t in range(TT)]
        for t in range(TT):
            def roots(t=t):
                l = dma("sync", usem[t], lambda e: e.dma_start(U[:, t, :], rootd[t * PT:(t + 1) * PT, :]), done_mix, root_stored)
                u_done[t, 0] = u_done[t, 1] = pool(lambda e: e.tensor_tensor(U[:, t, :], U[:, t, :], BR[:, :], ALU.add), l, br_ok)
            roots()
        y_ok = [None] * 8
        y_used = [done_mix] * 7 + [list(u_done.values())]
        ar_ok, ar_used = [None, None], [done_mix, done_mix]
        manyr = {}

        def load_many(e):
            manyr[0] = e.alloc_register("pe_many")
            return e.load(manyr[0], manyi[0:1, 0:1])
        pe(load_many, many_ok)

        def load_kind(r):
            i = r % 2
            ar_ok[i] = dma("gpsimd", arsem[i], lambda e: e.dma_start(AR[i][:, :, 0:N].bitcast(F32), adj[:, :, r, 0:N]), ar_used[i], stored)

        def make_y(r, h, m):
            n = 5 * (2 * r + h) + m
            b, i = n % 4, n % 8
            s = rows_tile(m, Wrel[r][h], XTH, XTL, b, [xt_ok, pads])
            W.split()
            x = act(lambda e: e.activation(YH[i][:, :], bank(b)[0:PT, :], ACT.Copy), s, y_used[i])
            y = dve(lambda e: e.tensor_tensor(YL[i][:, :], bank(b)[0:PT, :], YH[i][:, :], ALU.subtract), x)
            free(b, 1, x, y)
            y_ok[i] = [x, y]

        agg_n = [0]

        def aggregate(r, h):
            slots = [(5 * (2 * r + h) + m) % 8 for m in range(TT)]
            last = []
            banks = []
            for _ in range(TT):
                banks.append(4 + agg_n[0] % 4)
                agg_n[0] += 1

            def products(e, j, dt):
                for m in range(TT):
                    i = slots[m]
                    for n, y in enumerate((YH[i], YL[i])):
                        a, w = AR[r % 2][:, m, cols(j)], y[:, :]
                        if dt == F32:
                            a, w = a.bitcast(F32), w.bitcast(F32)
                        ins = e.matmul(bank(banks[j])[0:PT, :], a, w, start=m == 0 and n == 0, stop=m == TT - 1 and n == 1)
                return ins
            for j in range(TT):
                def one(j=j):
                    b = banks[j]

                    def emit(e):
                        sem, value = s.sem, 1
                        with e.If_ne(manyr[0], 0):
                            products(e, j, F32).then_inc(sem, value)
                        with e.Else():
                            products(e, j, F32R).then_inc(sem, value)
                        return None
                    s = pe(emit, [y_ok[i] for i in slots], ar_ok[r % 2], freed[b])
                    s.own = True
                    u = dve(lambda e: e.scalar_tensor_tensor(U[:, j, 512 * h:512 * h + 512], bank(b)[0:PT, :], rc[:, j, r:r + 1], U[:, j, 512 * h:512 * h + 512],
                                                             op0=ALU.mult, op1=ALU.add), s, rc_ok, u_done[j, h])
                    free(b, 1, u)
                    u_done[j, h] = u
                    last.append(s)
                one()
            for i in slots:
                y_used[i] = last
            if h == 1:
                ar_used[r % 2] = last

        load_kind(0)
        load_kind(1)
        for r in range(8):
            if r == 6:
                W.drop(range(11, 14))
            for h in range(2):
                for m in range(TT):
                    if m == 2 and (r, h) != (0, 0):
                        pr, ph = (r, 0) if h else (r - 1, 1)
                        aggregate(pr, ph)
                        if ph == 1 and pr + 2 < 8:
                            load_kind(pr + 2)
                    make_y(r, h, m)

        G0 = P1 + 20480
        UTH = at("ut_high", [128, 8, NP], F32R, G0)
        UTL = at("ut_low", [128, 8, NP], F32R, G0 + 20096)
        XG = [at(f"x_tile{i}", [PT, D], F32, LENT + 4096 * i) for i in range(2)]
        BG = at("bias_g", [PT, D], F32, LENT + 8192)
        GT = [at(f"g_tile{i}", [PT, 512], F32, G0 + 40192 + 2048 * i) for i in range(4)]
        AP_ = [at(f"a_tile{i}", [PT, 512], F32, G0 + 48384 + 2048 * i) for i in range(4)]
        xgs = [q.sem(f"xg_sem{i}") for i in range(2)]
        aps = [q.sem(f"ap_sem{i}") for i in range(4)]

        def gate_rows(h, t, top, b):
            for j, part in enumerate(Wgate[h][top]):
                s = rows(bank(b)[0:PT, :], UTH if top else XTH, UTL if top else XTL, cols(t), part, (2 * j, 2 * j + 1),
                         top == 0 and j == 0, top == 1 and j == 3, freed[b] if not top else None, ut_ok[t] if top else [xt_ok, pads])
                if t == TT - 1:
                    W.release(part, s)
            W.split()
            return s

        ut_ok, d_ok, xg_free = {}, {}, [None, None]
        gate_rows(0, 0, 0, 0)
        gate_rows(0, 1, 0, 1)
        aggregate(7, 1)
        agg_last = [y_used, ar_used, list(u_done.values())]
        bg_ok = dma("sync", q.sem("bg_sem"), lambda e: e.dma_start(BG[:, :], A["L0_gnn_b_gate"].partition_broadcast(PT)), W.lent())

        def delta(t):
            i = t % 2
            ut_ok[t] = transpose_tile(t, U[:, t, :], UTH, UTL, 6, u_done[t, 0], u_done[t, 1], agg_last)
            l = dma("sync", xgs[i], lambda e: e.dma_start(XG[i][:, :], A["x"][t * PT:(t + 1) * PT, :]), W.lent(), xg_free[i])
            n = normalize(t, XG[i][:, :], XG[i][:, :], rstd, l)
            x = act(lambda e: e.activation(U[:, t, :], U[:, t, :], ACT.Tanh), ut_ok[t])
            d_ok[t] = xg_free[i] = pool(lambda e: e.tensor_tensor(U[:, t, :], U[:, t, :], XG[i][:, :], ALU.subtract), x, n)

        x1_done = {}
        ap_ok, gt_free = [], [None] * 4

        def load_acc(*after):
            n = len(ap_ok)
            h, t = divmod(n, TT)
            if h < 2:
                ap_ok.append(dma("sync", aps[n % 4], lambda e: e.dma_start(AP_[n % 4][:, :], acc[t * PT:(t + 1) * PT, 512 * h:512 * h + 512]), acc_stored, *after))

        def gated(h, t, s):
            i = (5 * h + t) % 4
            sl = slice(512 * h, 512 * h + 512)
            l = ap_ok[5 * h + t]
            z = dve(lambda e: e.tensor_tensor(GT[i][:, :], bank(t)[0:PT, :], BG[:, sl], ALU.add), s, bg_ok, gt_free[i], agg_last)
            free(t, 1, z)
            w = dve(lambda e: e.tensor_tensor(GT[i][:, :], GT[i][:, :], U[:, t, sl], ALU.mult), z, d_ok[t])
            x = dve(lambda e: e.tensor_tensor(U[:, t, sl], GT[i][:, :], AP_[i][:, :], ALU.add), w, l)
            gt_free[i] = x
            load_acc(x)
            x1_done[t, h] = x

        for t in range(2, TT):
            gate_rows(0, t, 0, t)
            delta(t - 2)
        for _ in range(4):
            load_acc(agg_last)
        for t in range(TT):
            s = gate_rows(0, t, 1, t)
            if t + 3 < TT:
                delta(t + 3)
            gated(0, t, s)
        for t in range(TT):
            gate_rows(1, t, 0, t)

        x1d, xn1d = scratch("x1_rows", [N, D]), scratch("xn1_rows", [N, D])
        scale2 = const("scale2", [PT, TT], F32)
        x1s = [q.sem(f"x1_sem{t}") for t in range(TT)]
        n1s = [q.sem(f"n1_sem{t}") for t in range(TT)]
        x1_stored, xn1_stored, xt1_ok = {}, {}, {}

        def ln_then_std(a, b, x, after):
            ve, v, s, w, h = [lnt[:, k, a:b] for k in (0, 2, 3, 4, 5)]
            c = dve(lambda e: e.tensor_scalar(ve, lnmv[:, a:b, 1], EPS, None, op0=ALU.add), moments(a, b, x, after))
            c = dve(lambda e: e.reciprocal(s, ve), c)
            c = dve(lambda e: e.scalar_tensor_tensor(v, lnmv[:, a:b, 1], 1024.0 / 1023.0, s, op0=ALU.mult, op1=ALU.mult), c)
            c = dve(lambda e: e.tensor_scalar(v, v, 1e-30, None, op0=ALU.max), c)
            c = rsqrt(v, s, w, h, c)
            c = dve(lambda e: e.tensor_tensor(v, v, s, ALU.mult), c)
            c = dve(lambda e: e.scalar_tensor_tensor(v, v, EPS, ve, op0=ALU.add, op1=ALU.mult), c)
            return rsqrt(v, scale2[:, a:b], w, h, c)

        K0 = R0 + 67584
        S16 = at("right_kqv", [PT, TT, 3, 256], F16, K0)
        PATH = [[at(f"path{i}{j}", [PT, 3, 256], F16, K0 + 7680 + 1536 * (2 * i + j)) for j in range(2)] for i in range(2)]
        QVP = [at(f"path_qv{t}", [PT, 2, 256], F16, K0 + 13824 + 1024 * t) for t in range(TT)]
        SL16 = [at(f"slot16{i}", [PT, TT, 128], F16, K0 + 18944 + 1280 * i) for i in range(2)]
        PQ = at("path_leaf", [PT, 256], F32, K0 + 21504)
        NB3 = at("node_b", [PT, 768], F32, LENT)
        tokidi = at("tokid_int", [PT, TT], I32, LENT + 4096)
        iotai = at("iota2_int", [128, 128], I32, LENT + 4128)
        tri16 = const("tri16", [128, 128], F16)
        thr = const("group_first", [128, 9], F32)
        tokid = const("tokid", [PT, TT], F32)
        leaf = {f: const(f"leaf_{f}", [PT, TT, n], F32) for f, n in (("k", 1), ("qv", 2), ("f", 1))}
        H16 = const("group_from", [PT, 10, 9], F16)
        G16 = const("group16", [PT, 10, 8], F16)
        gx = const("group_rank", [PT, 10, 8], F32)
        rank = const("rank", [PT, 10], F32)
        grp = const("group_number", [PT, 10], F32)
        MV = const("moving16", [PT, 10, 24], F16)
        stmp = const("slot_tmp", [128, 16], F32)
        cnt = const("group_counts", [1, 40], F32)
        OUTI = {f: const(f"row_{f}", [128, 8], U32) for f in FF}
        LF = {f: const(f"slot_leaf_{f}", [128, 8], F32) for f in FF}
        PLACE = {f: const(f"place_{f}", [PT, TT], F32) for f in FF}
        MV4 = {f: const(f"moving4_{f}", [PT, TT, 4], F16) for f in FF}
        MORE = const("more_rounds", [1, 4], I32)

        def bc(ap, n):
            return ap.unsqueeze(2).to_broadcast([ap.shape[0], ap.shape[1], n])

        def node_logits(f, t, dsts, xh, xl, xs, *after):
            for parts, dst in zip(Wnode[f], dsts):
                w = dst.shape[-1]
                kts = 1024 // w
                for j, part in enumerate(parts):
                    wh, wl = W.pair(part)

                    def emit(e, j=j, wh=wh, wl=wl, w=w, kts=kts, dst=dst, parts=parts):
                        for k in range(kts):
                            c = slice(w * k, w * k + w)
                            for n, (x, y) in enumerate(((xh, wh), (xh, wl), (xl, wh))):
                                ins = e.matmul(dst, x[:, kts * j + k, xs], y[:, c], start=j == 0 and k == 0 and n == 0,
                                               stop=j == len(parts) - 1 and k == kts - 1 and n == 2)
                        return ins
                    s = pe(emit, W.ready(part), *after)
                    if t == TT - 1:
                        W.release(part, s)
            return s

        def goes_right(S, ps, nb, *after):
            return dve(lambda e: e.scalar_tensor_tensor(S, nb, -1.0, ps, op0=ALU.mult, op1=ALU.is_lt), *after)

        def paths(add, S, pair, final, *after):
            n = S.shape[1]
            src, dst = [x[:, 0:n, :] for x in pair]
            last = [add(lambda e, p=src: e.tensor_copy(p[:, :, 1], S[:, :, 0]), *after),
                    add(lambda e, p=src: e.tensor_scalar(p[:, :, 0], S[:, :, 0], -1.0, 1.0, op0=ALU.mult, op1=ALU.add), *after)]
            for l in range(1, 8):
                def level(w=1 << l, src=src, dst=final if l == 7 else dst, last=last):
                    d = dst[:, :, 0:2 * w].rearrange("p n (j c) -> p n j c", c=2)
                    a = add(lambda e: e.tensor_tensor(d[:, :, :, 1], src[:, :, 0:w], S[:, :, w - 1:2 * w - 1], ALU.mult), last)
                    return [add(lambda e: e.tensor_tensor(d[:, :, :, 0], src[:, :, 0:w], d[:, :, :, 1], ALU.subtract), a)]
                last = level()
                src, dst = dst, src
            return last

        pq_free = []

        def numbers(P, lf, *after):
            out = []
            for i in range(P.shape[1]):
                pq_free[:] = [dve(lambda e, i=i: e.scalar_tensor_tensor(PQ[:, :], P[:, i, :], 1.0, iota16[0:PT, 0:256], op0=ALU.mult, op1=ALU.mult, accum_out=lf[:, i:i + 1]), pq_free[:], *after)]
                out += pq_free
            return out

        def route(fs, lf, leaf_ok, b, *after):
            n = len(fs)
            m = TT * n
            ps = bank(b)
            g3 = G16[:, 0:m, :]
            h = dve(lambda e: e.tensor_tensor(H16[:, 0:m, :], thr[0:PT, :].unsqueeze(1).to_broadcast([PT, m, 9]),
                                              bc(lf[:, :, :].rearrange("p t f -> p (t f)"), 9), ALU.is_le), leaf_ok, *after)
            g = dve(lambda e: e.tensor_tensor(g3, H16[:, 0:m, 0:8], H16[:, 0:m, 1:9], ALU.subtract), h)

            def ranks(e):
                for t in range(TT):
                    for u in range(t + 1):
                        ins = e.matmul(ps[0:PT, 8 * n * t:8 * n * t + 8 * n], (tri16 if u == t else ones16)[0:PT, 0:PT], G16[:, n * u:n * u + n, :].rearrange("p f g -> p (f g)"),
                                       start=u == 0, stop=u == t)
                for t in range(TT):
                    ins = e.matmul(ps[0:PT, 128:128 + 8 * n], ones16[0:PT, 0:PT], G16[:, n * t:n * t + n, :].rearrange("p f g -> p (f g)"), start=t == 0, stop=t == TT - 1)
                return ins
            v = [dve(lambda e: e.tensor_tensor(MV[:, 0:m, 8:16], g3, bc(lf[:, :, :].rearrange("p t f -> p (t f)"), 8), ALU.mult), g, *after),
                 dve(lambda e: e.tensor_copy(MV[:, 0:m, 16:24], g3), g, *after)]
            for i in range(n):
                v.append(dve(lambda e, i=i: e.tensor_tensor(MV[:, i:m:n, 0:8], G16[:, i:m:n, :], bc(tokid[:, :], 8), ALU.mult), g, tok_ok))
            yield
            k = pe(ranks, g, tri_ok, freed[b])
            yield
            x = dve(lambda e: e.tensor_tensor(gx[:, 0:m, :], ps[0:PT, 0:8 * m].rearrange("p (m g) -> p m g", g=8), g3, ALU.mult), k, *after)
            r = dve(lambda e: e.tensor_reduce(rank[:, 0:m], gx[:, 0:m, :], axis=AX.X, op=ALU.add), x)
            hot = []
            for i in range(n):
                hot += [dve(lambda e, t=t, i=i: e.tensor_scalar(SL16[i][:, t, :], iota16[0:PT, 0:128], rank[:, n * t + i:n * t + i + 1], None, op0=ALU.is_equal), r, *after)
                        for t in range(TT)]
            c = dve(lambda e: e.tensor_copy(cnt[:, 0:8 * n], ps[0:1, 128:128 + 8 * n]), k, *after)
            yield

            def tokens(e):
                for i in range(n):
                    for t in range(TT):
                        ins = e.matmul(ps[:, 192 + 32 * i:216 + 32 * i], SL16[i][:, t, :], MV[:, n * t + i, :], start=t == 0, stop=t == TT - 1)
                return ins
            s = pe(tokens, hot, v, x, c)
            yield
            read = []
            for i, f in enumerate(fs):
                def layer(i=i, f=f, o=ps[:, 192 + 32 * i:216 + 32 * i], tmp=stmp[:, 8 * i:8 * i + 8]):
                    w = dve(lambda e: e.tensor_scalar(tmp, o[:, 16:24], -4096.0, 4096.0, op0=ALU.mult, op1=ALU.add), s, *after)
                    j = dve(lambda e: e.tensor_copy(LF[f][:, :], o[:, 8:16]), s)
                    w = dve(lambda e: e.tensor_tensor(OUTI[f][:, :], tmp, o[:, 0:8], ALU.add), w)
                    routed[f] = {"rows": w, "leaves": j, "all": [w, j]}
                    read.extend([w, j])
                layer()
            free(b, 1, read)
            yield
            y = dve(lambda e: e.tensor_reduce(grp[:, 0:m], H16[:, 0:m, :], axis=AX.X, op=ALU.add), g)
            y = dve(lambda e: e.tensor_scalar(grp[:, 0:m], grp[:, 0:m], -1.0, None, op0=ALU.add), y)
            c = dve(lambda e: e.tensor_reduce(cnt[:, 24:24 + n], cnt[:, 0:8 * n].rearrange("o (f g) -> o f g", g=8), axis=AX.X, op=ALU.max), c)
            for i, f in enumerate(fs):
                def more(i=i, f=f, c=c):
                    lt, gr, rk = lf[:, :, i], grp[:, i:m:n], rank[:, i:m:n]
                    out = [dve(lambda e: e.scalar_tensor_tensor(PLACE[f][:, :], gr, 640.0, rk, op0=ALU.mult, op1=ALU.add), y, r),
                           dve(lambda e: e.scalar_tensor_tensor(MV4[f][:, :, 1], gr, -32.0, lt, op0=ALU.mult, op1=ALU.add), y),
                           dve(lambda e: e.tensor_copy(MV4[f][:, :, 0], tokid[:, :]), tok_ok),
                           dve(lambda e: e.memset(MV4[f][:, :, 2], 1.0)),
                           dve(lambda e: e.tensor_copy(MV4[f][:, :, 3], lt), leaf_ok)]
                    a = dve(lambda e: e.tensor_scalar(cnt[:, 32:36], iota16[0:1, 1:5], 128.0, cnt[:, 24 + i:25 + i], op0=ALU.mult, op1=ALU.is_lt), c)
                    a = dve(lambda e: e.tensor_reduce(cnt[:, 36:37], cnt[:, 32:36], axis=AX.X, op=ALU.add), a)
                    a = dve(lambda e: e.tensor_copy(MORE[:, "kqvf".index(f):"kqvf".index(f) + 1], cnt[:, 36:37]), a)
                    routed[f]["all"] += out + [a]
                    return a
                c = more()
            yield

        routed = {}

        def finish(stages, n=-1):
            while n and next(stages, 0) is None:
                n -= 1

        x_used = list(d_ok.values())
        ia = pool(lambda e: e.iota(iotai[:, :], [[1, 128]], base=0, channel_multiplier=-1), x_used)
        ib = pool(lambda e: e.iota(tokidi[:, :], [[PT, TT]], base=0, channel_multiplier=1), x_used)
        tri_ok = dve(lambda e: e.tensor_scalar(tri16[:, :], iotai[:, :], 0.0, None, op0=ALU.is_gt), ia)
        tok_ok = [dve(lambda e: e.tensor_copy(tokid[:, :], tokidi[:, :]), ib),
                  dve(lambda e: e.tensor_scalar(thr[:, :], iota16[:, 0:9], 32.0, None, op0=ALU.mult))]
        nbs = q.sem("nb_sem")
        nb_ok = dma("sync", nbs, lambda e: e.dma_start(NB3[:, :], A["L0_ffn_nb"][0:768].partition_broadcast(PT)), x_used)
        second, decided, qv_path = {}, {}, {}
        leaf_ok = {"k": [], "qv": []}

        def norm_twice(a, b):
            x = {t: [x1_done[t, 0], x1_done[t, 1]] for t in range(a, b)}
            for t in range(a, b):
                x1_stored[t] = dma("sync", x1s[t], lambda e, t=t: e.dma_start(x1d[t * PT:(t + 1) * PT, :], U[:, t, :]), x[t])
            c = ln_then_std(a, b, U, x)
            for t in range(a, b):
                second[t] = normalize(t, U[:, t, :], U[:, t, :], scale2, c, x1_stored[t])
                xn1_stored[t] = dma("sync", n1s[t], lambda e, t=t: e.dma_start(xn1d[t * PT:(t + 1) * PT, :], U[:, t, :]), second[t])

        def turn_second(t):
            xt1_ok[t] = transpose_tile(t, U[:, t, :], XTH, XTL, (6, 0, 6, 4, 6)[t], second[t])

        def decide(t):
            b = 2 - 2 * (t % 2)
            s = node_logits("kqv", t, [bank(b)[0:PT, :], bank(b + 1)[0:PT, 0:256]], XTH, XTL, cols(t), xt1_ok[t], pads, freed[b], freed[b + 1])
            S = S16[:, t, :, :].rearrange("p f j -> p (f j)")
            r = [goes_right(S[:, 0:256], bank(b)[0:PT, 0:256], NB3[:, 0:256], s, nb_ok)]
            k = paths(dve, S16[:, t, 0:1, :], PATH[1], PATH[1][1][:, 0:1, :], r, leaf_ok["k"][-1:])
            leaf_ok["k"].append(numbers(PATH[1][1][:, 0:1, :], leaf["k"][:, t, :], k))
            r += [goes_right(S[:, 256:512], bank(b)[0:PT, 256:512], NB3[:, 256:512], s, nb_ok),
                  goes_right(S[:, 512:768], bank(b + 1)[0:PT, 0:256], NB3[:, 512:768], s, nb_ok)]
            free(b, 2, r)
            qv_path[t] = r
            return s

        def follow_qv(t):
            qv_path[t] = paths(pool, S16[:, t, 1:3, :], PATH[0], QVP[t][:, :, :], qv_path[t])

        for t in range(TT):
            gated(1, t, gate_rows(1, t, 1, t))
            if t == 1:
                norm_twice(0, 2)
        turn_second(0)
        turn_second(1)
        W.split(2)
        norm_twice(2, 5)
        decide(0)
        follow_qv(0)
        turn_second(2)
        decide(1)
        follow_qv(1)
        turn_second(3)
        turn_second(4)
        decide(2)
        follow_qv(2)
        decide(3)
        logits_done = decide(4)
        decided = [qv_path[t] for t in range(3, TT)]
        xt1_all, xn1_all = [xt1_ok[t] for t in range(TT)], [xn1_stored[t] for t in range(TT)]
        stages = route("k", leaf["k"], leaf_ok["k"], 4)
        finish(stages, 5)
        yb = {f: scratch(f"leaf_rows_{f}", [N, D]) for f in FF}
        XGH = [at(f"xg_high{i}", [128, 8, 128], F32R, R0 + 8192 * i) for i in range(2)]
        XGL = [at(f"xg_low{i}", [128, 8, 128], F32R, R0 + 8192 * i + 4096) for i in range(2)]
        HM = [at(f"h_masked{i}", [128, 512], F32, R0 + 16384 + 2048 * i) for i in range(2)]
        HTH = [at(f"ht_high{i}", [128, 4, 128], F32R, R0 + 20480 + 4096 * i) for i in range(2)]
        HTL = [at(f"ht_low{i}", [128, 4, 128], F32R, R0 + 20480 + 4096 * i + 2048) for i in range(2)]
        YO = [at(f"y_out{i}", [128, D], F32, R0 + 28672 + 4096 * i) for i in range(2)]
        XR = [at(f"xg_rows{i}", [128, D], F32, R0 + 36864 + 4096 * i) for i in range(2)]
        LMT = [at(f"leaf_cols{i}", [128, 128], F32R, R0 + 45056 + 512 * i) for i in range(3)]
        LM = at("leaf_mask", [128, 128], F32, R0 + 46592)
        BR1, BL1, BH1 = [at(f"b1_{n}", [128, 512], dt, R0 + o) for n, dt, o in (("raw", F32, 47104), ("low", F32R, 47104), ("high", F32R, 49152))]
        BR2, BL2, BH2 = [at(f"b2_{n}", [128, D], dt, R0 + o) for n, dt, o in (("raw", F32, 51200), ("low", F32R, 51200), ("high", F32R, 55296))]
        QA = [at(f"q_rows{i}", [PT, D], F32, R0 + 59392 + 4096 * i) for i in range(2)]
        sx = [q.sem(f"xg2_sem{i}") for i in range(2)]
        sb = [q.sem(f"leaf_b_sem{i}") for i in range(2)]
        sy = [q.sem(f"yo_sem{i}") for i in range(2)]
        sqa = [q.sem(f"qa_sem{i}") for i in range(2)]

        def rows_of(table, index):
            return dict(in_=table, out_offset=None, in_offset=bass.IndirectOffsetOnAxis(ap=index, axis=0))

        class Leaves:

            def __init__(self):
                self.n = 0
                self.xg_free, self.xt_free, self.hm_free, self.ht_free = [[None, None] for _ in range(4)]
                self.yo_free, self.lm_free, self.lmt_free = [None, None], None, [None, None, None]
                self.b_free, self.b_ok, self.unsplit = [None, None], [None, None], [None, None]

            def biases(self, layer, f, half, *after):
                raw, lo, hi = ((BR1, BL1, BH1), (BR2, BL2, BH2))[layer]
                src = A[f"L0_ffn_{f}_bd"][half] if layer == 0 else A[f"L0_ffn_{f}_b2"][128 * half:128 * half + 128, :]
                l = dma("sync", sb[layer], lambda e: e.dma_start(raw[:, :], src), self.b_free[layer], *after)
                self.unsplit[layer] = lambda: self.split(layer, raw, lo, hi, l, *after)

            def split(self, layer, raw, lo, hi, l, *after):
                h = act(lambda e: e.activation(hi[:, :], raw[:, :], ACT.Copy), l, self.b_free[layer], *after)
                self.b_ok[layer] = [h, dve(lambda e: e.tensor_tensor(lo[:, :], raw[:, :], hi[:, :], ALU.subtract), h)]

            def split_biases(self, layer):
                if self.unsplit[layer]:
                    self.unsplit[layer]()
                    self.unsplit[layer] = None

            def gather(self, n, f, g, table, ready, *after):
                i = n % 2
                return dma("gpsimd", sx[i], lambda e: e.indirect_dma_start(out=XR[i][:, :], **rows_of(table, OUTI[f][:, g:g + 1]), bounds_check=N - 1, oob_is_err=False),
                           ready, self.xg_free[i], *after)

            def turn(self, n, f, g, got, lf, *after):
                i = n % 2
                ps = bank(0, 2).rearrange("p (k c) -> p k c", k=8)
                m = dve(lambda e: e.tensor_scalar(LM[:, :], iota16[:, 128 * (g // 4):128 * (g // 4) + 128], LF[f][:, g:g + 1], None, op0=ALU.is_equal), lf, self.lm_free, *after)

                def emit(e):
                    for k in range(8):
                        ins = e.transpose(ps[:, k, :], XR[i][:, 128 * k:128 * k + 128], ident[:, :])
                    return ins
                a = pe(emit, got, freed[0], freed[1])
                t = pe(lambda e: e.transpose(bank(3)[:, 0:128], LM[:, :], ident[:, :]), m, freed[3])
                h = act(lambda e: e.activation(XGH[i][:, :, :], ps, ACT.Copy), a, self.xt_free[i], *after)
                l = dve(lambda e: e.tensor_tensor(XGL[i][:, :, :], ps, XGH[i][:, :, :], ALU.subtract), h)
                o = act(lambda e: e.activation(LMT[n % 3][:, :], bank(3)[:, 0:128], ACT.Copy), t, self.lmt_free[n % 3], *after)
                free(0, 2, h, l)
                free(3, 1, o)
                self.xg_free[i] = a
                return [h, l], [t, m, o]

            def first(self, n, f, g, xt, lm, gelu, *after):
                i, b = n % 2, 7
                for j, part in enumerate(Wf1[f, g]):
                    s = rows(bank(b), XGH[i], XGL[i], slice(0, 128), part, (2 * j, 2 * j + 1), j == 0, False, freed[b], xt)
                    W.release(part, s)
                    W.split()
                    if j == 1:
                        self.split_biases(0)

                def bias(e):
                    e.matmul(bank(b), LMT[n % 3][:, :], BH1[:, :], start=False, stop=False)
                    return e.matmul(bank(b), LMT[n % 3][:, :], BL1[:, :], start=False, stop=True)
                s = pe(bias, lm, self.b_ok[0])
                self.b_free[0] = s
                self.xt_free[i] = s
                hm = HM[i][:, :].rearrange("p (l w) -> p l w", w=16)
                mask = bc(LM[:, 32 * (g % 4):32 * (g % 4) + 32], 16)
                if gelu:
                    c = act(lambda e: e.activation(HM[i][:, :], bank(b), ACT.Gelu), s, self.hm_free[i], *after)
                    d = dve(lambda e: e.tensor_tensor(hm, hm, mask, ALU.mult), c)
                else:
                    c = d = dve(lambda e: e.scalar_tensor_tensor(hm, bank(b).rearrange("p (l w) -> p l w", w=16), 0.0, mask, op0=ALU.max, op1=ALU.mult), s, self.hm_free[i], *after)
                free(b, 1, c)
                self.lm_free = [d, lm]
                return d

            def turn_h(self, n, d, *after):
                i = n % 2
                ps = bank(4).rearrange("p (k c) -> p k c", k=4)

                def emit(e):
                    for k in range(4):
                        ins = e.transpose(ps[:, k, :], HM[i][:, 128 * k:128 * k + 128], ident[:, :])
                    return ins
                a = pe(emit, d, freed[4])
                h = act(lambda e: e.activation(HTH[i][:, :, :], ps, ACT.Copy), a, self.ht_free[i], *after)
                l = dve(lambda e: e.tensor_tensor(HTL[i][:, :, :], ps, HTH[i][:, :, :], ALU.subtract), h)
                free(4, 1, h, l)
                self.hm_free[i] = a
                return [h, l]

            def second(self, n, f, g, ht, *after):
                i = n % 2

                for k, part in enumerate(Wf2[f, g]):
                    wh, wl = W.pair(part)

                    def emit(e, k=k, wh=wh, wl=wl):
                        for h in range(2):
                            c = slice(512 * h, 512 * h + 512)
                            e.matmul(bank(5 + h), HTH[i][:, k, :], wh[:, c], start=k == 0, stop=False)
                            e.matmul(bank(5 + h), HTH[i][:, k, :], wl[:, c], start=False, stop=False)
                            ins = e.matmul(bank(5 + h), HTL[i][:, k, :], wh[:, c], start=False, stop=False)
                        return ins
                    s = pe(emit, W.ready(part), ht, [freed[5], freed[6]] if k == 0 else None)
                    W.release(part, s)
                    W.split()
                    if k == 1:
                        self.split_biases(1)
                self.ht_free[i] = s

                def bias(e):
                    for h in range(2):
                        c = slice(512 * h, 512 * h + 512)
                        e.matmul(bank(5 + h), LMT[n % 3][:, :], BH2[:, c], start=False, stop=False)
                        ins = e.matmul(bank(5 + h), LMT[n % 3][:, :], BL2[:, c], start=False, stop=True)
                    return ins
                s = self.b_free[1] = self.lmt_free[n % 3] = pe(bias, self.b_ok[1])
                y = act(lambda e: e.activation(YO[i][:, :], bank(5, 2), ACT.Copy), s, self.yo_free[i], *after)
                free(5, 2, y)
                d = dma("gpsimd", sy[i], lambda e: e.indirect_dma_start(
                    out=yb[f], out_offset=bass.IndirectOffsetOnAxis(ap=OUTI[f][:, g:g + 1], axis=0), in_=YO[i][:, :], in_offset=None,
                    bounds_check=N - 1, oob_is_err=False), y, routed[f]["rows"])
                self.yo_free[i] = d
                return d

            def run(self, units, table, table_ok, routed, gelu, between, *after):
                got, xt, lm, ht, stored = {}, {}, {}, {}, {}
                n0, count = self.n, len(units)
                clean = [fill(XR[i][:, :], 0.0, *after) if n0 == 0 else None for i in range(2)]

                def fetch(u):
                    f, g = units[u]
                    got[u] = self.gather(n0 + u, f, g, table, [routed[f]["rows"], table_ok, clean], *after)

                def turn(u):
                    f, g = units[u]
                    xt[u], lm[u] = self.turn(n0 + u, f, g, got[u], routed[f]["leaves"], *after)
                fetch(0)
                fetch(1)
                self.biases(0, units[0][0], 0, *after)
                self.biases(1, units[0][0], 0, *after)
                turn(0)
                for u in range(count + 1):
                    if u < count:
                        f, g = units[u]
                        d = self.first(n0 + u, f, g, xt[u], lm[u], gelu, *after)
                    if u + 1 < count:
                        turn(u + 1)
                        if (u + 1) % 4 == 0:
                            self.biases(0, units[u + 1][0], (u + 1) // 4 % 2, *after)
                    if u + 2 < count:
                        fetch(u + 2)
                    if u:
                        f, g = units[u - 1]
                        stored[f, g] = self.second(n0 + u - 1, f, g, ht[u - 1], *after)
                        if u % 4 == 0 and u < count:
                            self.biases(1, units[u][0], u // 4 % 2, *after)
                    if u < count:
                        ht[u] = self.turn_h(n0 + u, d, *after)
                    between(u, stored)
                self.n += count
                return stored

        M0 = K0
        RX = at("more_rows", [128, D], F32, M0)
        RT = at("more_cols", [128, 8, 128], F32, M0 + 4096)
        RW = at("more_weights", [128, 1024], F32, M0 + 8192)
        RB = at("more_b1", [128, 512], F32, M0 + 12288)
        RH = at("more_h", [128, 512], F32, M0 + 14336)
        RHT = at("more_ht", [128, 4, 128], F32, M0 + 16384)
        RS = at("more_slot", [PT, TT, 128], F16, M0 + 18432)
        RC = at("more_shift", [PT, TT], F32, M0 + 19712)
        RI = at("more_index", [128, 4], U32, M0 + 19744)
        RM = at("more_mask", [128, 32], F32, M0 + 19776)
        RV = at("more_values", [128, 8], F32, M0 + 19904)
        PLN = at("more_current", [128, 2], F32, M0 + 19936)
        chain, fetched, begun = [{f: q.sem(f"more_{n}_{f}") for f in FF} for n in ("step", "rows", "begun")]

        def round_steps(f, table, gelu):
            ps = bank(3)
            w1, w2, b1 = A[f"L0_ffn_{f}_w1"], A[f"L0_ffn_{f}_w2"], A[f"L0_ffn_{f}_b1"]
            steps = []

            def step(engine):
                return lambda emit: steps.append((engine, emit))

            @step("vector")
            def _(e, g):
                return e.tensor_scalar(RC[:, :], PLACE[f][:, :], PLN[0:PT, 0:1], None, op0=ALU.subtract)

            @step("vector")
            def _(e, g):
                for t in range(TT):
                    ins = e.tensor_scalar(RS[:, t, :], iota16[0:PT, 0:128], RC[:, t:t + 1], None, op0=ALU.is_equal)
                return ins

            @step("tensor")
            def _(e, g):
                for t in range(TT):
                    ins = e.matmul(ps[:, 0:4], RS[:, t, :], MV4[f][:, t, :], start=t == 0, stop=t == TT - 1)
                return ins

            @step("vector")
            def _(e, g):
                return e.tensor_copy(RV[:, 0:4], ps[:, 0:4])

            @step("vector")
            def _(e, g):
                e.tensor_copy(RI[:, 0:1], RV[:, 0:1])
                e.tensor_copy(RI[:, 2:3], RV[:, 3:4])
                e.tensor_scalar(RM[:, :], iota16[:, 0:32], RV[:, 1:2], None, op0=ALU.is_equal)
                return e.tensor_scalar(RV[:, 4:5], RV[:, 2:3], -4096.0, 4096.0, op0=ALU.mult, op1=ALU.add)

            @step("vector")
            def _(e, g):
                return e.tensor_tensor(RI[:, 1:2], RV[:, 4:5], RV[:, 0:1], ALU.add)

            @step("gpsimd")
            def _(e, g):
                return e.indirect_dma_start(out=RX[:, :], **rows_of(table, RI[:, 0:1]))

            def turn(src, dst, k0):
                @step("tensor")
                def _(e, g):
                    for k in range(4):
                        ins = e.transpose(ps[:, 128 * k:128 * k + 128], src[:, 128 * (k0 + k):128 * (k0 + k) + 128], ident[:, :])
                    return ins

                @step("scalar")
                def _(e, g):
                    return e.activation(dst[:, k0:k0 + 4, :], ps.rearrange("p (k c) -> p k c", k=4), ACT.Copy)

            turn(RX, RT, 0)
            turn(RX, RT, 4)
            for j in range(4):
                @step("sync")
                def _(e, g, j=j):
                    return e.dma_start(RW[:, :], w1[bass.ds(g, 1), :, 1024 * j:1024 * j + 1024].rearrange("o p c -> (o p) c"))

                @step("tensor")
                def _(e, g, j=j):
                    for k in range(2):
                        ins = e.matmul(ps, RT[:, 2 * j + k, :], RW[:, 512 * k:512 * k + 512], start=j == 0 and k == 0, stop=j == 3 and k == 1)
                    return ins

            @step("sync")
            def _(e, g):
                return e.dma_start(RB[:, :], b1[bass.ds(g, 1), :].rearrange("o c -> (o c)").partition_broadcast(128))

            @step("vector")
            def _(e, g):
                return e.tensor_tensor(RH[:, :], ps, RB[:, :], ALU.add)

            @step("scalar")
            def _(e, g):
                return e.activation(RH[:, :], RH[:, :], ACT.Gelu if gelu else ACT.Relu)

            @step("vector")
            def _(e, g):
                h = RH[:, :].rearrange("p (l w) -> p l w", w=16)
                return e.tensor_tensor(h, h, bc(RM[:, :], 16), ALU.mult)

            turn(RH, RHT, 0)
            for h in range(2):
                for k in range(4):
                    @step("sync")
                    def _(e, g, h=h, k=k):
                        c = 1024 * k + 512 * h
                        return e.dma_start(RW[:, 0:512], w2[bass.ds(g, 1), :, c:c + 512].rearrange("o p c -> (o p) c"))

                    @step("tensor")
                    def _(e, g, k=k):
                        return e.matmul(ps, RHT[:, k, :], RW[:, 0:512], start=k == 0, stop=k == 3)

                @step("scalar")
                def _(e, g, h=h):
                    return e.activation(RX[:, 512 * h:512 * h + 512], ps, ACT.Copy)

            @step("gpsimd")
            def _(e, g):
                return e.indirect_dma_start(out=RW[:, :], **rows_of(A[f"L0_ffn_{f}_b2"], RI[:, 2:3]))

            @step("vector")
            def _(e, g):
                return e.tensor_tensor(RX[:, :], RX[:, :], RW[:, :], ALU.add)

            @step("gpsimd")
            def _(e, g):
                return e.indirect_dma_start(out=yb[f], out_offset=bass.IndirectOffsetOnAxis(ap=RI[:, 1:2], axis=0), in_=RX[:, :], in_offset=None,
                                            bounds_check=N - 1, oob_is_err=False)

            @step("vector")
            def _(e, g):
                return e.tensor_scalar(PLN[:, 0:1], PLN[:, 0:1], 640.0, None, op0=ALU.add)

            @step("vector")
            def _(e, g):
                return e.tensor_scalar(PLN[:, 1:2], PLN[:, 0:1], 5120.0, -4992.0, op0=ALU.is_ge, op1=ALU.mult)

            @step("vector")
            def _(e, g):
                return e.tensor_tensor(PLN[:, 0:1], PLN[:, 0:1], PLN[:, 1:2], ALU.add)

            return steps

        def more_rounds(fs, table, gelu, *after):
            first = "kqvf".index(fs[0])
            ready = [routed[f]["all"] for f in fs]

            def rounds(e, engine, f, more):
                steps = round_steps(f, table, gelu)
                at_step = register(e, "at_step")
                e.reg_mov(at_step, 16)
                if engine == "vector":
                    e.memset(PLN[:, :], 128.0).then_inc(chain[f], 16)
                if engine == "gpsimd":
                    moved = register(e, "moved")
                    e.reg_mov(moved, 0)
                with e.Fori(0, more, 1):
                    with e.Fori(0, 8, 1) as g:
                        passed = 0
                        for n, (who, run) in enumerate(steps):
                            if who == engine:
                                e.reg_add(at_step, at_step, 16 * (n - passed))
                                passed = n
                                e.wait_ge(chain[f], at_step)
                                if engine == "gpsimd":
                                    e.sem_inc(begun[f], 1)
                                    e.reg_add(moved, moved, 16)
                                    run(e, g).then_inc(fetched[f], 16)
                                    e.wait_ge(fetched[f], moved)
                                    e.sem_inc(chain[f], 16)
                                else:
                                    run(e, g).then_inc(chain[f], 16)
                        e.reg_add(at_step, at_step, 16 * (len(steps) - passed))
                e.wait_ge(chain[f], at_step)
                e.sem_inc(begun[f], 1)

            def on(engine):
                def emit(e):
                    more = [register(e, f"more{i}") for i in range(len(fs))]
                    e.load(more, MORE[0:1, first:first + len(fs)])
                    for i, f in enumerate(fs):
                        with e.If_ne(more[i], 0):
                            rounds(e, engine, f, more[i])
                return emit
            for engine in q.ENGINES:
                q.add(engine, on(engine), flat([ready, freed[3], after] if engine == "vector" else ready))

        leaves = Leaves()
        asm_n = [0]
        qa_free = [None, None]

        def collect(f, t, stored, *after):
            i = asm_n[0] % 2
            asm_n[0] += 1
            ys = [stored[f, g] for g in range(8)]
            return i, dma("sync", sqa[i], lambda e: e.dma_start(QA[i][:, :], yb[f][t * PT:(t + 1) * PT, :]), ys, qa_free[i], *after)

        KTH = at("kt_high", [128, 8, NP], F32R, K0)
        KTL = at("kt_low", [128, 8, NP], F32R, K0 + 20096)
        QTH = at("qt_high", [128, 8, 126], F32R, K0 + 40192)
        QTL = at("qt_low", [128, 8, 126], F32R, K0 + 40192 + 4032)
        E = [at(f"weights{t}", [PT, NP], F32, LENT + 2528 * t if t < 4 else K0 + 48256) for t in range(TT)]
        smax = const("soft_max", [PT, 2], F32)
        ssum = const("soft_sum", [PT, TT, 2], F32)
        routed_all, stages_qv = [], []
        kt_ok, qt_ok, exp_ok, score_ok, held = {}, {}, {}, {}, {}

        def turn_tile(x, hi, lo, b, *after):
            ps = bank(b, 2).rearrange("p (k c) -> p k c", k=8)[:, :, 0:PT]

            def emit(e):
                for k in range(8):
                    ins = e.transpose(ps[:, k, :], x[:, 128 * k:128 * k + 128], ident[0:PT, 0:PT])
                return ins
            a = pe(emit, freed[b], freed[b + 1], *after)
            h = act(lambda e: e.activation(hi[:, :, 0:PT], ps, ACT.Copy), a, *after)
            l = dve(lambda e: e.tensor_tensor(lo[:, :, 0:PT], ps, hi[:, :, 0:PT], ALU.subtract), h)
            free(b, 2, h, l)
            return [h, l]

        def scores(t):
            def emit(e):
                for k in range(8):
                    for n, (x, w) in enumerate(((QTH, KTH), (QTH, KTL), (QTL, KTH))):
                        for h in range(2):
                            ins = e.matmul(bank(2 + h)[0:PT, 0:NH], x[:, k, 0:PT], w[:, k, NH * h:NH * h + NH], start=k == 0 and n == 0, stop=k == 7 and n == 2)
                return ins
            s = score_ok[t] = pe(emit, qt_ok[t], k_ok, freed[2], freed[3])
            ps = bank(2, 2)[0:PT, :].rearrange("p (a c) -> p a c", a=2)[:, :, 0:NH]
            m = smax[:, t % 2:t % 2 + 1]
            a = dve(lambda e: e.tensor_reduce(m, ps, axis=AX.XY, op=ALU.max), s, exp_ok.get(t - 2))
            a = dve(lambda e: e.tensor_scalar(m, m, -1.0 / 32.0, None, op0=ALU.mult), a)
            x = [act(lambda e, h=h, w=w: e.activation(E[t][:, NH * h:NH * h + w], bank(2 + h)[0:PT, 0:w], ACT.Exp, bias=m, scale=1.0 / 32.0, accum_out=ssum[:, t, h:h + 1]),
                     a, W.lent(), routed_all) for h, w in ((0, NH), (1, N - NH))]
            free(2, 2, x)
            exp_ok[t] = x

        def between_kqv(u, stored):
            if u == 13:
                W.drop(range(11, 14))
            if u == 0:
                follow_qv(3)
                follow_qv(4)
                finish(stages)
                routed_all.append(routed["k"]["all"])
            if u < 2:
                for t in ((0, 1, 2), (3, 4))[u]:
                    leaf_ok["qv"].append(numbers(QVP[t][:, :, :], leaf["qv"][:, t, :], qv_path[t]))
            if u == 1:
                stages_qv.append(route("qv", leaf["qv"], leaf_ok["qv"], 2, routed_all))
            if 1 <= u < 7:
                finish(stages_qv[0], 1)
            if u == 6:
                routed_all.extend([routed["q"]["all"], routed["v"]["all"], leaf_ok["qv"]])
            if u == 8:
                more_rounds("kqv", xn1d, False, routed_all)
            t = u - 10
            if 0 <= t < TT:
                i, c = held["k"]
                kt_ok[t] = transpose_tile(t, QA[i][:, :], KTH, KTL, 0, c, routed_all)
                qa_free[i] = kt_ok[t]
            if 0 <= t + 1 < TT:
                held["k"] = collect("k", t + 1, stored, logits_done)
            if t == TT:
                kt = [kt_ok[i] for i in range(TT)]
                pad = [dve(lambda e, x=x: e.tensor_copy(x[:, :, N:NP], x[:, :, N - 1:N].to_broadcast([128, 8, NP - N])), kt) for x in (KTH, KTL)]
                k_ok.extend([kt, pad])
            t = u - 20
            if 0 <= t < TT:
                i, c = held["q"]
                qt_ok[t] = turn_tile(QA[i][:, :], QTH, QTL, 0, c, score_ok.get(t - 1), routed_all)
                qa_free[i] = qt_ok[t]
                scores(t)
            if 0 <= t + 1 < TT:
                held["q"] = collect("q", t + 1, stored)

        k_ok = []
        W.grow(range(11, 14), decided, x_used)
        W.ahead = 4
        W.pooled = (1, 3)
        W.split(8)
        leaf_stored = leaves.run(units, xn1d, xn1_all, routed, False, between_kqv, logits_done, xt1_all, xn1_all)

        VH = at("v_high", [PT, TT, D], F32R, R0)
        VL = at("v_low", [PT, TT, D], F32R, R0 + 20480)
        YTH = [at(f"yt_high{i}", [128, 8, 126], F32R, o) for i, o in enumerate((R0 + 40960, K0 + 2560))]
        YTL = [at(f"yt_low{i}", [128, 8, 126], F32R, o) for i, o in enumerate((R0 + 44992, K0 + 13824))]
        ETH = [at(f"et_high{i}", [PT, TT, 126], F32R, R0 + 49024 + 5056 * i) for i in range(2)]
        ETL = [at(f"et_low{i}", [PT, TT, 126], F32R, R0 + 49024 + 5056 * i + 2528) for i in range(2)]
        SF16 = at("right_f", [PT, TT, 1, 256], F16, K0)
        NBF = at("node_b_f", [PT, 256], F32, K0 + 22528)
        X2 = at("x2", [PT, TT, D], F32, K0 + 24576)
        yd = scratch("y_rows", [N, D])
        sinv = const("soft_inv", [PT, TT], F32)
        x2l = [q.sem(f"x2l_sem{t}") for t in range(TT)]
        x2d = scratch("x2_rows", [N, D])

        leaf_done = [leaf_stored[f, g] for f in "kqv" for g in range(8)]
        scored = [score_ok[t] for t in range(TT)]
        nbf_ok = dma("scalar", nbs, lambda e: e.dma_start(NBF[:, :], A["L0_ffn_nb"][768:1024].partition_broadcast(PT)), scored)
        si = dve(lambda e: e.tensor_tensor(sinv[:, :], ssum[:, :, 0], ssum[:, :, 1], ALU.add), [exp_ok[t] for t in range(TT)])
        sinv_ok = dve(lambda e: e.reciprocal(sinv[:, :], sinv[:, :]), si)
        v_ok, et_ok, att_ok, y_done, y_stored, turned, f_leaf = {}, {}, {}, {}, {}, {}, []
        yt_free, base_ok = {}, {}

        def take_v(t):
            i, c = collect("v", t, leaf_stored)
            h = act(lambda e: e.activation(VH[:, t, :], QA[i][:, :], ACT.Copy), c, leaf_done)
            l = dve(lambda e: e.tensor_tensor(VL[:, t, :], QA[i][:, :], VH[:, t, :], ALU.subtract), h)
            qa_free[i] = v_ok[t] = [h, l]

        def turn_weights(t):
            ps = bank(4, 2)[0:PT, :].rearrange("p (k c) -> p k c", c=128)[:, 0:TT, 0:PT]

            def emit(e):
                for k in range(TT):
                    ins = e.transpose(ps[:, k, :], E[t][:, k * PT:(k + 1) * PT], ident[0:PT, 0:PT])
                return ins
            a = pe(emit, exp_ok[t], freed[4], freed[5])
            h = act(lambda e: e.activation(ETH[t % 2][:, :, 0:PT], ps, ACT.Copy), a, leaf_done, att_ok.get(t - 2))
            l = dve(lambda e: e.tensor_tensor(ETL[t % 2][:, :, 0:PT], ps, ETH[t % 2][:, :, 0:PT], ALU.subtract), h)
            free(4, 2, h, l)
            et_ok[t] = [h, l]
            return a

        def attend(t):
            xh, xl = ETH[t % 2], ETL[t % 2]
            rs = slice(t * PT, (t + 1) * PT)
            for k in range(TT):
                def emit(e, k=k):
                    for n, (x, v) in enumerate(((xh, VH), (xh, VL), (xl, VH))):
                        for h in range(2):
                            ins = e.matmul(bank(6 + h)[0:PT, :], x[:, k, 0:PT], v[:, k, 512 * h:512 * h + 512], start=k == 0 and n == 0, stop=k == TT - 1 and n == 2)
                    return ins
                s = pe(emit, et_ok[t], v_ok[k], freed[6], freed[7])
            att_ok[t] = s
            y = y_done[t] = dve(lambda e: e.scalar_tensor_tensor(X2[:, t, :], bank(6, 2)[0:PT, :], sinv[:, t:t + 1], X2[:, t, :], op0=ALU.mult, op1=ALU.add), s, sinv_ok, xn_back[t])
            free(6, 2, y)
            y_stored[t] = dma("sync", x2l[t], lambda e: e.dma_start(yd[rs, :], X2[:, t, :]), y)

        def turn_y(t):
            turned[t] = turn_tile(X2[:, t, :], YTH[t % 2], YTL[t % 2], 0, y_done[t], leaf_done, scored, yt_free.get(t - 2))

        def decide_f(t):
            b = 2 + t % 2
            s = node_logits("f", t, [bank(b)[0:PT, 0:256]], YTH[t % 2], YTL[t % 2], slice(0, PT), turned[t], freed[b])
            yt_free[t] = s
            W.split(2)
            g = goes_right(SF16[:, t, 0, :], bank(b)[0:PT, 0:256], NBF[:, :], s, nbf_ok)
            free(b, 1, g)
            p = paths(dve, SF16[:, t, :, :], PATH[0], PATH[0][1][:, 0:1, :], g, scored, f_leaf[-1:])
            f_leaf.append(numbers(PATH[0][1][:, 0:1, :], leaf["f"][:, t, :], p))

        def add_x1(t):
            i = asm_n[0] % 2
            asm_n[0] += 1
            l = dma("sync", sqa[i], lambda e: e.dma_start(QA[i][:, :], x1d[t * PT:(t + 1) * PT, :]), x1_stored[t], qa_free[i])
            base_ok[t] = qa_free[i] = pool(lambda e: e.tensor_tensor(X2[:, t, :], X2[:, t, :], QA[i][:, :], ALU.add), l, turned[t], y_stored[t])

        xn_back = [dma("sync", x2l[t], lambda e, t=t: e.dma_start(X2[:, t, :], xn1d[t * PT:(t + 1) * PT, :]), scored) for t in range(TT)]
        for t in range(2):
            turn_weights(t)
        for t in range(TT):
            take_v(t)
        for t in range(TT):
            attend(t)
            if t + 2 < TT:
                e_last = turn_weights(t + 2)
            if t:
                turn_y(t - 1)
            if t > 1:
                decide_f(t - 2)
                add_x1(t - 2)
        W.grow(range(11, 14), e_last)
        turn_y(4)
        decide_f(3)
        decide_f(4)
        finish(route("f", leaf["f"], f_leaf, 4, scored))
        add_x1(3)
        add_x1(4)
        attended = [list(yt_free.values()), list(y_done.values()), list(turned.values()), list(att_ok.values()), list(et_ok.values())]

        f_routed = [routed["f"]["all"], f_leaf, attended]
        W.ahead, W.pooled = 4, (3,)
        f_stored = leaves.run([("f", g) for g in range(8)], yd, list(y_stored.values()), routed, True, lambda u, stored: None, attended)
        more_rounds("f", yd, True, f_routed)
        W.ahead, W.pooled = 6, ()
        x2_done, x2_stored, x2_normal, xt2_ok = {}, {}, {}, {}
        f_done = [f_stored["f", g] for g in range(8)]
        XQ = [at(f"x2_tile{t}", [PT, D], F32, R0 + o) for t, o in enumerate((59392, 63488, 51200, 55296, 47104))]
        f_back = [dma("sync", x2l[t], lambda e, t=t: e.dma_start(XQ[t][:, :], yb["f"][t * PT:(t + 1) * PT, :]), f_done, list(base_ok.values())) for t in range(TT)]
        for t in range(TT):
            add = dve if t == 0 else pool
            x2_done[t] = add(lambda e, t=t: e.tensor_tensor(X2[:, t, :], X2[:, t, :], XQ[t][:, :], ALU.add), base_ok[t], f_back[t])
            x2_stored[t] = dma("sync", x2l[t], lambda e, t=t: e.dma_start(x2d[t * PT:(t + 1) * PT, :], X2[:, t, :]), x2_done[t])
        shift = lnx[:, 0, :]
        for a, b in ((0, 1), (1, 3), (3, 5)):
            def finish_x2(a=a, b=b):
                r = ln_stats(a, b, X2, x2_done)
                r = dve(lambda e: e.scalar_tensor_tensor(shift[:, a:b], lnmv[:, a:b, 0], -1.0, rstd[:, a:b], op0=ALU.mult, op1=ALU.mult), r)
                for t in range(a, b):
                    x2_normal[t] = act(lambda e, t=t: e.activation(XQ[t][:, :], X2[:, t, :], ACT.Identity, bias=shift[:, t:t + 1], scale=rstd[:, t:t + 1]), r, x2_done[t])
                for t in range(a, b):
                    xt2_ok[t] = transpose_tile(t, XQ[t][:, :], XTH, XTL, 2 * (t % 2), x2_normal[t], f_done)
            finish_x2()
        x2_done, x2_stored, x2_normal, xt2_ok = [[d[t] for t in range(TT)] for d in (x2_done, x2_stored, x2_normal, xt2_ok)]
        GH = at("gnn_high", [PT, TT, 512], F32R, R0 + 69632)
        GL = at("gnn_low", [PT, TT, 512], F32R, R0 + 69632 + 10240)
        AT = at("adjacency_t", [PT, TT, NP], F32R, R0 + 92160)
        GB = at("bias_gnn", [PT, 512], F32, R0 + 114976)
        BO1 = at("bias_o1", [PT, D], F32, R0 + 114528)
        SG = [at(f"gnn_row{i}", [PT, 512], F32, o) for i, o in enumerate((R0 + 67584, R0 + 90112, R0 + 104736, R0 + 65536))]
        acc1 = scratch("x2_mixed", [N, D])
        atsem = q.sem("at_sem")
        sgs = [q.sem(f"sg_sem{i}") for i in range(4)]
        sgo = [q.sem(f"sgo_sem{i}") for i in range(4)]
        BK1 = at("bias_k1", [PT, D], F32, R0 + 106784)
        BV1 = at("bias_v1", [PT, D], F32, R0 + 97472)
        gb_ok = [bias_rows(GB[:, :], A["L1_gnn_b"][0:512], attended)]
        at_ok = dma("sync", atsem, lambda e: e.dma_start(AT[:, :, 0:N].bitcast(F32), adjt[0:N, :].rearrange("(j p) s -> p j s", p=PT)),
                    x2_normal, x2_stored, at_stored)
        bk1 = bias_rows(BK1[:, :], "L1_mix_bk", x2_normal, x2_stored)
        pads2 = [fill(x[:, :, N:NP], 0.0, f_done, attended) for x in (XTH, XTL)]
        x2_free = [x2_normal, x2_stored, xt2_ok]
        g_ok, acc1_stored = {}, []
        g_used = None
        k1_done = []
        tmp_free[:] = [x2_free, x2_free]

        def gnn_rows(h, t, used):
            b = (5 * h + t) % 4
            sl = slice(512 * h, 512 * h + 512)
            s = rows_tile(t, Wgnn[h], XTH, XTL, b, [xt2_ok[t], pads2])
            W.split()
            w = SG[t % 4]
            a = dve(lambda e: e.tensor_tensor(w[:, :], bank(b)[0:PT, :], GB[:, :], ALU.add), s, gb_ok[h], sg_free[t % 4])
            gb_used[:] = [a]
            free(b, 1, a)
            x = act(lambda e: e.activation(GH[:, t, :], w[:, :], ACT.Copy, scale=dis[:, t:t + 1]), a, dis_ok, used)
            y = dve(lambda e: e.scalar_tensor_tensor(GL[:, t, :], w[:, :], dis[:, t:t + 1], GH[:, t, :], op0=ALU.mult, op1=ALU.subtract), x, used)
            g_ok[t] = [x, y]
            sg_free[t % 4] = [x, y]

        def keys1(h):
            for t in range(TT):
                b = 4 + t % 4
                s = rows_tile(t, Wk1[h], XTH, XTL, b, [xt2_ok[t], pads2])
                W.split()
                sl = slice(512 * h, 512 * h + 512)
                k1_done.append(keys_tile(KN[:, t, sl], b, t % 2, BK1[:, sl], s, bk1, x2_free))

        def gnn_sum(h):
            last = []
            sl = slice(512 * h, 512 * h + 512)

            def products(e, j, dt):
                for m in range(TT):
                    for n, y in enumerate((GH, GL)):
                        a, w = AT[:, m, cols(j)], y[:, m, :]
                        if dt == F32:
                            a, w = a.bitcast(F32), w.bitcast(F32)
                        ins = e.matmul(bank(j % 4)[0:PT, :], a, w, start=m == 0 and n == 0, stop=m == TT - 1 and n == 1)
                return ins
            for j in range(TT):
                def one(j=j, b=j % 4, w=SG[j % 4]):
                    rs = slice(j * PT, (j + 1) * PT)
                    l = dma("gpsimd", sgs[j % 4], lambda e: e.dma_start(w[:, :], x2d[rs, sl]), sg_free[j % 4], x2_stored)

                    def emit(e):
                        with e.If_ne(manyr[0], 0):
                            products(e, j, F32).then_inc(s.sem, 1)
                        with e.Else():
                            products(e, j, F32R).then_inc(s.sem, 1)
                        return None
                    s = pe(emit, [g_ok[m] for m in range(TT)], at_ok, freed[b])
                    s.own = True
                    last.append(s)
                    u = dve(lambda e: e.scalar_tensor_tensor(w[:, :], bank(b)[0:PT, :], dis[:, j:j + 1], w[:, :], op0=ALU.mult, op1=ALU.add), s, l)
                    free(b, 1, u)
                    d = dma("scalar", sgo[j % 4], lambda e: e.dma_start(acc1[rs, sl], w[:, :]), u)
                    sg_free[j % 4] = d
                    acc1_stored.append(d)
                one()
            return last

        sg_free = [attended, attended, x2_free, x2_free]
        gb_used = []
        for h in range(2):
            for t in range(TT):
                gnn_rows(h, t, g_used)
            if h == 0:
                gb_ok.append(bias_rows(GB[:, :], A["L1_gnn_b"][512:1024], gb_used))
                keys1(0)
            g_used = gnn_sum(h)
        bv1 = bias_rows(BV1[:, :], "L1_mix_bv", g_used)
        before1 = [g_used, acc1_stored, x2_free]
        ones_v1 = dve(lambda e: e.memset(VN[:, :, :, 128:130], 1.0), before1)
        keys1(1)
        v1_done = []
        for h in range(2):
            for t in range(TT):
                b = (5 * h + t) % 4
                s = rows_tile(t, Wv1[h], XTH, XTL, b, [xt2_ok, pads2])
                W.split()
                v1_done.append(values_tile(h, t, b, BV1[:, 512 * h:512 * h + 512], s, bv1, ones_v1))

        X3 = at("x3_rows", [PT, TT, D], F32, R0 + 81472)
        X4 = [at(f"x4_tile{i}", [PT, D], F32, R0 + 101952 + 4096 * i) for i in range(3)]
        x3d, x4d = scratch("x3_rows_kept", [N, D]), scratch("x4_rows", [N, D])
        x3s = [q.sem(f"x3_sem{t}") for t in range(TT)]
        x3_half, x3_base, x3_stored, x4_normal, x4_stored, xt4_ok = {}, {}, {}, {}, {}, {}
        bo1_ok = bias_rows(BO1[:, :], "L1_mix_bo", k1_done, acc1_stored)

        def mixed_base1():
            for t in range(TT):
                l = dma("sync", x3s[t], lambda e, t=t: e.dma_start(X3[:, t, :], acc1[t * PT:(t + 1) * PT, :]), heads_done["L1_mix"], acc1_stored)
                x3_base[t] = pool(lambda e, t=t: e.tensor_tensor(X3[:, t, :], X3[:, t, :], BO1[:, :], ALU.add), l, bo1_ok)

        def fourth(a, b):
            x = {t: [x3_half[t, 0], x3_half[t, 1]] for t in range(a, b)}
            for t in range(a, b):
                x3_stored[t] = dma("sync", x3s[t], lambda e, t=t: e.dma_start(x3d[t * PT:(t + 1) * PT, :], X3[:, t, :]), x[t])
            r = ln_stats(a, b, X3, x)
            r = dve(lambda e: e.scalar_tensor_tensor(shift[:, a:b], lnmv[:, a:b, 0], -1.0, rstd[:, a:b], op0=ALU.mult, op1=ALU.mult), r)
            for t in range(a, b):
                x4_normal[t] = act(lambda e, t=t: e.activation(X4[t % 3][:, :], X3[:, t, :], ACT.Identity, bias=shift[:, t:t + 1], scale=rstd[:, t:t + 1]),
                                   r, xt4_ok.get(t - 3), x4_stored.get(t - 3), heads_done["L1_mix"], ao1_ok)
                x4_stored[t] = dma("sync", x3s[t], lambda e, t=t: e.dma_start(x4d[t * PT:(t + 1) * PT, :], X4[t % 3][:, :]), x4_normal[t])

        def turn_fourth(t):
            xt4_ok[t] = transpose_tile(t, X4[t % 3][:, :], XTH, XTL, 4 + 2 * (t % 2), x4_normal[t])

        ao1_ok = []

        def add_mixed1(h, t, b, s):
            sl = slice(512 * h, 512 * h + 512)
            if not x3_base:
                mixed_base1()
            d = dve(lambda e: e.tensor_tensor(X3[:, t, sl], X3[:, t, sl], bank(b)[0:PT, :], ALU.add), x3_base[t], s)
            free(b, 1, d)
            x3_half[t, h] = d
            if h:
                if t == 0:
                    ao1_ok.append(s)
                if t == 2:
                    turn_fourth(0)
                if t == 4:
                    turn_fourth(1)
                if t % 2 == 0:
                    fourth(max(t - 1, 0), t + 1)

        mixed1 = mixer("L1_mix", XTH, XTL, [xt2_ok, pads2], P1 + 20480, k1_done, [v1_done, ones_v1], [before1, k1_done, v1_done], ALU.add, add_mixed1)
        def keep_at(name, shape, dt, offset):
            return at(name, shape, dt, R0 + offset)

        SHTH, SHTL = [keep_at(n, [128, 4, NP], F32R, o) for n, o in (("sh_high", 40192), ("sh_low", 50240))]
        XMH, XML = [keep_at(n, [128, 8, 128], F32R, o) for n, o in (("xm_high", 60288), ("xm_low", 64384))]
        XMR = keep_at("xm_rows", [128, D], F32, 68480)
        SB1, SB2, SLG, SLB = [keep_at(f"shared_row{i}", [PT, 512], F32, o) for i, o in enumerate((114528, 116576, 76672, 78720))]
        WGR, WGH, WGL = keep_at("gates", [128, 80], F32, 80768), keep_at("gates_high", [128, 8, 10], F32R, 81088), None
        WGL = keep_at("gates_low", [128, 8, 10], F32R, 80768)
        ELG, ELB = [keep_at(f"expert_row{i}", [128, 512], F32, 72576 + 2048 * i) for i in range(2)]
        S1 = [keep_at(f"shared_1{t}", [PT, 512], F32, 81472 + 4096 * t) for t in range(TT)]
        S2 = [keep_at(f"shared_2{i}", [PT, 512], F32, 83520 + 4096 * i) for i in range(2)]
        X3L = [keep_at(f"x3_back{i}", [PT, D], F32, 81472 + 4096 * i) for i in range(2)]
        EBR, EBL = [keep_at(f"expert_b_{n}", [8, 2, 512], dt, 104000) for n, dt in (("raw", F32), ("low", F32R))]
        EBH = [keep_at(f"expert_b_high{j}", [8, 512], F32R, 91712 + 4096 * j) for j in range(2)]
        ONE8 = keep_at("expert_row_of_ones", [8, 8, 128], F32R, 99904)
        H1 = [keep_at(f"expert_1{i}", [128, 512], F32, 108096 + 2048 * i) for i in range(2)]
        ZTH, ZTL = [keep_at(n, [128, 4, 128], F32R, o) for n, o in (("zt_high", 114240), ("zt_low", 116288))]
        OHM = keep_at("sel_onehot", [128, 640], F32R, 0)
        EMH, EML = [keep_at(n, [128, D], F32R, o) for n, o in (("em_high", 2560), ("em_low", 6656))]
        ER = keep_at("eb3_rows", [128, D], F32, 10752)
        SB3 = keep_at("shared_b3", [PT, D], F32, 14848)
        SO = keep_at("shared_out", [PT, TT, D], F32, 18944)
        MGB = const("gate_b", [128, 20], F32)
        sc = const("scores", [128, 10], F32)
        se = const("scores_tmp", [128, 24], F32)
        ohe = const("expert_onehot", [128, 8], F32)
        swo = const("weight_one", [128, 2], F32)
        expert = const("expert_index", [128, 1], U32)
        scl = const("token_scale", [PT, TT], F32)
        est = const("expert_stats", [128, 2, 16], F32)

        x3_all = [x3_half[t, h] for t in range(TT) for h in range(2)]
        mgb_ok = dma("sync", q.sem("mgb_sem"), lambda e: e.dma_start(MGB[:, :], A["L1_ffn_gate_b"].partition_broadcast(128)))
        wgl = dma("sync", q.sem("wg_sem"), lambda e: e.dma_start(WGR[:, :], A["L1_ffn_gates"]), heads_done["L1_mix"])
        srow = [bias_rows(x[:, :], f"L1_ffn_{n}", list(x3_base.values())) for x, n in ((SB1, "sb1"), (SB2, "sb2"))]

        W.pooled = (1, 3)

        def shared_1(t):
            b = t % 4
            s = rows_tile(t, Ws1, XTH, XTL, b, [xt4_ok[t]])
            W.split(4 if t == TT - 1 else 1)
            a = dve(lambda e: e.tensor_tensor(S1[t][:, :], bank(b)[0:PT, :], SB1[:, :], ALU.add), s, srow[0], x3_stored[t], x4_normal[t])
            free(b, 1, a)
            return act(lambda e: e.activation(S1[t][:, :], S1[t][:, :], ACT.Silu), a)

        def norm_of(x, st, p, *after):
            a = dve(lambda e: e.bn_stats(st[0:p, 0:6], x), *after)
            b = dve(lambda e: e.bn_aggr(st[0:p, 12:14], st[0:p, 0:6]), a)
            c = dve(lambda e: e.tensor_scalar(st[0:p, 14:15], st[0:p, 13:14], EPS, None, op0=ALU.add), b)
            return rsqrt(st[0:p, 14:15], st[0:p, 15:16], st[0:p, 11:12], st[0:p, 10:11], c)

        s2_free, s2_out, sh_ok = [None, None], [], []

        def shared_2(t, one):
            b, i = t % 4, t % 2
            s = rows_tile(t, Ws2, XTH, XTL, b, [xt4_ok[t]])
            W.split(4 if t == TT - 1 else 1)
            u = S1[t][:, :]
            a = dve(lambda e: e.tensor_tensor(S2[i][:, :], bank(b)[0:PT, :], SB2[:, :], ALU.add), s, srow[1], s2_free[i])
            free(b, 1, a)
            s2_out.append(a)
            m = dve(lambda e: e.tensor_tensor(u, u, S2[i][:, :], ALU.mult), a, one)
            s2_free[i] = m
            r = norm_of(u, est[:, i, :], PT, m, sh_ok[t - 2] if t > 1 else None)
            n = dve(lambda e: e.tensor_scalar(u, u, est[0:PT, i, 12:13], est[0:PT, i, 15:16], op0=ALU.subtract, op1=ALU.mult), r)
            g = pool(lambda e: e.tensor_tensor(u, u, SLG[:, :], ALU.mult), n, srow[2])
            sh_ok.append(pool(lambda e: e.tensor_tensor(u, u, SLB[:, :], ALU.add), g, srow[3]))
            return s

        def expert_biases():
            ebs = q.sem("eb_sem")
            for j in range(2):
                ebl = dma("sync", ebs, lambda e, j=j: e.dma_start(EBR[:, j, :], A[f"L1_ffn_eb{j + 1}"]), x4_free)
            ebh = [act(lambda e, j=j: e.activation(EBH[j][:, :], EBR[:, j, :], ACT.Copy), ebl) for j in range(2)]
            low = [dve(lambda e, j=j: e.tensor_tensor(EBL[:, j, :], EBR[:, j, :], EBH[j][:, :], ALU.subtract), ebh) for j in range(2)]
            ones = dve(lambda e: e.tensor_copy(ONE8[:, :, :], ident[0:8, 0:8].unsqueeze(2).to_broadcast([8, 8, 128])), x4_free)
            return [ebh, low, ones]

        def select():
            ps = bank(4, 2).rearrange("p (k c) -> p k c", k=8)

            def emit(e):
                for k in range(8):
                    ins = e.transpose(ps[:, k, :], XMR[:, 128 * k:128 * k + 128], ident[:, :])
                return ins
            a = pe(emit, got_m, freed[4], freed[5])
            h = act(lambda e: e.activation(XMH[:, :, :], ps, ACT.Copy), a, x3_all)
            l = dve(lambda e: e.tensor_tensor(XML[:, :, :], ps, XMH[:, :, :], ALU.subtract), h)
            free(4, 2, h, l)
            return [h, l]

        def scores_of(xm):
            def emit(e):
                for k in range(8):
                    for n, (x, w) in enumerate(((XMH, WGH), (XMH, WGL), (XML, WGH))):
                        ins = e.matmul(bank(4)[:, 0:10], x[:, k, :], w[:, k, :], start=k == 0 and n == 0, stop=k == 7 and n == 2)
                return ins
            s = pe(emit, xm, wg_ok, freed[4])
            a = dve(lambda e: e.tensor_tensor(sc[:, :], bank(4)[:, 0:10], MGB[:, 0:10], ALU.add), s, mgb_ok)
            free(4, 1, a)
            a = act(lambda e: e.activation(sc[:, :], sc[:, :], ACT.Sigmoid), a)
            b = dve(lambda e: e.tensor_tensor(se[:, 0:8], sc[:, 1:9], MGB[:, 10:18], ALU.add), a)
            c = dve(lambda e: e.tensor_reduce(se[:, 8:9], se[:, 0:8], axis=AX.X, op=ALU.max), b)
            c = dve(lambda e: e.scalar_tensor_tensor(se[:, 0:8], se[:, 0:8], se[:, 8:9], rev8[:, :], op0=ALU.is_ge, op1=ALU.mult), c, rev_ok)
            c = dve(lambda e: e.tensor_reduce(se[:, 9:10], se[:, 0:8], axis=AX.X, op=ALU.max), c)
            hot = dve(lambda e: e.tensor_scalar(ohe[:, :], rev8[:, :], se[:, 9:10], None, op0=ALU.is_equal), c)
            index = dve(lambda e: e.tensor_scalar(expert[:, :], se[:, 9:10], -1.0, 8.0, op0=ALU.mult, op1=ALU.add), c)
            d = dve(lambda e: e.tensor_tensor(se[:, 12:20], ohe[:, :], sc[:, 1:9], ALU.mult), hot)
            d = dve(lambda e: e.tensor_reduce(se[:, 21:22], se[:, 12:20], axis=AX.X, op=ALU.add), d)
            d = dve(lambda e: e.tensor_copy(se[:, 20:21], sc[:, 0:1]), d)
            f = dve(lambda e: e.tensor_reduce(se[:, 10:11], se[:, 20:22], axis=AX.X, op=ALU.max), d)
            f = dve(lambda e: e.tensor_scalar(se[:, 20:22], se[:, 20:22], se[:, 10:11], None, op0=ALU.subtract), f)
            f = act(lambda e: e.activation(se[:, 20:22], se[:, 20:22], ACT.Exp), f)
            g = dve(lambda e: e.tensor_reduce(se[:, 11:12], se[:, 20:22], axis=AX.X, op=ALU.add), f)
            g = dve(lambda e: e.reciprocal(se[:, 11:12], se[:, 11:12]), g)
            w = dve(lambda e: e.tensor_scalar(se[:, 20:22], se[:, 20:22], se[:, 11:12], None, op0=ALU.mult), g)
            return hot, index, w

        one = []
        for t in range(TT):
            one.append(shared_1(t))
            if t + 2 < TT:
                turn_fourth(t + 2)
        x3_stored, x4_stored, x4_normal, xt4_ok = [[d[t] for t in range(TT)] for d in (x3_stored, x4_stored, x4_normal, xt4_ok)]
        x4_free = [x3_stored, x4_stored, x4_normal, xt4_ok]
        srow += [bias_rows(x[:, :], f"L1_ffn_{n}", x3_all) for x, n in ((SLG, "s_ln_g"), (SLB, "s_ln_b"))]
        erow = [bias_rows(x[:, :], f"L1_ffn_sel_ln_{n}", x3_all) for x, n in ((ELG, "g"), (ELB, "b"))]
        got_m = dma("gpsimd", q.sem("xm_sem"), lambda e: e.indirect_dma_start(out=XMR[:, :], **rows_of(x4d, tokm[:, 0:1])), x4_stored, x3_all, tokm_ok)
        wgh = act(lambda e: e.activation(WGH[:, :, :].rearrange("p a b -> p (a b)"), WGR[:, :], ACT.Copy), wgl)
        wg_ok = [wgh, dve(lambda e: e.tensor_tensor(WGL[:, :, :].rearrange("p a b -> p (a b)"), WGR[:, :], WGH[:, :, :].rearrange("p a b -> p (a b)"), ALU.subtract), wgh)]
        two = []
        for t in range(TT):
            two.append(shared_2(t, one[t]))
            if t == 1:
                eb_ok = expert_biases()
            if t == 2:
                xm_ok = select()
        xt_dead = two
        hot_ok, index_ok, weight_ok = scores_of(xm_ok)
        er_ok = dma("gpsimd", q.sem("er_sem"), lambda e: e.indirect_dma_start(out=ER[:, :], **rows_of(A["L1_ffn_eb3"], expert[:, 0:1])), index_ok, xt_dead)
        sb3_ok = bias_rows(SB3[:, :], "L1_ffn_sb3", xt_dead)

        o1 = dve(lambda e: e.tensor_scalar(OHM[:, :], iota16[:, :], sel(6), sel(7), op0=ALU.is_equal, op1=ALU.mult), kept_ok, xt_dead)
        w1 = dve(lambda e: e.tensor_copy(swo[:, 0:1], se[:, 20:21]), weight_ok)
        w2 = dve(lambda e: e.memset(swo[:, 1:2], 1.0))

        def token_scale():
            def emit(e):
                for t in range(TT):
                    ins = e.matmul(bank(5)[0:PT, 2 * t:2 * t + 2], OHM[:, cols(t)].bitcast(F32), swo[:, :], start=True, stop=True)
                return ins
            s = pe(emit, o1, w1, w2, freed[5])
            ps = bank(5)[0:PT, 0:10].rearrange("p (t c) -> p t c", c=2)
            a = dve(lambda e: e.tensor_scalar(scl[:, :], ps[:, :, 1], -1.0, 1.0, op0=ALU.mult, op1=ALU.add), s)
            b = dve(lambda e: e.tensor_tensor(scl[:, :], scl[:, :], ps[:, :, 0], ALU.add), a)
            free(5, 1, a, b)
            return b

        h1_free, zt_free = [x4_free, x4_free], [s2_out]
        est_free = [sh_ok[4], sh_ok[4]]
        every = slice(0, 128)

        def expert_rows(j, x):
            b = 2 * j + x % 2

            def bias(e):
                e.matmul(bank(b), ONE8[:, x, :], EBH[j][:, :], start=True, stop=False)
                return e.matmul(bank(b), ONE8[:, x, :], EBL[:, j, :], start=False, stop=False)
            pe(bias, eb_ok, freed[b])
            for k, part in enumerate(We[j][x]):
                s = rows(bank(b), XMH, XML, every, part, (2 * k, 2 * k + 1), False, k == 3, xm_ok)
                W.release(part, s)
                W.split()
            return s

        def gate(x):
            i = x % 2
            a = act(lambda e: e.activation(H1[i][:, :], bank(i), ACT.Silu), expert_rows(0, x), h1_free[i])
            free(i, 1, a)
            return a

        def hidden(x, g):
            i = x % 2
            u = H1[i][:, :]
            m = dve(lambda e: e.tensor_tensor(u, u, bank(2 + i), ALU.mult), expert_rows(1, x), g)
            free(2 + i, 1, m)
            st = est[:, i, :]
            r = norm_of(u, st, 128, m, est_free[i])
            r = dve(lambda e: e.tensor_tensor(st[:, 15:16], st[:, 15:16], ohe[:, x:x + 1], ALU.mult), r, hot_ok)
            n = dve(lambda e: e.tensor_scalar(u, u, st[:, 12:13], st[:, 15:16], op0=ALU.subtract, op1=ALU.mult), r)
            est_free[i] = n
            n = dve(lambda e: e.tensor_tensor(u, u, ELG[:, :], ALU.mult), n, erow[0])
            return dve(lambda e: e.scalar_tensor_tensor(u, ELB[:, :], ohe[:, x:x + 1], u, op0=ALU.mult, op1=ALU.add), n, erow[1])

        def turn_z(x, z):
            ps = bank(4).rearrange("p (k c) -> p k c", k=4)

            def emit(e):
                for k in range(4):
                    ins = e.transpose(ps[:, k, :], H1[x % 2][:, 128 * k:128 * k + 128], ident[:, :])
                return ins
            a = pe(emit, z, freed[4])
            h = act(lambda e: e.activation(ZTH[:, :, :], ps, ACT.Copy), a, zt_free)
            l = dve(lambda e: e.tensor_tensor(ZTL[:, :, :], ps, ZTH[:, :, :], ALU.subtract), h)
            free(4, 1, h, l)
            h1_free[x % 2] = a
            return [h, l]

        def third(x, zt):
            done = []
            for h in range(2):
                for k, part in enumerate(We[2][x][h]):
                    s = rows(bank(6 + h), ZTH, ZTL, every, part, (2 * k, 2 * k + 1), x == 0 and k == 0, x == 7 and k == 1, freed[6 + h] if x == 0 else None, zt)
                    W.release(part, s)
                    W.split()
                done.append(s)
            zt_free[:] = [s]
            return done

        sht_ok = {}

        def turn_shared(t):
            ps = bank(5).rearrange("p (k c) -> p k c", k=4)[:, :, 0:PT]

            def emit(e):
                for k in range(4):
                    ins = e.transpose(ps[:, k, :], S1[t][:, 128 * k:128 * k + 128], ident[0:PT, 0:PT])
                return ins
            a = pe(emit, sh_ok[t], freed[5])
            h = act(lambda e: e.activation(SHTH[:, :, cols(t)], ps, ACT.Copy), a, x3_all)
            l = dve(lambda e: e.tensor_tensor(SHTL[:, :, cols(t)], ps, SHTH[:, :, cols(t)], ALU.subtract), h)
            free(5, 1, h, l)
            s1_free.append(a)
            sht_ok[t] = [h, l]

        s1_free, so_half = [], {}
        x3l_sem = [q.sem(f"x3l_sem{i}") for i in range(2)]
        x3l_free, so_done = [s1_free, s1_free], {}

        def shared_3(h, t):
            sl = slice(512 * h, 512 * h + 512)
            b = 4 + t % 2
            for k, part in enumerate(Ws3[h]):
                s = rows(bank(b)[0:PT, :], SHTH, SHTL, cols(t), part, (2 * k, 2 * k + 1), k == 0, k == 1, freed[b], sht_ok[t])
                if t == TT - 1:
                    W.release(part, s)
            W.split()
            i = t % 2
            l = dma("sync", x3l_sem[i], lambda e: e.dma_start(X3L[i][:, 512 * h:512 * h + 512], x3d[t * PT:(t + 1) * PT, sl]), x3l_free[i], x3_stored)
            a = dve(lambda e: e.tensor_tensor(SO[:, t, sl], bank(b)[0:PT, :], SB3[:, sl], ALU.add), s, sb3_ok, xt_dead)
            free(b, 1, a)
            c = dve(lambda e: e.scalar_tensor_tensor(SO[:, t, sl], SO[:, t, sl], scl[:, t:t + 1], X3L[i][:, 512 * h:512 * h + 512], op0=ALU.mult, op1=ALU.add), a, l, scl_ok)
            x3l_free[i] = c
            so_done[t, h] = c

        zt, z = {}, {}
        for x in range(8):
            g = gate(x)
            if x == 0:
                scl_ok = token_scale()
            else:
                zt[x - 1] = turn_z(x - 1, z[x - 1])
            if x < 2:
                turn_shared(2 * x)
            z[x] = hidden(x, g)
            if x < 2:
                turn_shared(2 * x + 1)
            if x:
                third(x - 1, zt[x - 1])
            if x == 2:
                turn_shared(4)
            if x in (3, 7):
                for t in range(TT):
                    shared_3(x // 4, t)
        zt[7] = turn_z(7, z[7])
        last = third(7, zt[7])

        em_ok = []
        for h in range(2):
            def weigh(h=h, sl=slice(512 * h, 512 * h + 512)):
                r = dve(lambda e: e.tensor_tensor(ER[:, sl], bank(6 + h), ER[:, sl], ALU.add), last[h], er_ok)
                m = act(lambda e: e.activation(EMH[:, sl], ER[:, sl], ACT.Copy, scale=se[:, 21:22]), r, weight_ok, xt_dead)
                em_ok.append(dve(lambda e: e.scalar_tensor_tensor(EML[:, sl], ER[:, sl], se[:, 21:22], EMH[:, sl], op0=ALU.mult, op1=ALU.subtract), m))
            weigh()
        for t in range(TT):
            for h in range(2):
                def last_rows(t=t, h=h, b=(2 * t + h) % 6, sl=slice(512 * h, 512 * h + 512)):
                    def emit(e):
                        for n, m in enumerate((EMH, EML)):
                            ins = e.matmul(bank(b)[0:PT, :], OHM[:, cols(t)], m[:, sl], start=n == 0, stop=n == 1)
                        return ins
                    s = pe(emit, em_ok[h], o1, freed[b])
                    d = dve(lambda e: e.tensor_tensor(SO[:, t, sl], SO[:, t, sl], bank(b)[0:PT, :], ALU.add), s, so_done[t, h])
                    free(b, 1, d)
                    return d
                d = last_rows()
            dma("sync", x3s[t], lambda e, t=t: e.dma_start(out[t * PT:(t + 1) * PT, :], SO[:, t, :]), d)
        q.emit_all()


def half(np, w):
    k, n = w.shape
    return np.ascontiguousarray(w.reshape(k // 128, 128, n // 512, 512).transpose(2, 1, 0, 3)).reshape(n // 512, 128, k // 128 * 512)


def lay_out(np, I):
    P = {n: I[n] for n in ("x", "L0_gnn_bias", "L0_gnn_b_gate", "L1_gnn_b")}
    e = np.zeros((3, 164 * 128), np.int32)
    e[1], e[2] = 1023, 7
    for i, n in enumerate(("src", "dst", "edge_type_8")):
        e[i, :20000] = I[n]
    P["edges"] = np.ascontiguousarray(e.reshape(3, 164, 128).transpose(1, 0, 2))
    for p in ("L0_mix_", "L1_mix_"):
        for n in "qkvo":
            w = I[f"{p}W{n}"]
            P[f"{p}W{n}"] = half(np, w if p[1] == "0" else w.T)
            P[f"{p}b{n}"] = I[f"{p}b{n}"]
        P[f"{p}bq"] = np.ascontiguousarray(I[f"{p}bq"].reshape(8, 128).T)
    P["L0_gnn_root"] = half(np, I["L0_gnn_root"])
    P["L0_gnn_weight"] = np.stack([half(np, w) for w in I["L0_gnn_weight"]])
    P["L0_gnn_w_gate"] = np.stack([half(np, I["L0_gnn_w_gate"][:1024]), half(np, I["L0_gnn_w_gate"][1024:])])
    P["L1_gnn_W"] = half(np, I["L1_gnn_W"].T)
    for fs in ("kq", "v", "f"):
        nodes = np.zeros((len(fs), 256, 1024), np.float32)
        for i, f in enumerate(fs):
            nodes[i, :255] = I[f"L0_ffn_{f}_nw"]
        P[f"L0_ffn_{fs}_nw"] = np.ascontiguousarray(nodes.reshape(len(fs) * 256, 8, 128).transpose(2, 1, 0)).reshape(128, -1)
    nb = np.zeros((4, 256), np.float32)
    leaf = np.arange(32)
    for i, f in enumerate("kqvf"):
        p = f"L0_ffn_{f}_"
        nb[i, :255] = I[p + "nb"]
        P[p + "w1"] = np.ascontiguousarray(I[p + "w1"].reshape(8, 32, 8, 128, 16).transpose(0, 3, 2, 1, 4)).reshape(8, 128, 4096)
        P[p + "w2"] = np.ascontiguousarray(I[p + "w2"].reshape(8, 4, 128, 1024).transpose(0, 2, 1, 3)).reshape(8, 128, 4096)
        P[p + "b1"], P[p + "b2"] = I[p + "b1"].reshape(8, 512), I[p + "b2"]
        blocks = np.zeros((2, 4, 32, 32, 16), np.float32)
        blocks[:, :, leaf, leaf, :] = I[p + "b1"].reshape(2, 4, 32, 16)
        P[p + "bd"] = blocks.reshape(2, 128, 512)
    P["L0_ffn_nb"] = nb.reshape(1024)
    f = "L1_ffn_"
    P[f + "index"] = np.ascontiguousarray(np.stack([I[f + "index_b"], I[f + "index_t"]], 1))
    for n in ("sw1", "sw2"):
        P[f + n] = half(np, I[f + n].T)[0]
    P[f + "sw3"] = half(np, I[f + "sw3"].T)
    for n in ("ew1", "ew2"):
        P[f + n] = np.stack([half(np, w.T)[0] for w in I[f + n]])
    P[f + "ew3"] = np.stack([half(np, w.T) for w in I[f + "ew3"]])
    for n in ("sb1", "sb2", "sb3", "s_ln_g", "s_ln_b", "eb1", "eb2", "eb3", "sel_ln_g", "sel_ln_b"):
        P[f + n] = I[f + n]
    gates = np.zeros((10, 1024), np.float32)
    gates[0:1], gates[1:9] = I[f + "sg_w"], I[f + "eg_w"]
    P[f + "gates"] = np.ascontiguousarray(gates.reshape(10, 8, 128).transpose(2, 1, 0)).reshape(128, 80)
    b = np.zeros(20, np.float32)
    b[0:1], b[1:9], b[10:18] = I[f + "sg_b"], I[f + "eg_b"], I[f + "exp_bias"]
    P[f + "gate_b"] = b
    return P


def kernel(**inputs):
    import numpy as np
    import concourse.bacc as bacc
    from concourse.bass_utils import run_bass_kernel_spmd

    laid = lay_out(np, {n: np.asarray(a) for n, a in inputs.items()})
    nc = bacc.Bacc("TRN2", target_bir_lowering=False, num_devices=1)
    arrays, A = {}, {}
    for name, a in laid.items():
        a = np.ascontiguousarray(a)
        arrays[f"in_{name}"] = a
        A[name] = nc.dram_tensor(f"in_{name}", a.shape, mybir.dt.from_np(a.dtype), kind="ExternalInput").ap()
    out = nc.dram_tensor("out_0", (N, D), F32, kind="ExternalOutput").ap()
    gps_layers(nc, A, out)
    r = run_bass_kernel_spmd(nc, [arrays], core_ids=[0])
    return r.results[0]["out_0"]
```

```python
from contextlib import ExitStack

import concourse.bass as bass
from concourse import mybir

F32 = mybir.dt.float32
F32R = mybir.dt.float32r
F16 = mybir.dt.float16
I32 = mybir.dt.int32
U32 = mybir.dt.uint32
U16 = mybir.dt.uint16
ALU = mybir.AluOpType
ACT = mybir.ActivationFunctionType
AX = mybir.AxisListType


class Step:

    def __init__(self, engine, emit, after, sem=None, value=0):
        self.engine, self.emit, self.after = engine, emit, after
        self.sem, self.value, self.wanted = sem, value, sem is not None
        self.own = False


def flat(after):
    out = []
    for a in after:
        if isinstance(a, Step):
            out.append(a)
        elif a is not None:
            out += flat(a)
    return out


class Queues:

    ENGINES = ("tensor", "scalar", "vector", "gpsimd", "sync")

    def __init__(self, nc, ctx):
        self.nc, self.ctx = nc, ctx
        self.steps = {e: [] for e in self.ENGINES}
        self.counter = {e: ctx.enter_context(nc.semaphore(f"done_{e}")) for e in self.ENGINES}
        self.last = {}
        self.pooled = None

    def add(self, engine, emit, after):
        step = Step(engine, emit, flat(after))
        for a in step.after:
            a.wanted = True
        self.steps[engine].append(step)
        return step

    def pe(self, emit, *after):
        return self.add("tensor", emit, after)

    def act(self, emit, *after):
        return self.add("scalar", emit, after)

    def dve(self, emit, *after):
        return self.add("vector", emit, after)

    def pool(self, emit, *after):
        self.pooled = self.add("gpsimd", emit, (after, self.pooled))
        return self.pooled

    def sp(self, emit, *after):
        return self.add("sync", emit, after)

    def sem(self, name):
        return self.ctx.enter_context(self.nc.semaphore(name))

    def dma(self, engine, sem, emit, *after):
        before = self.last.get(sem.name)
        step = Step(engine, emit, flat(after) + ([before] if before else []), sem, 16 + (before.value if before else 0))
        for a in step.after:
            a.wanted = True
        self.last[sem.name] = step
        self.steps[engine].append(step)
        return step

    def emit_all(self):
        self.sp(lambda e: e.nop(), list(self.last.values()))
        for e in self.ENGINES:
            n = 0
            for s in self.steps[e]:
                if s.sem is None and s.wanted:
                    n += 1
                    s.sem, s.value = self.counter[e], n
        with self.nc.Block() as block:
            for e in self.ENGINES:
                self.emit_engine(block, e)

    def emit_engine(self, block, e):
        def run(engine):
            seen = {}
            for s in self.steps[e]:
                for a in s.after:
                    if seen.get(a.sem.name, 0) < a.value:
                        engine.wait_ge(a.sem, a.value)
                        seen[a.sem.name] = a.value
                last = s.emit(engine)
                if s.wanted and not s.own:
                    last.then_inc(s.sem, 16 if s.sem.name != self.counter[e].name else 1)

        {"tensor": block.tensor, "scalar": block.scalar, "vector": block.vector,
         "gpsimd": block.gpsimd, "sync": block.sync}[e](run)

N, D, TT, PT = 625, 1024, 5, 125
NP, NH = 628, 314
EPS = 1e-5


def gps_layers(nc, A, out):
    ctx = ExitStack()
    with ctx:
        q = Queues(nc, ctx)
        pe, act, dve, pool, sp, dma = q.pe, q.act, q.dve, q.pool, q.sp, q.dma

        C0 = 16512
        RL0 = C0 + 12288
        NRING, NHIGH = 14, 6
        HI0 = RL0 + NRING * 4096
        R0 = HI0 + NHIGH * 4096
        LENT = HI0 - 3 * 4096
        TOP = 229344

        def size_of(shape, dt):
            n = 1
            for s in shape[1:]:
                n *= s
            return n * (2 if dt == F16 else 4)

        def at(name, shape, dt, offset):
            assert offset + size_of(shape, dt) <= TOP, (name, offset + size_of(shape, dt) - TOP)
            return nc.alloc_sbuf_tensor_at(name, shape, dt, offset=offset)

        here = [C0]

        def const(name, shape, dt):
            o = here[0]
            here[0] += (size_of(shape, dt) + 31) // 32 * 32
            assert here[0] <= RL0, name
            return nc.alloc_sbuf_tensor_at(name, shape, dt, offset=o)

        PS = ctx.enter_context(nc.psum_tensor("PS", [128, 4096], F32))

        def bank(i, n=1):
            return PS[:, i * 512:(i + n) * 512]

        freed = [[] for _ in range(8)]

        def free(b, n, *steps):
            for i in range(b, b + n):
                freed[i] = list(steps)

        def scratch(name, shape, dt=F32):
            return nc.dram_tensor(name, shape, dt, kind="Internal").ap()

        ident = const("ident", [128, 128], F32)
        iota16 = const("iota16", [128, 640], F16)
        ones16 = const("ones16", [128, 128], F16)
        zeros16 = const("zeros16", [128, 512], F16)
        bdmask = const("bdmask", [128, 130], F32)
        rstd = const("rstd", [PT, TT], F32)
        lnst = const("lnst", [PT, TT, 2, 6], F32)
        lnmv = const("lnmv", [PT, TT, 2], F32)
        lnt = const("lnt", [PT, 8, TT], F32)
        ii = at("iota_int", [128, 640], I32, R0 + 81024)

        io = pool(lambda e: e.iota(ii[:, 0:128], [[1, 128]], base=0, channel_multiplier=-1))
        ident_ok = dve(lambda e: e.tensor_scalar(ident[:, :], ii[:, 0:128], 0.0, None, op0=ALU.is_equal), io)
        io2 = pool(lambda e: e.iota(ii[:, :], [[1, 640]], base=0, channel_multiplier=0), ident_ok)
        iota_ok = dve(lambda e: e.tensor_copy(iota16[:, :], ii[:, :]), io2)
        ones_ok = pool(lambda e: e.memset(ones16[:, :], 1.0))
        zeros_ok = pool(lambda e: e.memset(zeros16[:, :], 0.0))

        def fill(ap, value, *after):
            if ap.dtype == F32R:
                ap = ap.bitcast(F32)
            return pool(lambda e: e.memset(ap, value), *after)

        m0 = fill(bdmask[:, :], 0.0)
        bd_ok = [fill(bdmask[0:64, 0:64], 1.0, m0), fill(bdmask[64:128, 64:128], 1.0, m0),
                 fill(bdmask[0:64, 128:129], 1.0, m0), fill(bdmask[64:128, 129:130], 1.0, m0)]

        K0 = R0 + 67584
        PLACES = [RL0 + 4096 * i for i in range(NRING)]
        LAST = range(11, 14)
        LEAF_K = range(14, 21)
        LEAF_Q = range(21, 23)
        AFTER_K, ROUTED = range(23, 25), range(25, 29)
        PLACES += [K0 + 11520 + 4096 * i for i in range(7)] + [K0 + 40192, K0 + 44288]
        PLACES += [K0 + 16384, K0 + 20480] + [K0 + 4096 * i for i in range(4)]
        RAW = [at(f"raw{i}", [128, 1024], F32, o) for i, o in enumerate(PLACES)]
        LOW = [at(f"low{i}", [128, 1024], F32R, o) for i, o in enumerate(PLACES)]
        HIGH = [at(f"high{i}", [128, 1024], F32R, HI0 + 4096 * i) for i in range(NHIGH)]
        RAWS = [q.sem(f"raw_sem{i}") for i in range(23)]
        RAWS += RAWS[14:20]

        class Stream:

            def __init__(self, places):
                self.src, self.loaded, self.high, self.low, self.used = [], [], [], [], []
                self.order = list(places)
                self.place = []
                self.tenant = {}
                self.ahead = NHIGH
                self.raw_guard = {}
                self.subtract = dve
                self.paused = False
                self.pooled = ()

            def declare(self, ap, parts=4):
                w = ap.shape[-1] // parts
                self.src += [ap[:, j * w:(j + 1) * w] for j in range(parts)]
                self.load()
                return list(range(len(self.src) - parts, len(self.src)))

            def grow(self, places, *after):
                self.order = list(places) + self.order
                for p in places:
                    self.raw_guard[p] = after
                self.load()

            def drop(self, places):
                for p in places:
                    self.order.remove(p)

            def lent(self, places):
                return [self.used[self.tenant[p]] for p in places if p in self.tenant]

            def load(self):
                while not self.paused and len(self.loaded) < len(self.src) and self.tenant.get(self.order[0], -1) < len(self.used):
                    self.load_one()

            def resume(self):
                self.paused = False
                self.load()

            def load_one(self):
                i, p = len(self.loaded), self.order.pop(0)
                raw, src = RAW[p], self.src[i]
                before = self.used[self.tenant[p]] if p in self.tenant else None
                self.loaded.append(dma("sync", RAWS[p], lambda e: e.dma_start(raw[:, 0:src.shape[-1]], src),
                                       before, self.raw_guard.pop(p, None)))
                self.tenant[p] = i
                self.place.append(p)
                self.order.append(p)

            def split_one(self):
                i = len(self.high)
                w = self.src[i].shape[-1]
                raw, low, high = RAW[self.place[i]], LOW[self.place[i]], HIGH[i % NHIGH]
                h = act(lambda e: e.activation(high[:, 0:w], raw[:, 0:w], ACT.Copy),
                        self.loaded[i], self.used[i - NHIGH] if i >= NHIGH else None)
                self.high.append(h)
                on = pool if i % 4 in self.pooled else self.subtract
                self.low.append(on(lambda e: e.tensor_tensor(low[:, 0:w], raw[:, 0:w], high[:, 0:w], ALU.subtract), h))

            def split(self, n=1):
                for _ in range(n):
                    if len(self.high) < len(self.place) and len(self.high) - len(self.used) < self.ahead:
                        self.split_one()

            def ready(self, i):
                while len(self.high) <= i:
                    self.split_one()
                return [self.high[i], self.low[i]]

            def pair(self, i):
                return HIGH[i % NHIGH], LOW[self.place[i]]

            def release(self, i, step):
                assert len(self.used) == i
                self.used.append(step)
                self.load()

        W = Stream([*range(7), 12, 13])

        def rsqrt(v, r, w, h, *after):
            b = dve(lambda e: e.tensor_scalar(w.bitcast(I32), v.bitcast(I32), 1, None, op0=ALU.arith_shift_right), *after)
            m = dve(lambda e: e.tensor_scalar(h, v, -0.5, None, op0=ALU.mult), *after)
            b = dve(lambda e, b=b: e.tensor_scalar(r.bitcast(I32), w.bitcast(I32), -1.0, float(0x5F3759DF), op0=ALU.mult, op1=ALU.add), b)
            for _ in range(3):
                if v.shape[-1] == 1:
                    b = dve(lambda e: e.scalar_tensor_tensor(w, r, r, h, op0=ALU.mult, op1=ALU.mult), b, m)
                else:
                    b = dve(lambda e: e.tensor_tensor(w, r, r, ALU.mult), b)
                    b = dve(lambda e: e.tensor_tensor(w, w, h, ALU.mult), b, m)
                b = dve(lambda e: e.scalar_tensor_tensor(r, w, 1.5, r, op0=ALU.add, op1=ALU.mult), b)
            return b

        def moments(a, b, x, after):
            last = []
            for t in range(a, b):
                for h in range(2):
                    last.append(dve(lambda e, t=t, h=h: e.bn_stats(lnst[:, t, h, :], x[:, t, 512 * h:512 * h + 512]), after[t]))
            for t in range(a, b):
                last.append(dve(lambda e, t=t: e.bn_aggr(lnmv[:, t, :], lnst[:, t, :, :].rearrange("p a b -> p (a b)")), last[2 * (t - a):2 * (t - a) + 2]))
            return last

        def deviations(a, b, *after):
            d = dve(lambda e: e.tensor_scalar(lnt[:, 0, a:b], lnmv[:, a:b, 1], EPS, None, op0=ALU.add), *after)
            return rsqrt(lnt[:, 0, a:b], rstd[:, a:b], lnt[:, 1, a:b], lnt[:, 5, a:b], d)

        def ln_stats(a, b, x, after):
            return deviations(a, b, moments(a, b, x, after))

        def normalize(t, dst, x, scale, *after):
            return dve(lambda e: e.tensor_scalar(dst, x, lnmv[:, t, 0:1], scale[:, t:t + 1],
                                                 op0=ALU.subtract, op1=ALU.mult), *after)

        def cols(t):
            return slice(t * PT, (t + 1) * PT)

        def transpose_tile(t, x, hi, lo, b, *after):
            ps = bank(b, 2).rearrange("p (k c) -> p k c", k=8)[:, :, 0:PT]

            def emit(e):
                for k in range(8):
                    ins = e.transpose(ps[:, k, :], x[:, k * 128:(k + 1) * 128], ident[0:PT, 0:PT])
                return ins
            a = pe(emit, ident_ok, freed[b], freed[b + 1], *after)
            h = act(lambda e: e.activation(hi[:, :, cols(t)], ps, ACT.Copy), a)
            l = dve(lambda e: e.tensor_tensor(lo[:, :, cols(t)], ps, hi[:, :, cols(t)], ALU.subtract), h)
            free(b, 2, h, l)
            return [h, l]

        def rows(dst, xh, xl, xs, part, kts, first, last, *after):
            wh, wl = W.pair(part)

            def emit(e):
                for j, kt in enumerate(kts):
                    c = slice(512 * j, 512 * j + 512)
                    e.matmul(dst, xh[:, kt, xs], wh[:, c], start=first and j == 0, stop=False)
                    e.matmul(dst, xh[:, kt, xs], wl[:, c], start=False, stop=False)
                    ins = e.matmul(dst, xl[:, kt, xs], wh[:, c], start=False, stop=last and j == len(kts) - 1)
                return ins
            return pe(emit, W.ready(part), *after)

        def rows_tile(t, parts, xh, xl, b, ready, first=True, last=True, done=None):
            for j, part in enumerate(parts):
                s = rows(bank(b)[0:PT, :], xh, xl, cols(t), part, (2 * j, 2 * j + 1),
                         first and j == 0, last and j == 3, freed[b] if first else None, ready)
                if done is None and t == TT - 1:
                    W.release(part, s)
            return s

        XTH = at("xt_high", [128, 8, NP], F32R, R0)
        XTL = at("xt_low", [128, 8, NP], F32R, R0 + 20096)
        P1 = R0 + 40192
        SPARE = RL0 + 7 * 4096
        XN = at("x_rows", [PT, TT, D], F32, P1)

        xsem = [q.sem(f"x_sem{t}") for t in range(TT)]

        def load_x(t):
            return dma("sync", xsem[t], lambda e: e.dma_start(XN[:, t, :], A["x"][t * PT:(t + 1) * PT, :]))

        xload = [load_x(0)]

        EI0 = at("edges0", [128, 3, 128], I32, P1 + 59904)
        EI1 = at("edges1", [36, 3, 128], I32, P1 + 61440)
        esem = [q.sem("e_sem0"), q.sem("e_sem1")]
        eload = [dma("scalar", esem[0], lambda e: e.dma_start(EI0[:, :, :], A["edges"][0:128])),
                 dma("scalar", esem[1], lambda e: e.dma_start(EI1[:, :, :], A["edges"][128:164]))]

        NB, LOOK = 40, 4
        tidi = at("e_tidi", [128, 2], I32, P1 + 66432)
        bsti = at("e_bsti", [128, NB], I32, P1 + 66624)
        tgt = const("target_id", [64, 10], F32)
        tgti = const("target_int", [64, 10], I32)
        ti = pool(lambda e: e.iota(tidi[:, :], [[128, 2]], base=0, channel_multiplier=1))
        bi = pool(lambda e: e.iota(bsti[:, :], [[128, NB]], base=0, channel_multiplier=0))
        gi = pool(lambda e: e.iota(tgti[:, :], [[64, 10]], base=0, channel_multiplier=1))

        W.paused = True
        Wk = [W.declare(A["L0_mix_Wk"][h]) for h in range(2)]
        for t in range(1, TT):
            W.load_one()
            xload.append(load_x(t))
        W.resume()
        Wv = [W.declare(A["L0_mix_Wv"][h]) for h in range(2)]
        Wroot = [W.declare(A["L0_gnn_root"][h]) for h in range(2)]
        Wq = [W.declare(A["L0_mix_Wq"][h]) for h in range(2)]
        Wo = [W.declare(A["L0_mix_Wo"][h]) for h in range(2)]
        Wrel = [[W.declare(A["L0_gnn_weight"][r, h]) for h in range(2)] for r in range(8)]
        Wgate = []
        for h in range(2):
            Wgate.append([W.declare(A["L0_gnn_w_gate"][1, h]), W.declare(A["L0_gnn_w_gate"][0, h])])
        FF = ("k", "q", "v", "f")
        Wnode = {"k": W.declare(A["L0_ffn_k_nw"], 2), "qv": W.declare(A["L0_ffn_qv_nw"])}
        Wf1, Wf2 = {}, {}

        def declare_units(units):
            for n in range(len(units) + 1):
                if n < len(units):
                    Wf1[units[n]] = W.declare(A[f"L0_ffn_{units[n][0]}_w1"][units[n][1]])
                if n:
                    Wf2[units[n - 1]] = W.declare(A[f"L0_ffn_{units[n - 1][0]}_w2"][units[n - 1][1]])

        units = [(f, g) for f in "kqv" for g in range(8)]
        declare_units(units)
        Wnode["f"] = W.declare(A["L0_ffn_f_nw"], 2)
        declare_units([("f", g) for g in range(8)])
        Wgnn, Wk1 = [], []
        for h in range(2):
            Wgnn.append(W.declare(A["L1_gnn_W"][h]))
            Wk1.append(W.declare(A["L1_mix_Wk"][h]))
        Wv1 = [W.declare(A["L1_mix_Wv"][h]) for h in range(2)]
        Wq_of, Wo_of = [{"L0_mix": w0, "L1_mix": [W.declare(A[f"L1_mix_W{n}"][h]) for h in range(2)]} for n, w0 in (("q", Wq), ("o", Wo))]
        Ws1, Ws2 = W.declare(A["L1_ffn_sw1"]), W.declare(A["L1_ffn_sw2"])
        Ws3, We = [], [[], [], []]
        for x in range(9):
            if x < 8:
                We[0].append(W.declare(A["L1_ffn_ew1"][x]))
                We[1].append(W.declare(A["L1_ffn_ew2"][x]))
            if x:
                We[2].append([W.declare(A["L1_ffn_ew3"][x - 1, h], 2) for h in range(2)])
            if x in (3, 7):
                Ws3.append(W.declare(A["L1_ffn_sw3"][x // 4], 2))

        adj = scratch("adjacency", [PT, TT, 8, 640])
        cntd = scratch("counts", [5120])
        STG = [at(f"a_stage{i}", [PT, TT, 8, 64], F32, P1 + 41280 + 10240 * i) for i in range(2)]
        TA = [at(f"at_stage{i}", [64, TT, PT], F32, P1 + 61760 + 2528 * i) for i in range(2)]
        ALLC = [at(f"a_sum{i}", [PT, TT, 64], F32, P1 + 66816 + 1280 * i) for i in range(3)]
        TMP = [at(f"tmp{i}", [PT, 512], F32, P1 + 70688 + 2048 * i) for i in range(2)]
        OHS = at("one_src", [128, 9, 640], F16, SPARE)
        OHK = at("one_key", [128, 9, 128], F16, SPARE + 11520)
        EC = at("e_bucket", [128, 2, LOOK, 2], F32, SPARE + 15136)
        BKV = [at(f"bias_kv{i}", [PT, 512], F32, SPARE + 15200 + 2048 * i) for i in range(2)]
        CST = [at(f"c_stage{i}", [1, 256], F32, P1 + 75424 + 1024 * i) for i in range(2)]
        KN = at("k_rows", [PT, TT, D], F32, P1)
        VN = at("v_rows", [PT, TT, 8, 130], F32, P1 + 20480)

        bias_sem = [q.sem(f"bias_sem{i}") for i in range(3)]
        bias_n = [0]

        def bias_rows(tile, name, *after):
            bias_n[0] += 1
            src = A[name] if isinstance(name, str) else name
            return dma("gpsimd", bias_sem[bias_n[0] % 3], lambda e: e.dma_start(tile, src.partition_broadcast(tile.shape[0])), *after)

        tmp_free = [None, None]

        def keys_tile(dst, b, i, bias, *after):
            w = TMP[i][:, :]
            a = dve(lambda e: e.tensor_tensor(dst, bank(b)[0:PT, :], bias, ALU.add), *after)
            free(b, 1, a)
            m = act(lambda e: e.activation(w, dst, ACT.Relu, scale=-1.0), a, tmp_free[i])
            x = act(lambda e: e.activation(w, w, ACT.Exp, scale=-1.0), m)
            r = act(lambda e: e.activation(dst, dst, ACT.Relu), m)
            s = pool(lambda e: e.tensor_tensor(dst, dst, w, ALU.add), x, r)
            tmp_free[i] = s
            return s

        def values_tile(h, t, b, bias, *after):
            v = dve(lambda e: e.tensor_tensor(VN[:, t, 4 * h:4 * h + 4, 0:128], bank(b)[0:PT, :].rearrange("p (a c) -> p a c", a=4),
                                              bias.rearrange("p (a c) -> p a c", a=4), ALU.add), *after)
            free(b, 1, v)
            return v

        bias_kv = {("k", h): bias_rows(BKV[h][:, :], A["L0_mix_bk"][512 * h:512 * h + 512]) for h in range(2)}
        ones_v = dve(lambda e: e.memset(VN[:, :, :, 128:130], 1.0), iota_ok)
        k_done, v_done, late = [], [], []

        rootd = scratch("x_root", [N, D])
        rsem = [q.sem(f"root_sem{i}") for i in range(2)]
        root_stored = []

        def root_tile(h, t, b, i, s):
            a = act(lambda e: e.activation(TMP[i][:, :], bank(b)[0:PT, :], ACT.Copy), s, tmp_free[i])
            free(b, 1, a)
            tmp_free[i] = dma("scalar", rsem[i], lambda e: e.dma_start(rootd[t * PT:(t + 1) * PT, 512 * h:512 * h + 512], TMP[i][:, :]), a)
            root_stored.append(tmp_free[i])

        def fill_halves():
            n = 0
            for of, w in (("k", Wk), ("v", Wv), ("root", Wroot)):
                for h in range(2):
                    if of == "v":
                        bias_kv["v", h] = bias_rows(BKV[h][:, :], A["L0_mix_bv"][512 * h:512 * h + 512], k_done)
                    for t in range(TT):
                        b = 4 + n % 2
                        for j, part in enumerate(w[h]):
                            s = rows(bank(b)[0:PT, :], XTH, XTL, cols(t), part, (2 * j, 2 * j + 1), j == 0, j == 3, freed[b] if j == 0 else None, xt_ok[t])
                            if t == TT - 1:
                                W.release(part, s)
                            if j == 1:
                                W.split()
                                yield
                        sl = slice(512 * h, 512 * h + 512)
                        if of == "k":
                            late.append(lambda h=h, t=t, b=b, n=n, sl=sl, s=s: k_done.append(keys_tile(KN[:, t, sl], b, n % 2, BKV[h][:, :], s, bias_kv["k", h])))
                        elif of == "root":
                            late.append(lambda h=h, t=t, b=b, n=n, s=s: root_tile(h, t, b, n % 2, s))
                        else:
                            late.append(lambda h=h, t=t, b=b, s=s: v_done.append(values_tile(h, t, b, BKV[h][:, :], s, bias_kv["v", h], ones_v)))
                        n += 1
                        W.split()
                        yield

        W.subtract = pool
        pads = [fill(XTH[:, :, N:NP], 0.0), fill(XTL[:, :, N:NP], 0.0)]
        xt_ok = []
        filler = fill_halves()

        def fill_gap(n=1):
            for _ in range(n):
                next(filler, None)

        def finish_late():
            while late:
                late.pop(0)()

        def normal(a, b, *after):
            r = deviations(a, b, *after)
            return {t: normalize(t, XN[:, t, :], XN[:, t, :], rstd, r) for t in range(a, b)}

        def turn(t, n):
            xt_ok.append(transpose_tile(t, XN[:, t, :], XTH, XTL, (6, 0, 2)[t % 3], n[t]))

        W.split(2)
        n = normal(0, 1, moments(0, 1, XN, xload))
        mom = moments(1, 3, XN, xload)
        turn(0, n)
        n = normal(1, 3, mom)
        mom = moments(3, 5, XN, xload)
        fill_gap(2)
        for t in range(1, 3):
            turn(t, n)
        n = normal(3, 5, mom)
        finish_late()
        fill_gap(2)
        for t in range(3, 5):
            turn(t, n)
        finish_late()
        fill_gap(2)
        ESF = at("e_src", [128, 2, 128], F32, P1 + 62976)
        EKF = at("e_key", [128, 2, 128], F32, P1 + 64000)
        E2 = at("e_cols", [128, 164, 2], F32, SPARE + 13824)
        kmin = at("e_kmin", [128, 2], F32, P1 + 66336)
        kmax = at("e_kmax", [128, 2], F32, P1 + 66368)
        tid = at("e_tid", [128, 2], F32, P1 + 66400)
        bst = at("e_bst", [128, NB], F32, P1 + 66464)
        em = at("e_m", [128, 2, 2, NB], F32, P1 + 66784)
        lohi = at("e_lohi", [NB, 2], F32, P1 + 67424)
        lohr = at("e_lohr", [1, 4, NB], F32, P1 + 67456)
        bnd = at("e_bnd", [1, 4 * NB], I32, P1 + 74784)
        many = const("many", [1, 2], F32)
        manyi = const("many_int", [1, 1], I32)

        EI = [EI0, EI1]
        NE = [128, 36]
        mt = const("sel_tmp", [128, 24], F32)

        def sel(i, n=1):
            return mt[:, i:i + n]

        m_own = dve(lambda e: e.tensor_scalar(sel(10), tidi[:, 0:1], 700.0, None, op0=ALU.add), ti)
        tgt_ok = dve(lambda e: e.tensor_copy(tgt[:, :], tgti[:, :]), gi)
        tf = dve(lambda e: e.tensor_copy(tid[:, :], tidi[:, :]), ti)
        bf = dve(lambda e: e.tensor_copy(bst[:, :], bsti[:, :]), bi)
        lo_hi = []
        edge_cols = []
        for h in range(2):
            def halves(h=h, n=NE[h], E=EI[h]):
                s = dve(lambda e: e.tensor_copy(ESF[0:n, h, :], E[:, 0, :]), eload[h])
                k = dve(lambda e: e.scalar_tensor_tensor(EKF[0:n, h, :], E[:, 1, :], 8.0, E[:, 2, :], op0=ALU.mult, op1=ALU.add), eload[h])
                a = dve(lambda e: e.tensor_reduce(kmin[0:n, h:h + 1], EKF[0:n, h, :], axis=AX.X, op=ALU.min), k)
                b = dve(lambda e: e.tensor_reduce(kmax[0:n, h:h + 1], EKF[0:n, h, :], axis=AX.X, op=ALU.max), k)
                c = dve(lambda e: e.tensor_scalar(em[0:n, h, 0, :], bst[0:n, :], kmax[0:n, h:h + 1], None, op0=ALU.is_le), b, bf)
                d = dve(lambda e: e.tensor_scalar(em[0:n, h, 1, :], bst[0:n, :], 127.0, kmin[0:n, h:h + 1], op0=ALU.add, op1=ALU.is_ge), a, bf)
                f = dve(lambda e: e.tensor_tensor(em[0:n, h, 1, :], em[0:n, h, 0, :], em[0:n, h, 1, :], ALU.mult), c, d)
                g = dve(lambda e: e.tensor_scalar(kmin[0:n, h:h + 1], tid[0:n, h:h + 1], -512.0, None, op0=ALU.add), tf, d)
                i = dve(lambda e: e.tensor_scalar(em[0:n, h, 0, :], em[0:n, h, 1, :], kmin[0:n, h:h + 1], 512.0, op0=ALU.mult, op1=ALU.add), f, g)
                j = dve(lambda e: e.tensor_scalar(kmax[0:n, h:h + 1], tid[0:n, h:h + 1], 1.0, None, op0=ALU.add), tf, c)
                l = dve(lambda e: e.tensor_scalar(em[0:n, h, 1, :], em[0:n, h, 1, :], kmax[0:n, h:h + 1], None, op0=ALU.mult), j, i)
                lo_hi.append(pe(lambda e: e.transpose(bank(0)[0:NB, h * 128:h * 128 + n], em[0:n, h, 0, :], ident[0:n, 0:n]), i, ident_ok, [freed[j] for j in range(4)]))
                lo_hi.append(pe(lambda e: e.transpose(bank(1)[0:NB, h * 128:h * 128 + n], em[0:n, h, 1, :], ident[0:n, 0:n]), l, ident_ok))
                edge_cols.append(pe(lambda e: e.transpose(bank(2)[:, h * 128:h * 128 + n], ESF[0:n, h, :], ident[0:n, 0:n]), s))
                edge_cols.append(pe(lambda e: e.transpose(bank(3)[:, h * 128:h * 128 + n], EKF[0:n, h, :], ident[0:n, 0:n]), k))
            halves()
            finish_late()
            fill_gap(2)
        c0 = act(lambda e: e.activation(E2[:, :, 0], bank(2)[:, 0:164], ACT.Copy), edge_cols)
        c1 = act(lambda e: e.activation(E2[:, :, 1], bank(3)[:, 0:164], ACT.Copy), edge_cols)
        edges_ok = [c0, c1]
        a = dve(lambda e: e.tensor_reduce(lohi[:, 0:1], bank(0)[0:NB, 0:164], axis=AX.X, op=ALU.min), lo_hi)
        b = dve(lambda e: e.tensor_reduce(lohi[:, 1:2], bank(1)[0:NB, 0:164], axis=AX.X, op=ALU.max), lo_hi)
        t0 = pe(lambda e: e.transpose(bank(6)[0:1, 0:NB], lohi[:, 0:1], ident[0:NB, 0:NB]), a, freed[6])
        t1 = pe(lambda e: e.transpose(bank(6)[0:1, NB:2 * NB], lohi[:, 1:2], ident[0:NB, 0:NB]), b)
        fill_gap(2)
        lo = dve(lambda e: e.tensor_scalar(lohr[:, 0, :], bank(6)[0:1, 0:NB], 164.0 - LOOK, None, op0=ALU.min), t0, t1)
        c = dve(lambda e: e.tensor_scalar(lohr[:, 1, :], lohr[:, 0, :], float(LOOK), None, op0=ALU.add), lo)
        d = dve(lambda e: e.tensor_tensor(lohr[:, 2, :], lohr[:, 1, :], bank(6)[0:1, NB:2 * NB], ALU.max), c)
        f = dve(lambda e: e.tensor_tensor(lohr[:, 3, :], lohr[:, 2, :], lohr[:, 1, :], ALU.subtract), d)
        g = dve(lambda e: e.tensor_reduce(many[:, 0:1], lohr[:, 3, :], axis=AX.X, op=ALU.max), f)
        many_ok = dve(lambda e: e.tensor_scalar(manyi[:, :], many[:, 0:1], 31.0 - LOOK, None, op0=ALU.is_gt), g)
        edges_done = [edges_ok, many_ok]
        bounds_ok = dve(lambda e: e.tensor_copy(bnd[:, :].rearrange("o (g w b) -> o w g b", g=10, w=4), lohr[:, :, :].rearrange("o w (g b) -> o w g b", b=4)), f)
        free(0, 1, a)
        free(1, 1, b)
        free(2, 1, c0)
        free(3, 1, c1)
        free(6, 1, lo, d)

        made, taken = [[q.sem(f"one_{n}{j}") for j in range(4)] for n in ("made", "taken")]
        asem = [q.sem(f"a_sem{i}") for i in range(2)]
        csem = [q.sem(f"c_sem{i}") for i in range(2)]
        regs = {}

        def register(e, name):
            if (e.engine, name) not in regs:
                regs[e.engine, name] = e.alloc_register(f"{e.engine.name}_{name}")
            return regs[e.engine, name]

        def bounds_of(e, g):
            r = [register(e, f"bound{i}") for i in range(16)]
            e.load(r, bnd[0:1, 16 * g:16 * g + 16])
            return r

        bounds = {}

        def load_bounds(add, g):
            def emit(e):
                bounds[e.engine] = bounds_of(e, g)
            return add(emit, bounds_ok)

        looked = []

        def edge_columns(b):
            def emit(e):
                lowest = e.snap(bounds[e.engine][b % 4], min_val=0, max_val=164 - LOOK)
                return e.tensor_copy(EC[:, b % 2, :, :], E2[:, bass.ds(lowest, LOOK), :])
            return dve(emit, edges_ok)

        def one_hot(e, i, b, src, key):
            e.tensor_scalar(OHS[:, i, 0:626], iota16[:, 0:626], src, None, op0=ALU.is_equal)
            return e.tensor_scalar(OHK[:, i, :], iota16[:, 0:128], 128.0 * b, key, op0=ALU.add, op1=ALU.is_equal)

        def one_hots(b, columns_ok):
            made_ok = []
            for k in range(LOOK):
                n = LOOK * b + k
                made_ok.append(dve(lambda e, k=k, n=n: one_hot(e, n % 5, b, EC[:, b % 2, k, 0:1], EC[:, b % 2, k, 1:2]), columns_ok, iota_ok, looked[n - 5] if n >= 5 else None))

            def past(e):
                r = bounds[e.engine]
                it = register(e, "round")
                with e.If_ne(r[12 + b % 4], 0):
                    with e.Fori(r[4 + b % 4], r[8 + b % 4], 4) as i:
                        e.reg_add(it, it, 1)
                        for j in range(4):
                            e.wait_ge(taken[j], it)
                            one_hot(e, 5 + j, b, E2[:, bass.ds(i + j, 1), 0], E2[:, bass.ds(i + j, 1), 1]).then_inc(made[j], 1)
            dve(past)
            return made_ok

        def count(b, s, made_ok):
            ps = bank(2 * s, 2)

            def look(e, i, first, last):
                for m in range(TT):
                    e.matmul(ps[0:PT, 128 * m:128 * m + 128], OHS[:, i, cols(m)], OHK[:, i, :], start=first and m in (0, 4), stop=last, skip_group_check=True)
                return e.matmul(ps[:, 640:768], ones16[:, :], OHK[:, i, :], start=False, stop=last, skip_group_check=True)
            for k in range(LOOK):
                n = LOOK * b + k
                looked.append(pe(lambda e, n=n, k=k: look(e, n % 5, k == 0, k == LOOK - 1), made_ok[k], ones_ok, freed[2 * s] if k == 0 else None, freed[2 * s + 1] if k == 0 else None))

            def past(e):
                r = bounds[e.engine]
                it = register(e, "round")
                with e.If_ne(r[12 + b % 4], 0):
                    with e.Fori(0, r[12 + b % 4], 4):
                        e.reg_add(it, it, 1)
                        for j in range(4):
                            e.wait_ge(made[j], it)
                            look(e, 5 + j, False, True).then_inc(taken[j], 1)
                return e.matmul(ps[0:PT, 0:8], zeros16[:, 0:PT], zeros16[:, 0:8], start=False, stop=True, skip_group_check=True)
            return pe(past, zeros_ok)

        def start_rounds(add, credit):
            def emit(e):
                e.reg_mov(register(e, "round"), 0)
                if credit:
                    for j in range(4):
                        e.sem_inc(taken[j], 1)
            return add(emit)
        start_rounds(dve, False)
        start_rounds(pe, True)
        edges_done.append(bounds_ok)
        stg_free = [edges_done, edges_done]
        stored, cnt_stored, summed, sum_free, evac, at_stored, degrees = [], [], [], [None] * 3, [], [], []
        adjt = scratch("adjacency_sum", [640, N])
        tas = [q.sem(f"ta_sem{i}") for i in range(2)]
        dis = const("rsqrt_degree", [PT, TT], F32)
        deg = const("degree", [PT, 2, TT], F32)
        deg_ok = dve(lambda e: e.memset(deg[:, 0, :], 1.0))

        def sum_kinds(c):
            stg, total = STG[c % 2], ALLC[c % 3][:, :, :]
            a = pool(lambda e: e.tensor_tensor(total, stg[:, :, 0, :], stg[:, :, 1, :], ALU.add), evac[c], sum_free[c % 3], edges_done)
            for r in range(2, 8):
                a = pool(lambda e, r=r: e.tensor_tensor(total, total, stg[:, :, r, :], ALU.add), a)
            summed.append(a)
            stg_free[c % 2] = [stg_free[c % 2], a]

        def turn_sum(c):
            ps = bank(6, 2).rearrange("p (m c) -> p m c", c=128)[0:64, 0:TT, 0:PT]
            i = c % 2

            def emit(e):
                for m in range(TT):
                    ins = e.transpose(ps[:, m, :], ALLC[c % 3][:, m, :], ident[0:PT, 0:PT])
                return ins
            a = pe(emit, summed[c], freed[6], freed[7])
            d = dve(lambda e: e.tensor_reduce(deg[:, 1, :], ALLC[c % 3][:, :, :], axis=AX.X, op=ALU.add), summed[c], degrees[-1] if degrees else deg_ok)
            degrees.append(dve(lambda e: e.tensor_tensor(deg[:, 0, :], deg[:, 0, :], deg[:, 1, :], ALU.add), d))
            b = dve(lambda e: e.scalar_tensor_tensor(TA[i][:, :, :], iota16[0:64, 0:N].rearrange("p (m c) -> p m c", m=TT), tgt[:, c:c + 1], ps,
                                                     op0=ALU.is_equal, op1=ALU.add), a, tgt_ok, edges_done, at_stored[c - 2] if c > 1 else None)
            free(6, 2, b)
            sum_free[c % 3] = [a, d]
            at_stored.append(dma("sync", tas[i], lambda e: e.dma_start(adjt[64 * c:64 * c + 64, :], TA[i][:, :, :].rearrange("p m c -> p (m c)")), b))

        load_bounds(dve, 0)
        columns_ok = edge_columns(0)
        finish_late()
        for b in range(NB):
            if b % 4 == 0:
                load_bounds(pe, b // 4)
            made_ok = one_hots(b, columns_ok)
            if b + 1 < NB:
                if b % 4 == 3:
                    load_bounds(dve, b // 4 + 1)
                columns_ok = edge_columns(b + 1)
            p = count(b, b % 2, made_ok)
            c, j = b // 4, b % 4
            if j == 0:
                evac.append([])

            def copy_out(b=b, p=p, c=c, j=j, stg=STG[c % 2], cst=CST[b // 2 % 2]):
                ps = bank(2 * (b % 2), 2)
                x = act(lambda e: e.activation(stg[:, :, :, 16 * j:16 * j + 16], ps[0:PT, 0:640].rearrange("p (m d r) -> p m r d", m=TT, d=16), ACT.Copy),
                        p, stg_free[c % 2] if j == 0 else None)
                y = act(lambda e: e.activation(cst[0:1, 128 * (b % 2):128 * (b % 2) + 128], ps[0:1, 640:768], ACT.Copy), p, cnt_stored[-2:-1] if b % 2 == 0 else None)
                free(2 * (b % 2), 2, x, y)
                evac[c].extend([x, y])
            copy_out()
            if b % 2:
                cnt_stored.append(dma("scalar", csem[b // 2 % 2], lambda e, b=b: e.dma_start(cntd[128 * b - 128:128 * b + 128].unsqueeze(0), CST[b // 2 % 2][:, :]), evac[c][-4:]))
            if j == 3:
                def store(c=c, stg=STG[c % 2]):
                    stored.append(dma("scalar", asem[c % 2], lambda e: e.dma_start(adj.rearrange("p m r d -> p (m r) d")[:, :, 64 * c:64 * c + 64], stg[:, :, :, :].rearrange("p m r d -> p (m r) d")), evac[c]))
                    stg_free[c % 2] = [stored[-1]]
                store()
                sum_kinds(c)
            if j == 2 and c >= 2:
                turn_sum(c - 2)
            finish_late()
            fill_gap()
        while next(filler, True) is None:
            finish_late()
        finish_late()
        turn_sum(8)
        turn_sum(9)
        dis_ok = rsqrt(deg[:, 0, :], dis[:, :], lnt[:, 6, :], lnt[:, 7, :], degrees[-1])
        W.subtract = dve
        mi = const("sel_int", [128, 2], I32)
        tokm = const("sel_token", [128, 1], U32)
        eqm = at("sel_equal", [128, 128], F32, P1 + 75776)
        eqi = at("sel_order", [128, 128], I32, P1 + 75776)
        low = at("sel_lower", [128, 128], F32, P1 + 76288)
        rev8 = const("sel_rev", [128, 8], F32)

        ml = dma("scalar", q.sem("sel_sem"), lambda e: e.dma_start(mi[:, :], A["L1_ffn_index"]))
        m_low = pool(lambda e: e.iota(eqi[:, :], [[1, 128]], base=0, channel_multiplier=-1), k_done)
        m_low = dve(lambda e: e.tensor_scalar(low[:, :], eqi[:, :], 0.0, None, op0=ALU.is_lt), m_low)
        rev_ok = dve(lambda e: e.tensor_scalar(rev8[:, :], iota16[:, 0:8], -1.0, 8.0, op0=ALU.mult, op1=ALU.add), iota_ok)
        m = dve(lambda e: e.tensor_copy(sel(0, 2), mi[:, :]), ml)
        m = dve(lambda e: e.tensor_scalar(sel(2, 2), sel(0, 2), 0.0, None, op0=ALU.is_lt), m)
        m = dve(lambda e: e.tensor_tensor(sel(0), sel(0), sel(2), ALU.add), m)
        m = dve(lambda e: e.scalar_tensor_tensor(sel(1), sel(3), float(N), sel(1), op0=ALU.mult, op1=ALU.add), m)
        m = dve(lambda e: e.tensor_scalar(sel(4), sel(1), 0.0, float(N - 1), op0=ALU.max, op1=ALU.min), m)
        tokm_ok = dve(lambda e: e.tensor_copy(tokm[:, :], sel(4)), m)
        m = dve(lambda e: e.tensor_tensor(sel(5), sel(4), sel(1), ALU.is_equal), tokm_ok)
        m = dve(lambda e: e.scalar_tensor_tensor(sel(5), sel(0), 0.0, sel(5), op0=ALU.is_equal, op1=ALU.mult), m)
        m = dve(lambda e: e.tensor_tensor(sel(6), sel(4), sel(10), ALU.subtract), m, m_own)
        m = dve(lambda e: e.scalar_tensor_tensor(sel(6), sel(6), sel(5), sel(10), op0=ALU.mult, op1=ALU.add), m)
        m = dve(lambda e: e.tensor_copy(eqm[:, :], sel(6).to_broadcast([128, 128])), m, m_low)

        def kept_places(m):
            m = pe(lambda e: e.transpose(bank(5)[:, 0:128], eqm[:, :], ident[:, :]), m, ident_ok, freed[5])
            m = dve(lambda e: e.scalar_tensor_tensor(eqm[:, :], bank(5)[:, 0:128], sel(6), low[:, :], op0=ALU.is_equal, op1=ALU.mult), m, m_low)
            free(5, 1, m)
            m = dve(lambda e: e.tensor_reduce(sel(7), eqm[:, :], axis=AX.X, op=ALU.max), m)
            return dve(lambda e: e.tensor_scalar(sel(7), sel(7), -1.0, 1.0, op0=ALU.mult, op1=ALU.add), m)

        def columns(b, xh, xl, mb, part, first, last, *after):
            wh, wl = W.pair(part)

            def emit(e):
                for j in range(2):
                    kt = 2 * (part % 4) + j
                    c = slice(512 * j + 128 * mb, 512 * j + 128 * mb + 128)
                    for n, (w, x) in enumerate(((wh, xh), (wh, xl), (wl, xh))):
                        for h in range(2):
                            ins = e.matmul(bank(b + h)[:, 0:NH], w[:, c], x[:, kt, NH * h:NH * h + NH],
                                           start=first and j == 0 and n == 0, stop=last and j == 1 and n == 2)
                return ins
            return pe(emit, W.ready(part), *after)

        def mixer(p, XH, XL, x_ok, base, k_done, v_done, before, denominator, finish):
            QT = at(f"q_cols_{p}", [128, 8, NP], F32, base + 20800)
            KV = at(f"kv_{p}", [128, 8, 130], F32, base + 40896)
            tmp = [at(f"q_tmp{i}_{p}", [128, 2, NH], F32, base + 45056 + 2528 * i) for i in range(2)]
            BQ = const(f"bias_q_{p}", [128, 8], F32)
            AO = [at(f"ao{i}_{p}", [PT, D], F32, base + 45056 + 4096 * i) for i in range(2)]
            nrm = [const(f"norm{i}_{p}", [PT, 8], F32) for i in range(2)]
            bq_ok = dma("gpsimd", q.sem(f"bq_{p}"), lambda e: e.dma_start(BQ[:, :], A[f"{p}_bq"]))
            q_done = []
            tmp_free = [before, before]
            for h in range(2):
                for mb in range(4):
                    def queries(h=h, mb=mb, m=4 * h + mb):
                        b, i = 2 * (m % 2), m % 2
                        for j, part in enumerate(Wq_of[p][h]):
                            s = columns(b, XH, XL, mb, part, j == 0, j == 3, freed[b], freed[b + 1], x_ok)
                            if mb == 3:
                                W.release(part, s)
                        W.split()
                        ps = bank(b, 2).rearrange("p (a c) -> p a c", a=2)[:, :, 0:NH]
                        qt = QT[:, m, :].rearrange("p (a c) -> p a c", a=2)
                        r = act(lambda e: e.activation(qt, ps, ACT.Relu, bias=BQ[:, m:m + 1]), s, bq_ok, before)
                        n = dve(lambda e: e.tensor_scalar(tmp[i][:, :, :], ps, BQ[:, m:m + 1], 0.0, op0=ALU.add, op1=ALU.min), s, bq_ok, r, tmp_free[i])
                        x = act(lambda e: e.activation(tmp[i][:, :, :], tmp[i][:, :, :], ACT.Exp), n)
                        d = dve(lambda e: e.tensor_tensor(qt, qt, tmp[i][:, :, :], ALU.add), x, r)
                        free(b, 2, r, n)
                        tmp_free[i] = d
                        q_done.append(d)
                    queries()

            kvp = bank(4, 4).rearrange("p (a c) -> p a c", a=8)

            def outer(e):
                for a in range(8):
                    for t in range(TT):
                        ins = e.matmul(kvp[:, a, 0:130], KN[:, t, 128 * a:128 * a + 128], VN[:, t, a, :], start=t == 0, stop=t == TT - 1)
                return ins
            o = pe(outer, k_done, v_done, [freed[i] for i in range(4, 8)])
            kv_ok = dve(lambda e: e.tensor_tensor(KV[:, :, :], kvp[:, :, 0:130], bdmask[:, :].unsqueeze(1).to_broadcast([128, 8, 130]), ALU.mult), o, bd_ok, before)
            free(4, 4, kv_ok)

            OH = at(f"ao_high_{p}", [128, 8, NP], F32R, base - 20480)
            OL = at(f"ao_low_{p}", [128, 8, NP], F32R, base - 20480 + 20096)
            ao_free, ao_ok = [None, None], []
            heads_done[p] = []
            for t in range(TT):
                halves = []
                for g in range(2):
                    def heads(t=t, g=g, b=2 * g):
                        ps = bank(b, 2).rearrange("p (a c) -> p a c", a=4)

                        def emit(e):
                            for a in range(4):
                                ins = e.matmul(ps[0:PT, a, 0:130], QT[:, 4 * g + a, cols(t)], KV[:, 4 * g + a, :], start=True, stop=True)
                            return ins
                        s = pe(emit, q_done, kv_ok, freed[b], freed[b + 1])
                        n = nrm[g][:, :].rearrange("p (a c) -> p a c", a=4)
                        m = dve(lambda e: e.tensor_scalar(n, ps[0:PT, :, 128:130], 1e-6, None, op0=denominator), s, ao_free[t % 2])
                        r = dve(lambda e: e.reciprocal(nrm[g][:, :], nrm[g][:, :]), m)
                        d = dve(lambda e: e.tensor_tensor(AO[t % 2][:, 512 * g:512 * g + 512].rearrange("p (a c d) -> p a c d", a=4, c=2),
                                                          ps[0:PT, :, 0:128].rearrange("p a (c d) -> p a c d", c=2),
                                                          n.unsqueeze(3).to_broadcast([PT, 4, 2, 64]), ALU.mult), r)
                        free(b, 2, m, d)
                        halves.append(d)
                        heads_done[p].append(d)
                    heads()
                ao_free[t % 2] = halves
                if t:
                    ao_ok.append(transpose_tile(t - 1, AO[(t - 1) % 2][:, :], OH, OL, 4 + 2 * (t % 2), ao_free[(t - 1) % 2], kv_ok))
            ao_ok.append(transpose_tile(4, AO[0][:, :], OH, OL, 4, ao_free[0], kv_ok))
            for t in range(TT):
                ao_free[t % 2] = ao_free[t % 2] + ao_ok[t]
            for h in range(2):
                for t in range(TT):
                    b = (5 * h + t) % 4
                    s = rows_tile(t, Wo_of[p][h], OH, OL, b, ao_ok[t])
                    W.split(4 if t == TT - 1 else 1)
                    finish(h, t, b, s)
            return ao_ok

        heads_done = {}
        acc = scratch("x_mixed", [N, D])
        XB = at("x_base", [PT, TT, D], F32, P1 + 41280)
        BO = at("bias_o", [PT, 512], F32, P1 + 73728)
        bos = q.sem("bo_sem")
        xbs = [q.sem(f"xb_sem{t}") for t in range(TT)]
        abs_ = [q.sem(f"ab_sem{i}") for i in range(3)]
        lnx = const("x_twice", [PT, 2, TT], F32)
        acc_stored, xb_ok = [], {}

        def mixed_base():
            a = dve(lambda e: e.tensor_scalar(lnx[:, 0, :], rstd[:, :], 1.0, None, op0=ALU.add))
            b = dve(lambda e: e.scalar_tensor_tensor(lnx[:, 1, :], lnmv[:, :, 0], -1.0, rstd[:, :], op0=ALU.mult, op1=ALU.mult))
            n, o = {}, None
            for h in range(2):
                o = dma("sync", bos, lambda e, h=h: e.dma_start(BO[:, :], A["L0_mix_bo"][512 * h:512 * h + 512].partition_broadcast(PT)), counted, list(xb_ok.values()))
                for t in range(TT):
                    def tile(h=h, t=t, x=XB[:, t, :], sl=slice(512 * h, 512 * h + 512)):
                        if h == 0:
                            l = dma("scalar", xbs[t], lambda e: e.dma_start(x, A["x"][t * PT:(t + 1) * PT, :]), heads_done["L0_mix"])
                            n[t] = act(lambda e: e.activation(x, x, ACT.Identity, bias=lnx[:, 1, t:t + 1], scale=lnx[:, 0, t:t + 1]), l, a, b)
                        xb_ok[t, h] = pool(lambda e: e.tensor_tensor(x[:, sl], x[:, sl], BO[:, :], ALU.add), n[t], o)
                    tile()

        def add_mixed(h, t, b, s):
            i = (5 * h + t) % 3
            sl = slice(512 * h, 512 * h + 512)
            if not xb_ok:
                mixed_base()
            d = dve(lambda e: e.tensor_tensor(XB[:, t, sl], XB[:, t, sl], bank(b)[0:PT, :], ALU.add), xb_ok[t, h], s)
            free(b, 1, d)
            acc_stored.append(dma("sync", abs_[i], lambda e: e.dma_start(acc[t * PT:(t + 1) * PT, sl], XB[:, t, sl]), d))

        counted = [stored, cnt_stored, at_stored, dis_ok, evac, summed, degrees, k_done, v_done, root_stored]
        W.grow(range(7, 12), counted)
        mixed = mixer("L0_mix", XTH, XTL, [xt_ok, pads], P1 + 20480, k_done, [v_done, ones_v], counted, ALU.max, add_mixed)
        kept_ok = kept_places(m)

        U = at("u_rows", [PT, TT, D], F32, P1)
        AR = [at(f"a_kind{i}", [PT, TT, NP], F32R, P1 + 20480 + 12576 * i) for i in range(2)]
        Y0 = P1 + 45632
        YH = [at(f"y_high{i}", [PT, 512], F32R, Y0 + 4096 * i) for i in range(8)]
        YL = [at(f"y_low{i}", [PT, 512], F32R, Y0 + 4096 * i + 2048) for i in range(8)]
        BR = at("bias_root", [PT, D], F32, Y0 + 7 * 4096)
        rc = const("one_over_count", [PT, TT, 8], F32)
        arsem = [q.sem(f"ar_sem{i}") for i in range(2)]

        done_mix = [acc_stored, mixed, kept_ok]
        cl = dma("gpsimd", q.sem("cnt_sem"), lambda e: e.dma_start(rc[:, :, :], cntd[0:5000].rearrange("(j p r) -> p j r", p=PT, r=8)), cnt_stored)
        c1 = dve(lambda e: e.tensor_scalar(rc[:, :, :], rc[:, :, :], 1.0, None, op0=ALU.max), cl)
        rc_ok = dve(lambda e: e.reciprocal(rc[:, :, :], rc[:, :, :]), c1)
        br_ok = dma("sync", q.sem("br_sem"), lambda e: e.dma_start(BR[:, :], A["L0_gnn_bias"].partition_broadcast(PT)), done_mix)
        u_done = {}
        usem = [q.sem(f"u_sem{t}") for t in range(TT)]
        for t in range(TT):
            def roots(t=t):
                l = dma("sync", usem[t], lambda e: e.dma_start(U[:, t, :], rootd[t * PT:(t + 1) * PT, :]), done_mix, root_stored)
                u_done[t, 0] = u_done[t, 1] = pool(lambda e: e.tensor_tensor(U[:, t, :], U[:, t, :], BR[:, :], ALU.add), l, br_ok)
            roots()
        y_ok = [None] * 8
        y_used = [done_mix] * 7 + [list(u_done.values())]
        ar_ok, ar_used = [None, None], [done_mix, done_mix]
        manyr = {}

        def load_many(e):
            manyr[0] = e.alloc_register("pe_many")
            return e.load(manyr[0], manyi[0:1, 0:1])
        pe(load_many, many_ok)

        def load_kind(r):
            i = r % 2
            ar_ok[i] = dma("gpsimd", arsem[i], lambda e: e.dma_start(AR[i][:, :, 0:N].bitcast(F32), adj[:, :, r, 0:N]), ar_used[i], stored)

        def make_y(r, h, m):
            n = 5 * (2 * r + h) + m
            b, i = n % 4, n % 8
            s = rows_tile(m, Wrel[r][h], XTH, XTL, b, [xt_ok, pads])
            W.split()
            x = act(lambda e: e.activation(YH[i][:, :], bank(b)[0:PT, :], ACT.Copy), s, y_used[i])
            y = dve(lambda e: e.tensor_tensor(YL[i][:, :], bank(b)[0:PT, :], YH[i][:, :], ALU.subtract), x)
            free(b, 1, x, y)
            y_ok[i] = [x, y]

        agg_n = [0]

        def aggregate(r, h):
            slots = [(5 * (2 * r + h) + m) % 8 for m in range(TT)]
            last = []
            banks = []
            for _ in range(TT):
                banks.append(4 + agg_n[0] % 4)
                agg_n[0] += 1

            def products(e, j, dt):
                for m in range(TT):
                    i = slots[m]
                    for n, y in enumerate((YH[i], YL[i])):
                        a, w = AR[r % 2][:, m, cols(j)], y[:, :]
                        if dt == F32:
                            a, w = a.bitcast(F32), w.bitcast(F32)
                        ins = e.matmul(bank(banks[j])[0:PT, :], a, w, start=m == 0 and n == 0, stop=m == TT - 1 and n == 1)
                return ins
            for j in range(TT):
                def one(j=j):
                    b = banks[j]

                    def emit(e):
                        sem, value = s.sem, 1
                        with e.If_ne(manyr[0], 0):
                            products(e, j, F32).then_inc(sem, value)
                        with e.Else():
                            products(e, j, F32R).then_inc(sem, value)
                        return None
                    s = pe(emit, [y_ok[i] for i in slots], ar_ok[r % 2], freed[b])
                    s.own = True
                    u = dve(lambda e: e.scalar_tensor_tensor(U[:, j, 512 * h:512 * h + 512], bank(b)[0:PT, :], rc[:, j, r:r + 1], U[:, j, 512 * h:512 * h + 512],
                                                             op0=ALU.mult, op1=ALU.add), s, rc_ok, u_done[j, h])
                    free(b, 1, u)
                    u_done[j, h] = u
                    last.append(s)
                one()
            for i in slots:
                y_used[i] = last
            if h == 1:
                ar_used[r % 2] = last

        load_kind(0)
        load_kind(1)
        for r in range(8):
            if r == 6:
                W.drop(LAST)
            for h in range(2):
                for m in range(TT):
                    if m == 2 and (r, h) != (0, 0):
                        pr, ph = (r, 0) if h else (r - 1, 1)
                        aggregate(pr, ph)
                        if ph == 1 and pr + 2 < 8:
                            load_kind(pr + 2)
                    make_y(r, h, m)

        G0 = P1 + 20480
        UTH = at("ut_high", [128, 8, NP], F32R, G0)
        UTL = at("ut_low", [128, 8, NP], F32R, G0 + 20096)
        XG = [at(f"x_tile{i}", [PT, D], F32, LENT + 4096 * i) for i in range(2)]
        BG = at("bias_g", [PT, D], F32, LENT + 8192)
        GT = [at(f"g_tile{i}", [PT, 512], F32, G0 + 40192 + 2048 * i) for i in range(4)]
        AP_ = [at(f"a_tile{i}", [PT, 512], F32, G0 + 48384 + 2048 * i) for i in range(4)]
        xgs = [q.sem(f"xg_sem{i}") for i in range(2)]
        aps = [q.sem(f"ap_sem{i}") for i in range(4)]

        def gate_rows(h, t, top, b):
            for j, part in enumerate(Wgate[h][top]):
                s = rows(bank(b)[0:PT, :], UTH if top else XTH, UTL if top else XTL, cols(t), part, (2 * j, 2 * j + 1),
                         top == 0 and j == 0, top == 1 and j == 3, freed[b] if not top else None, ut_ok[t] if top else [xt_ok, pads])
                if t == TT - 1:
                    W.release(part, s)
            W.split()
            return s

        ut_ok, d_ok, xg_free = {}, {}, [None, None]
        gate_rows(0, 0, 0, 0)
        gate_rows(0, 1, 0, 1)
        aggregate(7, 1)
        agg_last = [y_used, ar_used, list(u_done.values())]
        bg_ok = dma("sync", q.sem("bg_sem"), lambda e: e.dma_start(BG[:, :], A["L0_gnn_b_gate"].partition_broadcast(PT)), W.lent(LAST))

        def delta(t):
            i = t % 2
            ut_ok[t] = transpose_tile(t, U[:, t, :], UTH, UTL, 6, u_done[t, 0], u_done[t, 1], agg_last)
            l = dma("sync", xgs[i], lambda e: e.dma_start(XG[i][:, :], A["x"][t * PT:(t + 1) * PT, :]), W.lent(LAST), xg_free[i])
            n = normalize(t, XG[i][:, :], XG[i][:, :], rstd, l)
            x = act(lambda e: e.activation(U[:, t, :], U[:, t, :], ACT.Tanh), ut_ok[t])
            d_ok[t] = xg_free[i] = pool(lambda e: e.tensor_tensor(U[:, t, :], U[:, t, :], XG[i][:, :], ALU.subtract), x, n)

        x1_done = {}
        ap_ok, gt_free = [], [None] * 4

        def load_acc(*after):
            n = len(ap_ok)
            h, t = divmod(n, TT)
            if h < 2:
                ap_ok.append(dma("sync", aps[n % 4], lambda e: e.dma_start(AP_[n % 4][:, :], acc[t * PT:(t + 1) * PT, 512 * h:512 * h + 512]), acc_stored, *after))

        def gated(h, t, s):
            i = (5 * h + t) % 4
            sl = slice(512 * h, 512 * h + 512)
            l = ap_ok[5 * h + t]
            z = dve(lambda e: e.tensor_tensor(GT[i][:, :], bank(t)[0:PT, :], BG[:, sl], ALU.add), s, bg_ok, gt_free[i], agg_last)
            free(t, 1, z)
            w = dve(lambda e: e.tensor_tensor(GT[i][:, :], GT[i][:, :], U[:, t, sl], ALU.mult), z, d_ok[t])
            x = dve(lambda e: e.tensor_tensor(U[:, t, sl], GT[i][:, :], AP_[i][:, :], ALU.add), w, l)
            gt_free[i] = x
            load_acc(x)
            x1_done[t, h] = x

        for t in range(2, TT):
            gate_rows(0, t, 0, t)
            delta(t - 2)
        for _ in range(4):
            load_acc(agg_last)
        for t in range(TT):
            s = gate_rows(0, t, 1, t)
            if t + 3 < TT:
                delta(t + 3)
            gated(0, t, s)
        for t in range(TT):
            gate_rows(1, t, 0, t)

        x1d, xn1d = scratch("x1_rows", [N, D]), scratch("xn1_rows", [N, D])
        scale2 = const("scale2", [PT, TT], F32)
        x1s = [q.sem(f"x1_sem{t}") for t in range(TT)]
        n1s = [q.sem(f"n1_sem{t}") for t in range(TT)]
        x1_stored, xn1_stored, xt1_ok = {}, {}, {}

        def ln_then_std(a, b, x, after):
            ve, v, s, w, h = [lnt[:, k, a:b] for k in (0, 2, 3, 4, 5)]
            c = dve(lambda e: e.tensor_scalar(ve, lnmv[:, a:b, 1], EPS, None, op0=ALU.add), moments(a, b, x, after))
            c = dve(lambda e: e.reciprocal(s, ve), c)
            c = dve(lambda e: e.scalar_tensor_tensor(v, lnmv[:, a:b, 1], 1024.0 / 1023.0, s, op0=ALU.mult, op1=ALU.mult), c)
            c = dve(lambda e: e.tensor_scalar(v, v, 1e-30, None, op0=ALU.max), c)
            c = rsqrt(v, s, w, h, c)
            c = dve(lambda e: e.tensor_tensor(v, v, s, ALU.mult), c)
            c = dve(lambda e: e.scalar_tensor_tensor(v, v, EPS, ve, op0=ALU.add, op1=ALU.mult), c)
            return rsqrt(v, scale2[:, a:b], w, h, c)

        S16 = at("right_kqv", [PT, TT, 3, 256], F16, K0)
        DOWN = at("leaf_of_node", [PT, 2, 128], F16, K0 + 7680)
        down_free = []
        SL16 = [at(f"slot16{i}", [PT, TT, 128], F16, K0 + 8192 + 1280 * i) for i in range(2)]
        NB3 = at("node_b", [PT, 768], F32, R0 + 61440)
        tokidi = at("tokid_int", [PT, TT], I32, R0 + 64512)
        iotai = at("iota2_int", [128, 128], I32, R0 + 64544)
        tri16 = const("tri16", [128, 128], F16)
        thr = const("group_first", [128, 9], F32)
        tokid = const("tokid", [PT, TT], F32)
        leaf = {f: const(f"leaf_{f}", [PT, TT, n], F32) for f, n in (("k", 1), ("qv", 2), ("f", 1))}
        H16 = const("group_from", [PT, 10, 9], F16)
        G16 = const("group16", [PT, 10, 8], F16)
        gx = const("group_rank", [PT, 10, 8], F32)
        rank = const("rank", [PT, 10], F32)
        grp = const("group_number", [PT, 10], F32)
        MV = const("moving16", [PT, 10, 24], F16)
        stmp = const("slot_tmp", [128, 16], F32)
        cnt = const("group_counts", [1, 40], F32)
        OUTI = {f: const(f"row_{f}", [128, 8], U32) for f in FF}
        LF = {f: const(f"slot_leaf_{f}", [128, 8], F32) for f in FF}
        PLACE = {f: const(f"place_{f}", [PT, TT], F32) for f in FF}
        MV4 = {f: const(f"moving4_{f}", [PT, TT, 4], F16) for f in FF}
        MORE = const("more_rounds", [1, 4], I32)

        def bc(ap, n):
            return ap.unsqueeze(2).to_broadcast([ap.shape[0], ap.shape[1], n])

        def node_logits(f, t, dst, xh, xl, xs, *after):
            w = dst.shape[-1]
            kts = 1024 // w
            for j, part in enumerate(Wnode[f]):
                def emit(e, j=j, last=j == len(Wnode[f]) - 1, pair=W.pair(part)):
                    wh, wl = pair
                    for k in range(kts):
                        c = slice(w * k, w * k + w)
                        for n, (x, y) in enumerate(((xh, wh), (xh, wl), (xl, wh))):
                            ins = e.matmul(dst, x[:, kts * j + k, xs], y[:, c], start=j == 0 and k == 0 and n == 0, stop=last and k == kts - 1 and n == 2)
                    return ins
                s = pe(emit, W.ready(part), *after)
                if t == TT - 1:
                    W.release(part, s)
            return s

        def goes_right(S, ps, nb, *after):
            return dve(lambda e: e.scalar_tensor_tensor(S, nb, -1.0, ps, op0=ALU.mult, op1=ALU.is_lt), *after)

        def leaf_numbers(S, n, lf, *after):
            v = DOWN[:, 0:n, :]
            d = dve(lambda e: e.scalar_tensor_tensor(v, iota16[0:PT, 0:128].unsqueeze(1).to_broadcast([PT, n, 128]), 2.0, S[:, :, 127:255], op0=ALU.mult, op1=ALU.add), down_free[:], *after)
            for l in range(6, -1, -1):
                def level(w=1 << l, step=64 >> l, d=d):
                    return dve(lambda e: e.copy_predicated(v[:, :, 0:128:2 * step], S[:, :, w - 1:2 * w - 1].bitcast(U16), v[:, :, step:128:2 * step]), d)
                d = level()
            down_free[:] = [dve(lambda e: e.tensor_copy(lf, v[:, :, 0]), d)]
            return down_free[:]

        def route(fs, lf, leaf_ok, b, *after):
            n = len(fs)
            m = TT * n
            ps = bank(b)
            g3 = G16[:, 0:m, :]
            h = dve(lambda e: e.tensor_tensor(H16[:, 0:m, :], thr[0:PT, :].unsqueeze(1).to_broadcast([PT, m, 9]),
                                              bc(lf[:, :, :].rearrange("p t f -> p (t f)"), 9), ALU.is_le), leaf_ok, *after)
            g = dve(lambda e: e.tensor_tensor(g3, H16[:, 0:m, 0:8], H16[:, 0:m, 1:9], ALU.subtract), h)

            def ranks(e):
                for t in range(TT):
                    for u in range(t + 1):
                        ins = e.matmul(ps[0:PT, 8 * n * t:8 * n * t + 8 * n], (tri16 if u == t else ones16)[0:PT, 0:PT], G16[:, n * u:n * u + n, :].rearrange("p f g -> p (f g)"),
                                       start=u == 0, stop=u == t)
                for t in range(TT):
                    ins = e.matmul(ps[0:PT, 128:128 + 8 * n], ones16[0:PT, 0:PT], G16[:, n * t:n * t + n, :].rearrange("p f g -> p (f g)"), start=t == 0, stop=t == TT - 1)
                return ins
            v = [dve(lambda e: e.tensor_tensor(MV[:, 0:m, 8:16], g3, bc(lf[:, :, :].rearrange("p t f -> p (t f)"), 8), ALU.mult), g, *after),
                 dve(lambda e: e.tensor_copy(MV[:, 0:m, 16:24], g3), g, *after)]
            for i in range(n):
                v.append(dve(lambda e, i=i: e.tensor_tensor(MV[:, i:m:n, 0:8], G16[:, i:m:n, :], bc(tokid[:, :], 8), ALU.mult), g, tok_ok))
            yield
            k = pe(ranks, g, tri_ok, freed[b])
            yield
            x = dve(lambda e: e.tensor_tensor(gx[:, 0:m, :], ps[0:PT, 0:8 * m].rearrange("p (m g) -> p m g", g=8), g3, ALU.mult), k, *after)
            r = dve(lambda e: e.tensor_reduce(rank[:, 0:m], gx[:, 0:m, :], axis=AX.X, op=ALU.add), x)
            hot = []
            for i in range(n):
                hot += [dve(lambda e, t=t, i=i: e.tensor_scalar(SL16[i][:, t, :], iota16[0:PT, 0:128], rank[:, n * t + i:n * t + i + 1], None, op0=ALU.is_equal), r, *after)
                        for t in range(TT)]
            c = dve(lambda e: e.tensor_copy(cnt[:, 0:8 * n], ps[0:1, 128:128 + 8 * n]), k, *after)
            yield

            def tokens(e):
                for i in range(n):
                    for t in range(TT):
                        ins = e.matmul(ps[:, 192 + 32 * i:216 + 32 * i], SL16[i][:, t, :], MV[:, n * t + i, :], start=t == 0, stop=t == TT - 1)
                return ins
            s = pe(tokens, hot, v, x, c)
            yield
            read = []
            for i, f in enumerate(fs):
                def layer(i=i, f=f, o=ps[:, 192 + 32 * i:216 + 32 * i], tmp=stmp[:, 8 * i:8 * i + 8]):
                    w = dve(lambda e: e.tensor_scalar(tmp, o[:, 16:24], -4096.0, 4096.0, op0=ALU.mult, op1=ALU.add), s, *after)
                    j = dve(lambda e: e.tensor_copy(LF[f][:, :], o[:, 8:16]), s)
                    w = dve(lambda e: e.tensor_tensor(OUTI[f][:, :], tmp, o[:, 0:8], ALU.add), w)
                    routed[f] = {"rows": w, "leaves": j, "all": [w, j]}
                    read.extend([w, j])
                layer()
            free(b, 1, read)
            yield
            y = dve(lambda e: e.tensor_reduce(grp[:, 0:m], H16[:, 0:m, :], axis=AX.X, op=ALU.add), g)
            y = dve(lambda e: e.tensor_scalar(grp[:, 0:m], grp[:, 0:m], -1.0, None, op0=ALU.add), y)
            c = dve(lambda e: e.tensor_reduce(cnt[:, 24:24 + n], cnt[:, 0:8 * n].rearrange("o (f g) -> o f g", g=8), axis=AX.X, op=ALU.max), c)
            for i, f in enumerate(fs):
                def more(i=i, f=f, c=c):
                    lt, gr, rk = lf[:, :, i], grp[:, i:m:n], rank[:, i:m:n]
                    out = [dve(lambda e: e.scalar_tensor_tensor(PLACE[f][:, :], gr, 640.0, rk, op0=ALU.mult, op1=ALU.add), y, r),
                           dve(lambda e: e.scalar_tensor_tensor(MV4[f][:, :, 1], gr, -32.0, lt, op0=ALU.mult, op1=ALU.add), y),
                           dve(lambda e: e.tensor_copy(MV4[f][:, :, 0], tokid[:, :]), tok_ok),
                           dve(lambda e: e.memset(MV4[f][:, :, 2], 1.0)),
                           dve(lambda e: e.tensor_copy(MV4[f][:, :, 3], lt), leaf_ok)]
                    a = dve(lambda e: e.tensor_scalar(cnt[:, 32:36], iota16[0:1, 1:5], 128.0, cnt[:, 24 + i:25 + i], op0=ALU.mult, op1=ALU.is_lt), c)
                    a = dve(lambda e: e.tensor_reduce(cnt[:, 36:37], cnt[:, 32:36], axis=AX.X, op=ALU.add), a)
                    a = dve(lambda e: e.tensor_copy(MORE[:, "kqvf".index(f):"kqvf".index(f) + 1], cnt[:, 36:37]), a)
                    routed[f]["all"] += out + [a]
                    return a
                c = more()
            yield

        routed = {}

        def finish(stages, n=-1):
            while n and next(stages, 0) is None:
                n -= 1

        second, decided, qv_ok = {}, {}, {}
        leaf_ok = {"k": [], "qv": []}

        def norm_twice(a, b):
            x = {t: [x1_done[t, 0], x1_done[t, 1]] for t in range(a, b)}
            for t in range(a, b):
                x1_stored[t] = dma("sync", x1s[t], lambda e, t=t: e.dma_start(x1d[t * PT:(t + 1) * PT, :], U[:, t, :]), x[t])
            c = ln_then_std(a, b, U, x)
            for t in range(a, b):
                second[t] = normalize(t, U[:, t, :], U[:, t, :], scale2, c, x1_stored[t])
                xn1_stored[t] = dma("sync", n1s[t], lambda e, t=t: e.dma_start(xn1d[t * PT:(t + 1) * PT, :], U[:, t, :]), second[t])

        def turn_second(t):
            xt1_ok[t] = transpose_tile(t, U[:, t, :], XTH, XTL, 6 - 2 * (t % 2), second[t])

        def decide_k(t):
            b = 2 + t % 2
            s = node_logits("k", t, bank(b)[0:PT, 0:256], XTH, XTL, cols(t), xt1_ok[t], freed[b])
            r = goes_right(S16[:, t, 0, :], bank(b)[0:PT, 0:256], NB3[:, 0:256], s, nb_ok)
            free(b, 1, r)
            leaf_ok["k"].append(leaf_numbers(S16[:, t, 0:1, :], 1, leaf["k"][:, t, :], r))

        def decide_qv(t):
            b = t % 2
            s = node_logits("qv", t, bank(b)[0:PT, :], XTH, XTL, cols(t), xt1_ok[t], freed[b])
            qv_ok[t] = goes_right(S16[:, t, 1:3, :].rearrange("p f j -> p (f j)"), bank(b)[0:PT, :], NB3[:, 256:768], s, nb_ok)
            free(b, 1, qv_ok[t])
            return s

        def leaves_qv(t):
            leaf_ok["qv"].append(leaf_numbers(S16[:, t, 1:3, :], 2, leaf["qv"][:, t, :], qv_ok[t]))

        for t in range(TT):
            gated(1, t, gate_rows(1, t, 1, t))
            if t == 1:
                norm_twice(0, 2)
        gate_done = list(x1_done.values())
        nbs = q.sem("nb_sem")
        nb_ok = dma("sync", nbs, lambda e: e.dma_start(NB3[:, :], A["L0_ffn_nb"][0:768].partition_broadcast(PT)), gate_done)
        W.pooled = (0, 1, 2, 3)
        turn_second(0)
        turn_second(1)
        W.split(6)
        norm_twice(2, 5)
        W.grow([*LEAF_K, *LEAF_Q, *LAST], gate_done)
        for t in range(2):
            decide_k(t)
        for t in range(2):
            decide_qv(t)
        turn_second(2)
        turn_second(3)
        decide_k(2)
        ia = pool(lambda e: e.iota(iotai[:, :], [[1, 128]], base=0, channel_multiplier=-1), gate_done)
        ib = pool(lambda e: e.iota(tokidi[:, :], [[PT, TT]], base=0, channel_multiplier=1), gate_done)
        tri_ok = dve(lambda e: e.tensor_scalar(tri16[:, :], iotai[:, :], 0.0, None, op0=ALU.is_gt), ia)
        tok_ok = [dve(lambda e: e.tensor_copy(tokid[:, :], tokidi[:, :]), ib),
                  dve(lambda e: e.tensor_scalar(thr[:, :], iota16[:, 0:9], 32.0, None, op0=ALU.mult))]
        turn_second(4)
        decide_k(3)
        decide_k(4)
        stages = route("k", leaf["k"], leaf_ok["k"], 4)
        finish(stages, 1)
        for t in range(2):
            leaves_qv(t)
        decide_qv(2)
        finish(stages, 2)
        decide_qv(3)
        finish(stages, 2)
        leaves_qv(2)
        logits_done = decide_qv(4)
        decided = [qv_ok[t] for t in range(3, TT)]
        xt1_all, xn1_all = [xt1_ok[t] for t in range(TT)], [xn1_stored[t] for t in range(TT)]
        yb = {f: scratch(f"leaf_rows_{f}", [N, D]) for f in FF}
        XGH = [at(f"xg_high{i}", [128, 8, 128], F32R, R0 + 8192 * i) for i in range(2)]
        XGL = [at(f"xg_low{i}", [128, 8, 128], F32R, R0 + 8192 * i + 4096) for i in range(2)]
        HM = [at(f"h_masked{i}", [128, 512], F32, R0 + 16384 + 2048 * i) for i in range(2)]
        HTH = [at(f"ht_high{i}", [128, 4, 128], F32R, R0 + 20480 + 4096 * i) for i in range(2)]
        HTL = [at(f"ht_low{i}", [128, 4, 128], F32R, R0 + 20480 + 4096 * i + 2048) for i in range(2)]
        YO = [at(f"y_out{i}", [128, D], F32, R0 + 28672 + 4096 * i) for i in range(2)]
        XR = [at(f"xg_rows{i}", [128, D], F32, R0 + o) for i, o in enumerate((47104, 40960))]
        LMT = [at(f"leaf_cols{i}", [128, 128], F32R, R0 + 45056 + 512 * i) for i in range(3)]
        LM = [at("leaf_mask0", [128, 128], F32, R0 + 46592), const("leaf_mask1", [128, 128], F32)]
        BR1, B1 = [at(f"b1_{n}", [128, 512], dt, R0 + o) for n, dt, o in (("raw", F32, 36864), ("parts", F32R, 38912))]
        BR2, B2 = [at(f"b2_{n}", [128, D], dt, R0 + o) for n, dt, o in (("raw", F32, 51200), ("parts", F32R, 55296))]
        QA = [at(f"q_rows{i}", [PT, D], F32, R0 + 59392 + 4096 * i) for i in range(2)]
        sx = [q.sem(f"xg2_sem{i}") for i in range(2)]
        sb = [[q.sem(f"leaf_b{i}_sem{j}") for j in range(2)] for i in range(2)]
        sy = [q.sem(f"yo_sem{i}") for i in range(2)]
        sqa = [q.sem(f"qa_sem{i}") for i in range(2)]

        def rows_of(table, index):
            return dict(in_=table, out_offset=None, in_offset=bass.IndirectOffsetOnAxis(ap=index, axis=0))

        class Leaves:

            def __init__(self):
                self.n = 0
                self.xg_free, self.xt_free, self.hm_free, self.ht_free = [[None, None] for _ in range(4)]
                self.yo_free, self.lm_free, self.lmt_free = [None, None], [None, None], [None, None, None]
                self.b_free, self.b_ok, self.b_raw, self.raw_free = [None, None], [None, None], [{}, {}], [[None, None], [None, None]]

            def biases(self, queue, layer, u, *after):
                f, g = self.units[u]
                raw, i = (BR1, BR2)[layer], u // 2 % 2
                src = A[f"L0_ffn_{f}_bd"] if layer == 0 else A[f"L0_ffn_{f}_b2"]
                self.b_raw[layer][u] = dma(queue, sb[layer][i], lambda e: e.dma_start(raw[64 * i:64 * i + 64, :], src[32 * g:32 * g + 64, :]),
                                           self.raw_free[layer][i], *after)

            def split_biases(self, layer, u, *after):
                i = u // 2 % 2
                raw, parts = ((BR1, B1), (BR2, B2))[layer]
                here, there = slice(64 * i, 64 * i + 64), slice(64 - 64 * i, 128 - 64 * i)
                h = act(lambda e: e.activation(parts[here, :], raw[here, :], ACT.Copy), self.b_raw[layer][u], self.b_free[layer], *after)
                l = dve(lambda e: e.tensor_tensor(parts[there, :], raw[here, :], parts[here, :], ALU.subtract), h, self.b_free[layer])
                self.b_ok[layer] = self.raw_free[layer][i] = [h, l]

            def gather(self, n, f, g, table, ready, *after):
                i = n % 2
                return dma("gpsimd", sx[i], lambda e: e.indirect_dma_start(out=XR[i][:, :], **rows_of(table, OUTI[f][:, g:g + 1]), bounds_check=N - 1, oob_is_err=False),
                           ready, self.xg_free[i], *after)

            def mask(self, n, f, g, lf, *after):
                i = n % 2
                some = iota16[:, 64 * (g // 2):64 * (g // 2) + 64].unsqueeze(1).to_broadcast([128, 2, 64])
                return dve(lambda e: e.tensor_scalar(LM[i][:, :].rearrange("p (a l) -> p a l", a=2), some, LF[f][:, g:g + 1], None, op0=ALU.is_equal), lf, self.lm_free[i], *after)

            def turn(self, n, m, got, *after):
                i = n % 2
                ps = bank(0, 2).rearrange("p (k c) -> p k c", k=8)

                def emit(e):
                    for k in range(8):
                        ins = e.transpose(ps[:, k, :], XR[i][:, 128 * k:128 * k + 128], ident[:, :])
                    return ins
                a = pe(emit, got, freed[0], freed[1])
                t = pe(lambda e: e.transpose(bank(4)[:, 0:128], LM[i][:, :], ident[:, :]), m, freed[4])
                h = act(lambda e: e.activation(XGH[i][:, :, :], ps, ACT.Copy), a, self.xt_free[i], *after)
                l = dve(lambda e: e.tensor_tensor(XGL[i][:, :, :], ps, XGH[i][:, :, :], ALU.subtract), h)
                o = act(lambda e: e.activation(LMT[n % 3][:, :], bank(4)[:, 0:128], ACT.Copy), t, self.lmt_free[n % 3], *after)
                free(0, 2, h, l)
                free(4, 1, o)
                self.xg_free[i] = a
                return [h, l], [t, m, o]

            def first(self, n, u, xt, lm, gelu, *after):
                f, g = self.units[u]
                i, b = n % 2, 7
                for j, part in enumerate(Wf1[f, g]):
                    s = rows(bank(b), XGH[i], XGL[i], slice(0, 128), part, (2 * j, 2 * j + 1), j == 0, False, freed[b], xt)
                    W.release(part, s)
                    W.split()
                    if j == 0 and u % 2 == 0:
                        self.split_biases(0, u, *after)

                s = pe(lambda e: e.matmul(bank(b), LMT[n % 3][:, :], B1[:, :], start=False, stop=True), lm, self.b_ok[0])
                self.b_free[0] = s
                self.xt_free[i] = s
                hm = HM[i][:, :].rearrange("p (l w) -> p l w", w=16)
                mask = bc(LM[i][:, 32 * (g % 2):32 * (g % 2) + 32], 16)
                if gelu:
                    c = act(lambda e: e.activation(HM[i][:, :], bank(b), ACT.Gelu), s, self.hm_free[i], *after)
                    d = dve(lambda e: e.tensor_tensor(hm, hm, mask, ALU.mult), c)
                else:
                    c = d = dve(lambda e: e.scalar_tensor_tensor(hm, bank(b).rearrange("p (l w) -> p l w", w=16), 0.0, mask, op0=ALU.max, op1=ALU.mult), s, self.hm_free[i], *after)
                free(b, 1, c)
                self.lm_free[i] = [d, lm]
                return d

            def turn_h(self, n, d, *after):
                i = n % 2
                ps = bank(4).rearrange("p (k c) -> p k c", k=4)

                def emit(e):
                    for k in range(4):
                        ins = e.transpose(ps[:, k, :], HM[i][:, 128 * k:128 * k + 128], ident[:, :])
                    return ins
                a = pe(emit, d, freed[4])
                h = act(lambda e: e.activation(HTH[i][:, :, :], ps, ACT.Copy), a, self.ht_free[i], *after)
                l = dve(lambda e: e.tensor_tensor(HTL[i][:, :, :], ps, HTH[i][:, :, :], ALU.subtract), h)
                free(4, 1, h, l)
                self.hm_free[i] = a
                return [h, l]

            def second(self, n, u, ht, *after):
                f, g = self.units[u]
                i = n % 2
                for k, part in enumerate(Wf2[f, g]):
                    wh, wl = W.pair(part)

                    def emit(e, k=k, wh=wh, wl=wl):
                        for h in range(2):
                            c = slice(512 * h, 512 * h + 512)
                            e.matmul(bank(5 + h), HTH[i][:, k, :], wh[:, c], start=k == 0, stop=False)
                            e.matmul(bank(5 + h), HTH[i][:, k, :], wl[:, c], start=False, stop=False)
                            ins = e.matmul(bank(5 + h), HTL[i][:, k, :], wh[:, c], start=False, stop=False)
                        return ins
                    s = pe(emit, W.ready(part), ht, [freed[5], freed[6]] if k == 0 else None)
                    W.release(part, s)
                    W.split()
                    if k == 0 and u % 2 == 0:
                        self.split_biases(1, u, *after)
                self.ht_free[i] = s

                def bias(e):
                    for h in range(2):
                        c = slice(512 * h, 512 * h + 512)
                        ins = e.matmul(bank(5 + h), LMT[n % 3][:, :], B2[:, c], start=False, stop=True)
                    return ins
                s = self.b_free[1] = self.lmt_free[n % 3] = pe(bias, self.b_ok[1])
                y = act(lambda e: e.activation(YO[i][:, :], bank(5, 2), ACT.Copy), s, self.yo_free[i], *after)
                free(5, 2, y)
                d = dma("gpsimd", sy[i], lambda e: e.indirect_dma_start(
                    out=yb[f], out_offset=bass.IndirectOffsetOnAxis(ap=OUTI[f][:, g:g + 1], axis=0), in_=YO[i][:, :], in_offset=None,
                    bounds_check=N - 1, oob_is_err=False), y, routed[f]["rows"])
                self.yo_free[i] = d
                return d

            def start(self, units, table, table_ok, late, *after):
                self.units, self.table, self.table_ok, self.got = units, table, table_ok, {}
                if self.n == 0:
                    self.table_ok = [table_ok, [fill(XR[i][:, :], 0.0, table_ok, *after) for i in range(2)]]
                self.fetch(0, *after)
                self.fetch(1, *after)
                for u in (0, 2):
                    self.biases("sync", 1, u, table_ok, *after)
                    self.biases("sync", 0, u, late, *after)

            def fetch(self, u, *after):
                f, g = self.units[u]
                self.got[u] = self.gather(self.n + u, f, g, self.table, [routed[f]["rows"], self.table_ok], *after)

            def run(self, gelu, within, between, *after):
                units, got, xt, lm, ht, stored = self.units, self.got, {}, {}, {}, {}
                n0, count = self.n, len(units)

                def mask(u):
                    f, g = units[u]
                    lm[u] = self.mask(n0 + u, f, g, routed[f]["leaves"], *after)

                def turn(u):
                    xt[u], lm[u] = self.turn(n0 + u, lm[u], got[u], *after)
                mask(0)
                turn(0)
                for u in range(count + 1):
                    if u + 1 < count:
                        mask(u + 1)
                    if u < count:
                        d = self.first(n0 + u, u, xt[u], lm[u], gelu, *after)
                    if u + 1 < count:
                        turn(u + 1)
                    within(u)
                    if u:
                        stored[units[u - 1]] = self.second(n0 + u - 1, u - 1, ht[u - 1], *after)
                    for n in range(u + 2 + (u > 0), min(u + 4, count)):
                        self.fetch(n, *after)
                    if u < count:
                        ht[u] = self.turn_h(n0 + u, d, *after)
                    b = u - u % 2 + 4
                    if b < count:
                        self.biases("scalar", u % 2, b, *after)
                    between(u, stored)
                self.n += count
                return stored

        M0 = K0
        RX = at("more_rows", [128, D], F32, M0)
        RT = at("more_cols", [128, 8, 128], F32, M0 + 4096)
        RW = at("more_weights", [128, 1024], F32, M0 + 8192)
        RB = at("more_b1", [128, 512], F32, M0 + 12288)
        RH = at("more_h", [128, 512], F32, M0 + 14336)
        RHT = at("more_ht", [128, 4, 128], F32, M0 + 16384)
        RS = at("more_slot", [PT, TT, 128], F16, M0 + 18432)
        RC = at("more_shift", [PT, TT], F32, M0 + 19712)
        RI = at("more_index", [128, 4], U32, M0 + 19744)
        RM = at("more_mask", [128, 32], F32, M0 + 19776)
        RV = at("more_values", [128, 8], F32, M0 + 19904)
        PLN = at("more_current", [128, 2], F32, M0 + 19936)
        chain, fetched, begun = [{f: q.sem(f"more_{n}_{f}") for f in FF} for n in ("step", "rows", "begun")]

        def round_steps(f, table, gelu):
            ps = bank(3)
            w1, w2, b1 = A[f"L0_ffn_{f}_w1"], A[f"L0_ffn_{f}_w2"], A[f"L0_ffn_{f}_b1"]
            steps = []

            def step(engine):
                return lambda emit: steps.append((engine, emit))

            @step("vector")
            def _(e, g):
                return e.tensor_scalar(RC[:, :], PLACE[f][:, :], PLN[0:PT, 0:1], None, op0=ALU.subtract)

            @step("vector")
            def _(e, g):
                for t in range(TT):
                    ins = e.tensor_scalar(RS[:, t, :], iota16[0:PT, 0:128], RC[:, t:t + 1], None, op0=ALU.is_equal)
                return ins

            @step("tensor")
            def _(e, g):
                for t in range(TT):
                    ins = e.matmul(ps[:, 0:4], RS[:, t, :], MV4[f][:, t, :], start=t == 0, stop=t == TT - 1)
                return ins

            @step("vector")
            def _(e, g):
                return e.tensor_copy(RV[:, 0:4], ps[:, 0:4])

            @step("vector")
            def _(e, g):
                e.tensor_copy(RI[:, 0:1], RV[:, 0:1])
                e.tensor_copy(RI[:, 2:3], RV[:, 3:4])
                e.tensor_scalar(RM[:, :], iota16[:, 0:32], RV[:, 1:2], None, op0=ALU.is_equal)
                return e.tensor_scalar(RV[:, 4:5], RV[:, 2:3], -4096.0, 4096.0, op0=ALU.mult, op1=ALU.add)

            @step("vector")
            def _(e, g):
                return e.tensor_tensor(RI[:, 1:2], RV[:, 4:5], RV[:, 0:1], ALU.add)

            @step("gpsimd")
            def _(e, g):
                return e.indirect_dma_start(out=RX[:, :], **rows_of(table, RI[:, 0:1]))

            def turn(src, dst, k0):
                @step("tensor")
                def _(e, g):
                    for k in range(4):
                        ins = e.transpose(ps[:, 128 * k:128 * k + 128], src[:, 128 * (k0 + k):128 * (k0 + k) + 128], ident[:, :])
                    return ins

                @step("scalar")
                def _(e, g):
                    return e.activation(dst[:, k0:k0 + 4, :], ps.rearrange("p (k c) -> p k c", k=4), ACT.Copy)

            turn(RX, RT, 0)
            turn(RX, RT, 4)
            for j in range(4):
                @step("sync")
                def _(e, g, j=j):
                    return e.dma_start(RW[:, :], w1[bass.ds(g, 1), :, 1024 * j:1024 * j + 1024].rearrange("o p c -> (o p) c"))

                @step("tensor")
                def _(e, g, j=j):
                    for k in range(2):
                        ins = e.matmul(ps, RT[:, 2 * j + k, :], RW[:, 512 * k:512 * k + 512], start=j == 0 and k == 0, stop=j == 3 and k == 1)
                    return ins

            @step("sync")
            def _(e, g):
                return e.dma_start(RB[:, :], b1[bass.ds(g, 1), :].rearrange("o c -> (o c)").partition_broadcast(128))

            @step("vector")
            def _(e, g):
                return e.tensor_tensor(RH[:, :], ps, RB[:, :], ALU.add)

            @step("scalar")
            def _(e, g):
                return e.activation(RH[:, :], RH[:, :], ACT.Gelu if gelu else ACT.Relu)

            @step("vector")
            def _(e, g):
                h = RH[:, :].rearrange("p (l w) -> p l w", w=16)
                return e.tensor_tensor(h, h, bc(RM[:, :], 16), ALU.mult)

            turn(RH, RHT, 0)
            for h in range(2):
                for k in range(4):
                    @step("sync")
                    def _(e, g, h=h, k=k):
                        c = 1024 * k + 512 * h
                        return e.dma_start(RW[:, 0:512], w2[bass.ds(g, 1), :, c:c + 512].rearrange("o p c -> (o p) c"))

                    @step("tensor")
                    def _(e, g, k=k):
                        return e.matmul(ps, RHT[:, k, :], RW[:, 0:512], start=k == 0, stop=k == 3)

                @step("scalar")
                def _(e, g, h=h):
                    return e.activation(RX[:, 512 * h:512 * h + 512], ps, ACT.Copy)

            @step("gpsimd")
            def _(e, g):
                return e.indirect_dma_start(out=RW[:, :], **rows_of(A[f"L0_ffn_{f}_b2"], RI[:, 2:3]))

            @step("vector")
            def _(e, g):
                return e.tensor_tensor(RX[:, :], RX[:, :], RW[:, :], ALU.add)

            @step("gpsimd")
            def _(e, g):
                return e.indirect_dma_start(out=yb[f], out_offset=bass.IndirectOffsetOnAxis(ap=RI[:, 1:2], axis=0), in_=RX[:, :], in_offset=None,
                                            bounds_check=N - 1, oob_is_err=False)

            @step("vector")
            def _(e, g):
                return e.tensor_scalar(PLN[:, 0:1], PLN[:, 0:1], 640.0, None, op0=ALU.add)

            @step("vector")
            def _(e, g):
                return e.tensor_scalar(PLN[:, 1:2], PLN[:, 0:1], 5120.0, -4992.0, op0=ALU.is_ge, op1=ALU.mult)

            @step("vector")
            def _(e, g):
                return e.tensor_tensor(PLN[:, 0:1], PLN[:, 0:1], PLN[:, 1:2], ALU.add)

            return steps

        def more_rounds(fs, table, gelu, *after):
            first = "kqvf".index(fs[0])
            ready = [routed[f]["all"] for f in fs]

            def rounds(e, engine, f, more):
                steps = round_steps(f, table, gelu)
                at_step = register(e, "at_step")
                e.reg_mov(at_step, 16)
                if engine == "vector":
                    e.memset(PLN[:, :], 128.0).then_inc(chain[f], 16)
                if engine == "gpsimd":
                    moved = register(e, "moved")
                    e.reg_mov(moved, 0)
                with e.Fori(0, more, 1):
                    with e.Fori(0, 8, 1) as g:
                        passed = 0
                        for n, (who, run) in enumerate(steps):
                            if who == engine:
                                e.reg_add(at_step, at_step, 16 * (n - passed))
                                passed = n
                                e.wait_ge(chain[f], at_step)
                                if engine == "gpsimd":
                                    e.sem_inc(begun[f], 1)
                                    e.reg_add(moved, moved, 16)
                                    run(e, g).then_inc(fetched[f], 16)
                                    e.wait_ge(fetched[f], moved)
                                    e.sem_inc(chain[f], 16)
                                else:
                                    run(e, g).then_inc(chain[f], 16)
                        e.reg_add(at_step, at_step, 16 * (len(steps) - passed))
                e.wait_ge(chain[f], at_step)
                e.sem_inc(begun[f], 1)

            def on(engine):
                def emit(e):
                    more = [register(e, f"more{i}") for i in range(len(fs))]
                    e.load(more, MORE[0:1, first:first + len(fs)])
                    for i, f in enumerate(fs):
                        with e.If_ne(more[i], 0):
                            rounds(e, engine, f, more[i])
                return emit
            for engine in q.ENGINES:
                q.add(engine, on(engine), flat([ready, freed[3], after] if engine == "vector" else ready))

        leaves = Leaves()
        asm_n = [0]
        qa_free = [None, None]

        def collect(f, t, stored, *after):
            i = asm_n[0] % 2
            asm_n[0] += 1
            ys = [stored[f, g] for g in range(8)]
            return i, dma("sync", sqa[i], lambda e: e.dma_start(QA[i][:, :], yb[f][t * PT:(t + 1) * PT, :]), ys, qa_free[i], *after)

        KTH = at("kt_high", [128, 8, NP], F32R, K0)
        KTL = at("kt_low", [128, 8, NP], F32R, K0 + 20096)
        QTH = at("qt_high", [128, 8, 126], F32R, K0 + 40192)
        QTL = at("qt_low", [128, 8, 126], F32R, K0 + 40192 + 4032)
        E = [at(f"weights{t}", [PT, NP], F32, LENT + 2528 * t if t < 4 else K0 + 48512) for t in range(TT)]
        smax = const("soft_max", [PT, 2], F32)
        ssum = const("soft_sum", [PT, TT, 2], F32)
        routed_all, stages_qv = [], []
        kt_ok, qt_ok, exp_ok, score_ok, held_k, held_q, stored_q = {}, {}, {}, {}, {}, {}, []

        def turn_tile(x, hi, lo, b, *after):
            ps = bank(b, 2).rearrange("p (k c) -> p k c", k=8)[:, :, 0:PT]

            def emit(e):
                for k in range(8):
                    ins = e.transpose(ps[:, k, :], x[:, 128 * k:128 * k + 128], ident[0:PT, 0:PT])
                return ins
            a = pe(emit, freed[b], freed[b + 1], *after)
            h = act(lambda e: e.activation(hi[:, :, 0:PT], ps, ACT.Copy), a, *after)
            l = dve(lambda e: e.tensor_tensor(lo[:, :, 0:PT], ps, hi[:, :, 0:PT], ALU.subtract), h)
            free(b, 2, h, l)
            return [h, l]

        def turn_q(t):
            i, c = held_q[t]
            qt_ok[t] = turn_tile(QA[i][:, :], QTH, QTL, 0, c, score_ok.get(t - 1), routed_all, W.lent(LEAF_Q))
            qa_free[i] = qt_ok[t]
            if t + 1 < TT:
                held_q[t + 1] = collect("q", t + 1, stored_q[0])

        def score_products(t, ks):
            def emit(e):
                for k in ks:
                    for n, (x, w) in enumerate(((QTH, KTH), (QTH, KTL), (QTL, KTH))):
                        for h in range(2):
                            ins = e.matmul(bank(2 + h)[0:PT, 0:NH], x[:, k, 0:PT], w[:, k, NH * h:NH * h + NH], start=k == 0 and n == 0, stop=k == 7 and n == 2)
                return ins
            score_ok[t] = pe(emit, qt_ok[t], k_ok, freed[2], freed[3])

        def numerators(t):
            s = score_ok[t]
            ps = bank(2, 2)[0:PT, :].rearrange("p (a c) -> p a c", a=2)[:, :, 0:NH]
            m = smax[:, t % 2:t % 2 + 1]
            a = dve(lambda e: e.tensor_reduce(m, ps, axis=AX.XY, op=ALU.max), s, exp_ok.get(t - 2))
            a = dve(lambda e: e.tensor_scalar(m, m, -1.0 / 32.0, None, op0=ALU.mult), a)
            x = [act(lambda e, h=h, w=w: e.activation(E[t][:, NH * h:NH * h + w], bank(2 + h)[0:PT, 0:w], ACT.Exp, bias=m, scale=1.0 / 32.0, accum_out=ssum[:, t, h:h + 1]),
                     a, W.lent(LAST), routed_all) for h, w in ((0, NH), (1, N - NH))]
            free(2, 2, x)
            exp_ok[t] = x

        thirds = [(t, ks) for t in range(TT - 1) for ks in (range(3), range(3, 6), range(6, 8))]

        def score_part(n):
            if 0 <= n < len(thirds):
                t, ks = thirds[n]
                score_products(t, ks)
                if ks[-1] == 7:
                    numerators(t)
                    turn_q(t + 1)

        def within_kqv(u):
            score_part(2 * u - 36)

        def between_kqv(u, stored):
            if u == 5:
                W.drop(LEAF_K)
            if u == 13:
                W.drop([*LAST, *LEAF_Q])
            W.paused = u == 23
            if u == 0:
                finish(stages)
                routed_all.append(routed["k"]["all"])
            if u < 2:
                leaves_qv(3 + u)
            if u == 1:
                stages_qv.append(route("qv", leaf["qv"], leaf_ok["qv"], 2, routed_all))
            if 1 <= u < 6:
                finish(stages_qv[0], 1 + (u == 4))
            if u == 5:
                routed_all.extend([routed["q"]["all"], routed["v"]["all"], leaf_ok["qv"]])
            if u == 8:
                more_rounds("kqv", xn1d, False, routed_all, W.lent(LEAF_K))
            t = u - 10
            if t == -1:
                held_k[0] = collect("k", 0, stored, logits_done, decided)
            if 0 <= t < TT:
                i, c = held_k[t]
                kt_ok[t] = transpose_tile(t, QA[i][:, :], KTH, KTL, 0, c, routed_all, W.lent(LEAF_K))
                qa_free[i] = kt_ok[t]
                if t + 1 < TT:
                    held_k[t + 1] = collect("k", t + 1, stored, logits_done, decided)
            if t == TT:
                kt = [kt_ok[i] for i in range(TT)]
                pad = [dve(lambda e, x=x: e.tensor_copy(x[:, :, N:NP], x[:, :, N - 1:N].to_broadcast([128, 8, NP - N])), kt) for x in (KTH, KTL)]
                k_ok.extend([kt, pad])
            if u == 16:
                stored_q.append(stored)
                held_q[0] = collect("q", 0, stored)
            if u == 17:
                turn_q(0)
            score_part(2 * u - 35)

        k_ok = []
        leaves.start(units, xn1d, xn1_all, logits_done, xt1_all)
        W.ahead = 4
        W.pooled = (3,)
        W.split(8)
        leaf_stored = leaves.run(False, within_kqv, between_kqv, logits_done, xt1_all, xn1_all)

        VH = at("v_high", [PT, TT, D], F32R, R0)
        VL = at("v_low", [PT, TT, D], F32R, R0 + 20480)
        YTH = [at(f"yt_high{i}", [128, 8, 126], F32R, o) for i, o in enumerate((R0 + 40960, K0 + 2560))]
        YTL = [at(f"yt_low{i}", [128, 8, 126], F32R, o) for i, o in enumerate((R0 + 44992, K0 + 10752))]
        ETH = [at(f"et_high{i}", [PT, TT, 126], F32R, R0 + 49152 + 5056 * i) for i in range(2)]
        ETL = [at(f"et_low{i}", [PT, TT, 126], F32R, R0 + 49152 + 5056 * i + 2528) for i in range(2)]
        VR = [at(f"v_raw{i}", [PT, D], F32, R0 + 40960 + 4096 * i) for i in range(2)]
        SF16 = at("right_f", [PT, TT, 1, 256], F16, K0)
        NBF = at("node_b_f", [PT, 256], F32, K0 + 14784)
        X2 = at("x2", [PT, TT, D], F32, K0 + 24576)
        yd = scratch("y_rows", [N, D])
        sinv = const("soft_inv", [PT, TT], F32)
        x2l = [q.sem(f"x2l_sem{t}") for t in range(TT)]
        x2d = scratch("x2_rows", [N, D])

        leaf_done = [leaf_stored[f, g] for f in "kqv" for g in range(8)]
        v_ok, et_ok, att_ok, y_done, y_stored, turned, f_leaf = {}, {}, {}, {}, {}, {}, []
        yt_free, base_ok = {}, {}

        def load_v(t):
            if t < 2:
                i, c = collect("v", t, leaf_stored)
                return QA[i], c, i
            dst, free_ok = (VR[t - 2][:, :], None) if t < 4 else (X2[:, t, :], scored)
            rs = slice(t * PT, (t + 1) * PT)
            return dst, dma("sync", x2l[t], lambda e: e.dma_start(dst, yb["v"][rs, :]), leaf_done, free_ok), None

        def take_v(t):
            x, c, i = v_loads[t]
            h = act(lambda e: e.activation(VH[:, t, :], x[:, :], ACT.Copy), c, leaf_done)
            l = dve(lambda e: e.tensor_tensor(VL[:, t, :], x[:, :], VH[:, t, :], ALU.subtract), h)
            v_ok[t] = [h, l]
            if i is not None:
                qa_free[i] = v_ok[t]

        def load_xn(t, *after):
            xn_back[t] = dma("sync", x2l[t], lambda e: e.dma_start(X2[:, t, :], xn1d[t * PT:(t + 1) * PT, :]), scored, *after)

        def turn_weights(t):
            b = 0 if t == 0 else 4
            ps = bank(b, 2)[0:PT, :].rearrange("p (k c) -> p k c", c=128)[:, 0:TT, 0:PT]

            def emit(e):
                for k in range(TT):
                    ins = e.transpose(ps[:, k, :], E[t][:, k * PT:(k + 1) * PT], ident[0:PT, 0:PT])
                return ins
            a = pe(emit, exp_ok[t], freed[b], freed[b + 1])
            h = act(lambda e: e.activation(ETH[t % 2][:, :, 0:PT], ps, ACT.Copy), a, leaf_done, att_ok.get(t - 2))
            l = dve(lambda e: e.tensor_tensor(ETL[t % 2][:, :, 0:PT], ps, ETH[t % 2][:, :, 0:PT], ALU.subtract), h)
            free(b, 2, h, l)
            et_ok[t] = [h, l]
            return a

        def attend(t):
            xh, xl = ETH[t % 2], ETL[t % 2]
            rs = slice(t * PT, (t + 1) * PT)
            for k in range(TT):
                def emit(e, k=k):
                    for n, (x, v) in enumerate(((xh, VH), (xh, VL), (xl, VH))):
                        for h in range(2):
                            ins = e.matmul(bank(6 + h)[0:PT, :], x[:, k, 0:PT], v[:, k, 512 * h:512 * h + 512], start=k == 0 and n == 0, stop=k == TT - 1 and n == 2)
                    return ins
                s = pe(emit, et_ok[t], v_ok[k], freed[6], freed[7])
            att_ok[t] = s
            y = y_done[t] = dve(lambda e: e.scalar_tensor_tensor(X2[:, t, :], bank(6, 2)[0:PT, :], sinv[:, t:t + 1], X2[:, t, :], op0=ALU.mult, op1=ALU.add), s, sinv_ok, xn_back[t])
            free(6, 2, y)
            y_stored[t] = dma("sync", x2l[t], lambda e: e.dma_start(yd[rs, :], X2[:, t, :]), y)

        def turn_y(t):
            turned[t] = turn_tile(X2[:, t, :], YTH[t % 2], YTL[t % 2], 0, y_done[t], leaf_done, scored, yt_free.get(t - 2))

        def decide_f(t):
            b = 2 + t % 2
            s = node_logits("f", t, bank(b)[0:PT, 0:256], YTH[t % 2], YTL[t % 2], slice(0, PT), turned[t], freed[b])
            yt_free[t] = s
            W.split(2)
            g = goes_right(SF16[:, t, 0, :], bank(b)[0:PT, 0:256], NBF[:, :], s, nbf_ok)
            free(b, 1, g)
            f_leaf.append(leaf_numbers(SF16[:, t, :, :], 1, leaf["f"][:, t, :], g, scored))

        def add_x1(t):
            i = asm_n[0] % 2
            asm_n[0] += 1
            l = dma("sync", sqa[i], lambda e: e.dma_start(QA[i][:, :], x1d[t * PT:(t + 1) * PT, :]), x1_stored[t], qa_free[i])
            base_ok[t] = qa_free[i] = pool(lambda e: e.tensor_tensor(X2[:, t, :], X2[:, t, :], QA[i][:, :], ALU.add), l, turned[t], y_stored[t])

        xn_back = {}
        v_loads = [load_v(t) for t in range(4)]
        turn_weights(0)
        for t in range(4):
            take_v(t)
        score_products(4, range(8))
        numerators(4)
        turn_weights(1)
        scored = [score_ok[t] for t in range(TT)]
        nbf_ok = dma("scalar", nbs, lambda e: e.dma_start(NBF[:, :], A["L0_ffn_nb"][768:1024].partition_broadcast(PT)), scored)
        si = dve(lambda e: e.tensor_tensor(sinv[:, :], ssum[:, :, 0], ssum[:, :, 1], ALU.add), [exp_ok[t] for t in range(TT)])
        sinv_ok = dve(lambda e: e.reciprocal(sinv[:, :], sinv[:, :]), si)
        v_loads.append(load_v(4))
        take_v(4)
        for t in range(TT):
            load_xn(t, v_ok[t])
        W.resume()
        W.grow(AFTER_K, scored)
        for t in range(TT):
            attend(t)
            if t + 2 < TT:
                e_last = turn_weights(t + 2)
            if t:
                turn_y(t - 1)
            if t > 1:
                decide_f(t - 2)
                add_x1(t - 2)
        W.grow(LAST, e_last)
        turn_y(4)
        decide_f(3)
        decide_f(4)
        finish(route("f", leaf["f"], f_leaf, 4, scored))
        W.grow(ROUTED, f_leaf, list(yt_free.values()), routed["f"]["all"])
        attended = [list(yt_free.values()), list(y_done.values()), list(turned.values()), list(att_ok.values()), list(et_ok.values())]
        leaves.start([("f", g) for g in range(8)], yd, list(y_stored.values()), None, attended)
        add_x1(3)
        add_x1(4)

        f_routed = [routed["f"]["all"], f_leaf, attended]
        W.ahead, W.pooled = 4, (3,)

        def pause_loads(u, stored):
            W.paused = u == 7
            if u == 2:
                W.drop([*AFTER_K, *ROUTED])

        f_stored = leaves.run(True, lambda u: None, pause_loads, attended)
        more_rounds("f", yd, True, f_routed, W.lent([*AFTER_K, *ROUTED]))
        W.ahead, W.pooled = 6, ()
        x2_done, x2_stored, x2_normal, xt2_ok = {}, {}, {}, {}
        f_done = [f_stored["f", g] for g in range(8)]
        XQ = [at(f"x2_tile{t}", [PT, D], F32, R0 + o) for t, o in enumerate((59392, 63488, 51200, 55296, 47104))]
        f_back = [dma("sync", x2l[t], lambda e, t=t: e.dma_start(XQ[t][:, :], yb["f"][t * PT:(t + 1) * PT, :]), f_done, list(base_ok.values())) for t in range(TT)]
        for t in range(TT):
            add = dve if t == 0 else pool
            x2_done[t] = add(lambda e, t=t: e.tensor_tensor(X2[:, t, :], X2[:, t, :], XQ[t][:, :], ALU.add), base_ok[t], f_back[t])
            x2_stored[t] = dma("sync", x2l[t], lambda e, t=t: e.dma_start(x2d[t * PT:(t + 1) * PT, :], X2[:, t, :]), x2_done[t])
        W.resume()
        shift = lnx[:, 0, :]

        def shifts(a, b, *after):
            r = deviations(a, b, *after)
            return dve(lambda e: e.scalar_tensor_tensor(shift[:, a:b], lnmv[:, a:b, 0], -1.0, rstd[:, a:b], op0=ALU.mult, op1=ALU.mult), r)

        def normal_x2(a, b, *after):
            r = shifts(a, b, *after)
            for t in range(a, b):
                x2_normal[t] = act(lambda e, t=t: e.activation(XQ[t][:, :], X2[:, t, :], ACT.Identity, bias=shift[:, t:t + 1], scale=rstd[:, t:t + 1]), r, x2_done[t])

        def turn_x2(t):
            xt2_ok[t] = transpose_tile(t, XQ[t][:, :], XTH, XTL, 4 + 2 * (t % 2), x2_normal[t], f_done)

        GH = at("gnn_high", [PT, TT, 512], F32R, R0 + 69632)
        GL = at("gnn_low", [PT, TT, 512], F32R, R0 + 69632 + 10240)
        AT = at("adjacency_t", [PT, TT, NP], F32R, R0 + 92160)
        GB = at("bias_gnn", [PT, 512], F32, R0 + 114976)
        BO1 = at("bias_o1", [PT, D], F32, R0 + 114528)
        SG = [at(f"gnn_row{i}", [PT, 512], F32, o) for i, o in enumerate((R0 + 67584, R0 + 90112, R0 + 104736, R0 + 65536))]
        acc1 = scratch("x2_mixed", [N, D])
        atsem = q.sem("at_sem")
        sgs = [q.sem(f"sg_sem{i}") for i in range(4)]
        sgo = [q.sem(f"sgo_sem{i}") for i in range(4)]
        BK1 = at("bias_k1", [PT, D], F32, R0 + 106784)
        BV1 = at("bias_v1", [PT, D], F32, R0 + 97472)
        gb_ok = [bias_rows(GB[:, :], A["L1_gnn_b"][0:512], attended)]
        pads2 = [fill(x[:, :, N:NP], 0.0, f_done, attended) for x in (XTH, XTL)]
        g_ok, acc1_stored = {}, []
        g_used = None
        k1_done = []

        def gnn_rows(h, t, used):
            b = (5 * h + t) % 4
            sl = slice(512 * h, 512 * h + 512)
            s = rows_tile(t, Wgnn[h], XTH, XTL, b, xt2_ok[t])
            W.split()
            w = SG[t % 4]
            a = dve(lambda e: e.tensor_tensor(w[:, :], bank(b)[0:PT, :], GB[:, :], ALU.add), s, gb_ok[h], sg_free[t % 4])
            gb_used[:] = [a]
            free(b, 1, a)
            x = act(lambda e: e.activation(GH[:, t, :], w[:, :], ACT.Copy, scale=dis[:, t:t + 1]), a, dis_ok, used)
            y = dve(lambda e: e.scalar_tensor_tensor(GL[:, t, :], w[:, :], dis[:, t:t + 1], GH[:, t, :], op0=ALU.mult, op1=ALU.subtract), x, used)
            g_ok[t] = [x, y]
            sg_free[t % 4] = [x, y]

        def keys1(h):
            for t in range(TT):
                b = 4 + t % 4
                s = rows_tile(t, Wk1[h], XTH, XTL, b, xt2_ok[t])
                W.split()
                sl = slice(512 * h, 512 * h + 512)
                k1_done.append(keys_tile(KN[:, t, sl], b, t % 2, BK1[:, sl], s, bk1, x2_free))

        def gnn_sum(h):
            last = []
            sl = slice(512 * h, 512 * h + 512)

            def products(e, j, dt):
                for m in range(TT):
                    for n, y in enumerate((GH, GL)):
                        a, w = AT[:, m, cols(j)], y[:, m, :]
                        if dt == F32:
                            a, w = a.bitcast(F32), w.bitcast(F32)
                        ins = e.matmul(bank(j % 4)[0:PT, :], a, w, start=m == 0 and n == 0, stop=m == TT - 1 and n == 1)
                return ins
            for j in range(TT):
                def one(j=j, b=j % 4, w=SG[j % 4]):
                    rs = slice(j * PT, (j + 1) * PT)
                    l = dma("scalar", sgs[j % 4], lambda e: e.dma_start(w[:, :], x2d[rs, sl]), sg_free[j % 4], list(x2_stored.values()))

                    def emit(e):
                        with e.If_ne(manyr[0], 0):
                            products(e, j, F32).then_inc(s.sem, 1)
                        with e.Else():
                            products(e, j, F32R).then_inc(s.sem, 1)
                        return None
                    s = pe(emit, [g_ok[m] for m in range(TT)], at_ok, freed[b])
                    s.own = True
                    last.append(s)
                    u = dve(lambda e: e.scalar_tensor_tensor(w[:, :], bank(b)[0:PT, :], dis[:, j:j + 1], w[:, :], op0=ALU.mult, op1=ALU.add), s, l)
                    free(b, 1, u)
                    d = dma("gpsimd", sgo[j % 4], lambda e: e.dma_start(acc1[rs, sl], w[:, :]), u)
                    sg_free[j % 4] = d
                    acc1_stored.append(d)
                one()
            return last

        gb_used = []
        sg_free = [attended] * 4
        normal_x2(0, 1, moments(0, 1, X2, x2_done))
        mom = moments(1, 3, X2, x2_done)
        turn_x2(0)
        normal_x2(1, 3, mom)
        mom = moments(3, 5, X2, x2_done)
        gnn_rows(0, 0, None)
        turn_x2(1)
        turn_x2(2)
        normal_x2(3, 5, mom)
        sg_free[2] = [list(x2_normal.values()), list(x2_stored.values())]
        sg_free[3] = [xt2_ok[1], attended]
        gnn_rows(0, 1, None)
        turn_x2(3)
        turn_x2(4)
        for t in range(2, TT):
            gnn_rows(0, t, None)
        x2_free = [list(d.values()) for d in (x2_normal, x2_stored, xt2_ok)]
        at_ok = dma("sync", atsem, lambda e: e.dma_start(AT[:, :, 0:N].bitcast(F32), adjt[0:N, :].rearrange("(j p) s -> p j s", p=PT)),
                    x2_free, at_stored)
        bk1 = bias_rows(BK1[:, :], "L1_mix_bk", x2_free)
        tmp_free[:] = [x2_free, x2_free]
        for h in range(2):
            if h:
                for t in range(TT):
                    gnn_rows(1, t, g_used)
            if h == 0:
                gb_ok.append(bias_rows(GB[:, :], A["L1_gnn_b"][512:1024], gb_used))
                keys1(0)
            g_used = gnn_sum(h)
        bv1 = bias_rows(BV1[:, :], "L1_mix_bv", g_used)
        before1 = [g_used, acc1_stored, x2_free]
        ones_v1 = dve(lambda e: e.memset(VN[:, :, :, 128:130], 1.0), before1)
        keys1(1)
        v1_done = []
        for h in range(2):
            for t in range(TT):
                b = (5 * h + t) % 4
                s = rows_tile(t, Wv1[h], XTH, XTL, b, xt2_ok[t])
                W.split()
                v1_done.append(values_tile(h, t, b, BV1[:, 512 * h:512 * h + 512], s, bv1, ones_v1))

        X3 = at("x3_rows", [PT, TT, D], F32, R0 + 81472)
        X4 = [at(f"x4_tile{i}", [PT, D], F32, R0 + (101952 + 4096 * i if i < 3 else 40192)) for i in (0, 1, 2, 0, 3)]
        x3d, x4d = scratch("x3_rows_kept", [N, D]), scratch("x4_rows", [N, D])
        x3s = [q.sem(f"x3_sem{t}") for t in range(TT)]
        x3_half, x3_base, x3_stored, x4_normal, x4_stored, xt4_ok = {}, {}, {}, {}, {}, {}
        bo1_ok = bias_rows(BO1[:, :], "L1_mix_bo", k1_done, acc1_stored)

        def mixed_base1():
            for t in range(TT):
                l = dma("sync", x3s[t], lambda e, t=t: e.dma_start(X3[:, t, :], acc1[t * PT:(t + 1) * PT, :]), heads_done["L1_mix"], acc1_stored)
                x3_base[t] = pool(lambda e, t=t: e.tensor_tensor(X3[:, t, :], X3[:, t, :], BO1[:, :], ALU.add), l, bo1_ok)

        def fourth(a, b):
            x = {t: [x3_half[t, 0], x3_half[t, 1]] for t in range(a, b)}
            for t in range(a, b):
                x3_stored[t] = dma("sync", x3s[t], lambda e, t=t: e.dma_start(x3d[t * PT:(t + 1) * PT, :], X3[:, t, :]), x[t])
            r = ln_stats(a, b, X3, x)
            r = dve(lambda e: e.scalar_tensor_tensor(shift[:, a:b], lnmv[:, a:b, 0], -1.0, rstd[:, a:b], op0=ALU.mult, op1=ALU.mult), r)
            for t in range(a, b):
                x4_normal[t] = act(lambda e, t=t: e.activation(X4[t][:, :], X3[:, t, :], ACT.Identity, bias=shift[:, t:t + 1], scale=rstd[:, t:t + 1]),
                                   r, [xt4_ok[0], x4_stored[0]] if t == 3 else None, x[t], heads_done["L1_mix"], ao1_ok)
                x4_stored[t] = dma("sync", x3s[t], lambda e, t=t: e.dma_start(x4d[t * PT:(t + 1) * PT, :], X4[t][:, :]), x4_normal[t])

        def turn_fourth(t):
            xt4_ok[t] = transpose_tile(t, X4[t][:, :], XTH, XTL, 4 + 2 * (t % 2), x4_normal[t])

        ao1_ok = []

        def add_mixed1(h, t, b, s):
            sl = slice(512 * h, 512 * h + 512)
            if not x3_base:
                mixed_base1()
            if (h, t) == (1, 4):
                turn_fourth(1)
                turn_fourth(2)
            d = dve(lambda e: e.tensor_tensor(X3[:, t, sl], X3[:, t, sl], bank(b)[0:PT, :], ALU.add), x3_base[t], s)
            free(b, 1, d)
            x3_half[t, h] = d
            if h:
                if t == 0:
                    ao1_ok.append(s)
                if t == 2:
                    turn_fourth(0)
                if t % 2 == 0:
                    fourth(max(t - 1, 0), t + 1)

        mixer("L1_mix", XTH, XTL, [list(xt2_ok.values()), pads2], P1 + 20480, k1_done, [v1_done, ones_v1], [before1, k1_done, v1_done], ALU.add, add_mixed1)
        def keep_at(name, shape, dt, offset):
            return at(name, shape, dt, R0 + offset)

        SHTH, SHTL = [keep_at(n, [128, 4, NP], F32R, o) for n, o in (("sh_high", 40192), ("sh_low", 50240))]
        XMH, XML = [keep_at(n, [128, 8, 128], F32R, o) for n, o in (("xm_high", 60288), ("xm_low", 64384))]
        XMR = keep_at("xm_rows", [128, D], F32, 68480)
        SB1, SB2, SLG, SLB = [keep_at(f"shared_row{i}", [PT, 512], F32, o) for i, o in enumerate((114528, 116576, 76672, 78720))]
        WGR, WGH, WGL = keep_at("gates", [128, 80], F32, 80768), keep_at("gates_high", [128, 8, 10], F32R, 81088), None
        WGL = keep_at("gates_low", [128, 8, 10], F32R, 80768)
        ELG, ELB = [keep_at(f"expert_row{i}", [128, 512], F32, 72576 + 2048 * i) for i in range(2)]
        S1 = [keep_at(f"shared_1{t}", [PT, 512], F32, 81472 + 4096 * t) for t in range(TT)]
        S2 = [keep_at(f"shared_2{i}", [PT, 512], F32, 83520 + 4096 * i) for i in range(2)]
        X3L = [keep_at(f"x3_back{i}", [PT, D], F32, 81472 + 4096 * i) for i in range(2)]
        EBR = keep_at("expert_b_raw", [8, 2, 512], F32, 104000)
        EB = [keep_at(f"expert_b_parts{j}", [40, 512], F32R, 91712 + 4096 * j) for j in range(2)]
        ONE8 = keep_at("expert_row_of_ones", [40, 8, 128], F32R, 99904)
        H1 = [keep_at(f"expert_1{i}", [128, 512], F32, 108096 + 2048 * i) for i in range(2)]
        ZTH, ZTL = [keep_at(n, [128, 4, 128], F32R, o) for n, o in (("zt_high", 114240), ("zt_low", 116288))]
        OHM = keep_at("sel_onehot", [128, 640], F32R, 0)
        EMH, EML = [keep_at(n, [128, D], F32R, o) for n, o in (("em_high", 2560), ("em_low", 6656))]
        ER = keep_at("eb3_rows", [128, D], F32, 10752)
        SB3 = keep_at("shared_b3", [PT, D], F32, 14848)
        SO = keep_at("shared_out", [PT, TT, D], F32, 18944)
        MGB = const("gate_b", [128, 20], F32)
        sc = const("scores", [128, 10], F32)
        se = const("scores_tmp", [128, 24], F32)
        ohe = const("expert_onehot", [128, 8], F32)
        swo = const("weight_one", [128, 2], F32)
        expert = const("expert_index", [128, 1], U32)
        scl = const("token_scale", [PT, TT], F32)
        est = const("expert_stats", [128, 2, 16], F32)

        x3_all = [x3_half[t, h] for t in range(TT) for h in range(2)]
        mgb_ok = dma("sync", q.sem("mgb_sem"), lambda e: e.dma_start(MGB[:, :], A["L1_ffn_gate_b"].partition_broadcast(128)))
        wgl = dma("sync", q.sem("wg_sem"), lambda e: e.dma_start(WGR[:, :], A["L1_ffn_gates"]), heads_done["L1_mix"])
        srow = [bias_rows(x[:, :], f"L1_ffn_{n}", list(x3_base.values())) for x, n in ((SB1, "sb1"), (SB2, "sb2"))]

        W.pooled = (1, 3)

        def shared_1(t):
            b = t % 4
            s = rows_tile(t, Ws1, XTH, XTL, b, [xt4_ok[t]])
            W.split(4 if t == TT - 1 else 1)
            a = dve(lambda e: e.tensor_tensor(S1[t][:, :], bank(b)[0:PT, :], SB1[:, :], ALU.add), s, srow[0], x3_stored[t], x4_normal[t])
            free(b, 1, a)
            return act(lambda e: e.activation(S1[t][:, :], S1[t][:, :], ACT.Silu), a)

        def norm_of(x, st, p, *after):
            a = dve(lambda e: e.bn_stats(st[0:p, 0:6], x), *after)
            b = dve(lambda e: e.bn_aggr(st[0:p, 12:14], st[0:p, 0:6]), a)
            c = dve(lambda e: e.tensor_scalar(st[0:p, 14:15], st[0:p, 13:14], EPS, None, op0=ALU.add), b)
            return rsqrt(st[0:p, 14:15], st[0:p, 15:16], st[0:p, 11:12], st[0:p, 10:11], c)

        s2_free, s2_out, sh_ok = [None, None], [], []

        def shared_2(t, one):
            b, i = (t + 1) % 4, t % 2
            s = rows_tile(t, Ws2, XTH, XTL, b, [xt4_ok[t]])
            W.split(4 if t == TT - 1 else 1)
            u = S1[t][:, :]
            a = dve(lambda e: e.tensor_tensor(S2[i][:, :], bank(b)[0:PT, :], SB2[:, :], ALU.add), s, srow[1], s2_free[i])
            free(b, 1, a)
            s2_out.append(a)
            m = dve(lambda e: e.tensor_tensor(u, u, S2[i][:, :], ALU.mult), a, one)
            s2_free[i] = m
            r = norm_of(u, est[:, i, :], PT, m, sh_ok[t - 2] if t > 1 else None)
            n = dve(lambda e: e.tensor_scalar(u, u, est[0:PT, i, 12:13], est[0:PT, i, 15:16], op0=ALU.subtract, op1=ALU.mult), r)
            g = pool(lambda e: e.tensor_tensor(u, u, SLG[:, :], ALU.mult), n, srow[2])
            sh_ok.append(pool(lambda e: e.tensor_tensor(u, u, SLB[:, :], ALU.add), g, srow[3]))
            return s

        def expert_biases():
            ebs = q.sem("eb_sem")
            for j in range(2):
                ebl = dma("sync", ebs, lambda e, j=j: e.dma_start(EBR[:, j, :], A[f"L1_ffn_eb{j + 1}"]), x4_free)
            zero = [fill(EB[j][:, :], 0.0, x4_free) for j in range(2)]
            high = [act(lambda e, j=j: e.activation(EB[j][0:8, :], EBR[:, j, :], ACT.Copy), ebl, zero[j]) for j in range(2)]
            low = [dve(lambda e, j=j: e.tensor_tensor(EB[j][32:40, :], EBR[:, j, :], EB[j][0:8, :], ALU.subtract), high[j], zero[j]) for j in range(2)]
            ones = dve(lambda e: e.tensor_tensor(ONE8[:, :, :], ident[0:40, 0:8].unsqueeze(2).to_broadcast([40, 8, 128]),
                                                 ident[0:40, 32:40].unsqueeze(2).to_broadcast([40, 8, 128]), ALU.add), x4_free)
            return [high, low, ones]

        def select():
            ps = bank(4, 2).rearrange("p (k c) -> p k c", k=8)

            def emit(e):
                for k in range(8):
                    ins = e.transpose(ps[:, k, :], XMR[:, 128 * k:128 * k + 128], ident[:, :])
                return ins
            a = pe(emit, got_m, freed[4], freed[5])
            h = act(lambda e: e.activation(XMH[:, :, :], ps, ACT.Copy), a, x3_all)
            l = dve(lambda e: e.tensor_tensor(XML[:, :, :], ps, XMH[:, :, :], ALU.subtract), h)
            free(4, 2, h, l)
            return [h, l]

        def scores_of(xm):
            def emit(e):
                for k in range(8):
                    for n, (x, w) in enumerate(((XMH, WGH), (XMH, WGL), (XML, WGH))):
                        ins = e.matmul(bank(4)[:, 0:10], x[:, k, :], w[:, k, :], start=k == 0 and n == 0, stop=k == 7 and n == 2)
                return ins
            s = pe(emit, xm, wg_ok, freed[4])
            a = dve(lambda e: e.tensor_tensor(sc[:, :], bank(4)[:, 0:10], MGB[:, 0:10], ALU.add), s, mgb_ok)
            free(4, 1, a)
            a = act(lambda e: e.activation(sc[:, :], sc[:, :], ACT.Sigmoid), a)
            b = dve(lambda e: e.tensor_tensor(se[:, 0:8], sc[:, 1:9], MGB[:, 10:18], ALU.add), a)
            c = dve(lambda e: e.tensor_reduce(se[:, 8:9], se[:, 0:8], axis=AX.X, op=ALU.max), b)
            c = dve(lambda e: e.scalar_tensor_tensor(se[:, 0:8], se[:, 0:8], se[:, 8:9], rev8[:, :], op0=ALU.is_ge, op1=ALU.mult), c, rev_ok)
            c = dve(lambda e: e.tensor_reduce(se[:, 9:10], se[:, 0:8], axis=AX.X, op=ALU.max), c)
            hot = dve(lambda e: e.tensor_scalar(ohe[:, :], rev8[:, :], se[:, 9:10], None, op0=ALU.is_equal), c)
            index = dve(lambda e: e.tensor_scalar(expert[:, :], se[:, 9:10], -1.0, 8.0, op0=ALU.mult, op1=ALU.add), c)
            d = dve(lambda e: e.tensor_tensor(se[:, 12:20], ohe[:, :], sc[:, 1:9], ALU.mult), hot)
            d = dve(lambda e: e.tensor_reduce(se[:, 21:22], se[:, 12:20], axis=AX.X, op=ALU.add), d)
            d = dve(lambda e: e.tensor_copy(se[:, 20:21], sc[:, 0:1]), d)
            f = dve(lambda e: e.tensor_reduce(se[:, 10:11], se[:, 20:22], axis=AX.X, op=ALU.max), d)
            f = dve(lambda e: e.tensor_scalar(se[:, 20:22], se[:, 20:22], se[:, 10:11], None, op0=ALU.subtract), f)
            f = act(lambda e: e.activation(se[:, 20:22], se[:, 20:22], ACT.Exp), f)
            g = dve(lambda e: e.tensor_reduce(se[:, 11:12], se[:, 20:22], axis=AX.X, op=ALU.add), f)
            g = dve(lambda e: e.reciprocal(se[:, 11:12], se[:, 11:12]), g)
            w = dve(lambda e: e.tensor_scalar(se[:, 20:22], se[:, 20:22], se[:, 11:12], None, op0=ALU.mult), g)
            return hot, index, w

        one = []
        for t in range(TT):
            one.append(shared_1(t))
            if t in (1, 2):
                turn_fourth(t + 2)
        x3_stored, x4_stored, x4_normal, xt4_ok = [[d[t] for t in range(TT)] for d in (x3_stored, x4_stored, x4_normal, xt4_ok)]
        x4_free = [x3_stored, x4_stored, x4_normal, xt4_ok]
        srow += [bias_rows(x[:, :], f"L1_ffn_{n}", x3_all) for x, n in ((SLG, "s_ln_g"), (SLB, "s_ln_b"))]
        erow = [bias_rows(x[:, :], f"L1_ffn_sel_ln_{n}", x3_all) for x, n in ((ELG, "g"), (ELB, "b"))]
        got_m = dma("gpsimd", q.sem("xm_sem"), lambda e: e.indirect_dma_start(out=XMR[:, :], **rows_of(x4d, tokm[:, 0:1])), x4_stored, x3_all, tokm_ok)
        wgh = act(lambda e: e.activation(WGH[:, :, :].rearrange("p a b -> p (a b)"), WGR[:, :], ACT.Copy), wgl)
        wg_ok = [wgh, dve(lambda e: e.tensor_tensor(WGL[:, :, :].rearrange("p a b -> p (a b)"), WGR[:, :], WGH[:, :, :].rearrange("p a b -> p (a b)"), ALU.subtract), wgh)]
        two = []
        for t in range(TT):
            two.append(shared_2(t, one[t]))
            if t == 1:
                eb_ok = expert_biases()
            if t == 2:
                xm_ok = select()
        xt_dead = two
        hot_ok, index_ok, weight_ok = scores_of(xm_ok)
        er_ok = dma("gpsimd", q.sem("er_sem"), lambda e: e.indirect_dma_start(out=ER[:, :], **rows_of(A["L1_ffn_eb3"], expert[:, 0:1])), index_ok, xt_dead)
        sb3_ok = bias_rows(SB3[:, :], "L1_ffn_sb3", xt_dead)


        def token_columns():
            return [dve(lambda e: e.tensor_scalar(OHM[:, :], iota16[:, :], sel(6), sel(7), op0=ALU.is_equal, op1=ALU.mult), kept_ok, xt_dead),
                    dve(lambda e: e.tensor_copy(swo[:, 0:1], se[:, 20:21]), weight_ok),
                    dve(lambda e: e.memset(swo[:, 1:2], 1.0))]

        def token_scale():
            def emit(e):
                for t in range(TT):
                    ins = e.matmul(bank(5)[0:PT, 2 * t:2 * t + 2], OHM[:, cols(t)].bitcast(F32), swo[:, :], start=True, stop=True)
                return ins
            s = pe(emit, columns_ok, freed[5])
            ps = bank(5)[0:PT, 0:10].rearrange("p (t c) -> p t c", c=2)
            a = dve(lambda e: e.tensor_scalar(scl[:, :], ps[:, :, 1], -1.0, 1.0, op0=ALU.mult, op1=ALU.add), s)
            b = dve(lambda e: e.tensor_tensor(scl[:, :], scl[:, :], ps[:, :, 0], ALU.add), a)
            free(5, 1, a, b)
            return b

        h1_free, zt_free = [x4_free, x4_free], [s2_out]
        est_free = [sh_ok[4], sh_ok[4]]
        every = slice(0, 128)

        def expert_rows(j, x):
            b = 2 * j + x % 2

            pe(lambda e: e.matmul(bank(b), ONE8[:, x, :], EB[j][:, :], start=True, stop=False), eb_ok, freed[b])
            for k, part in enumerate(We[j][x]):
                s = rows(bank(b), XMH, XML, every, part, (2 * k, 2 * k + 1), False, k == 3, xm_ok)
                W.release(part, s)
                W.split()
            return s

        def gate(x):
            i = x % 2
            a = act(lambda e: e.activation(H1[i][:, :], bank(i), ACT.Silu), expert_rows(0, x), h1_free[i])
            free(i, 1, a)
            return a

        def hidden(x, g):
            i = x % 2
            u = H1[i][:, :]
            m = dve(lambda e: e.tensor_tensor(u, u, bank(2 + i), ALU.mult), expert_rows(1, x), g)
            free(2 + i, 1, m)
            st = est[:, i, :]
            r = norm_of(u, st, 128, m, est_free[i])
            r = dve(lambda e: e.tensor_tensor(st[:, 15:16], st[:, 15:16], ohe[:, x:x + 1], ALU.mult), r, hot_ok)
            n = dve(lambda e: e.tensor_scalar(u, u, st[:, 12:13], st[:, 15:16], op0=ALU.subtract, op1=ALU.mult), r)
            est_free[i] = n
            n = dve(lambda e: e.tensor_tensor(u, u, ELG[:, :], ALU.mult), n, erow[0])
            return dve(lambda e: e.scalar_tensor_tensor(u, ELB[:, :], ohe[:, x:x + 1], u, op0=ALU.mult, op1=ALU.add), n, erow[1])

        def turn_z(x, z):
            ps = bank(4).rearrange("p (k c) -> p k c", k=4)

            def emit(e):
                for k in range(4):
                    ins = e.transpose(ps[:, k, :], H1[x % 2][:, 128 * k:128 * k + 128], ident[:, :])
                return ins
            a = pe(emit, z, freed[4])
            h = act(lambda e: e.activation(ZTH[:, :, :], ps, ACT.Copy), a, zt_free)
            l = dve(lambda e: e.tensor_tensor(ZTL[:, :, :], ps, ZTH[:, :, :], ALU.subtract), h)
            free(4, 1, h, l)
            h1_free[x % 2] = a
            return [h, l]

        def third(x, zt):
            done = []
            for h in range(2):
                for k, part in enumerate(We[2][x][h]):
                    s = rows(bank(6 + h), ZTH, ZTL, every, part, (2 * k, 2 * k + 1), x == 0 and k == 0, x == 7 and k == 1, freed[6 + h] if x == 0 else None, zt)
                    W.release(part, s)
                    W.split()
                done.append(s)
            zt_free[:] = [s]
            return done

        sht_ok = {}

        def turn_shared(t):
            ps = bank(5).rearrange("p (k c) -> p k c", k=4)[:, :, 0:PT]

            def emit(e):
                for k in range(4):
                    ins = e.transpose(ps[:, k, :], S1[t][:, 128 * k:128 * k + 128], ident[0:PT, 0:PT])
                return ins
            a = pe(emit, sh_ok[t], freed[5])
            h = act(lambda e: e.activation(SHTH[:, :, cols(t)], ps, ACT.Copy), a, x3_all)
            l = dve(lambda e: e.tensor_tensor(SHTL[:, :, cols(t)], ps, SHTH[:, :, cols(t)], ALU.subtract), h)
            free(5, 1, h, l)
            s1_free.append(a)
            sht_ok[t] = [h, l]

        s1_free = []
        x3l_sem = [q.sem(f"x3l_sem{i}") for i in range(2)]
        x3l_free, so_done = [s1_free, s1_free], {}

        def shared_3(h, t):
            sl = slice(512 * h, 512 * h + 512)
            b = 4 + t % 2
            for k, part in enumerate(Ws3[h]):
                s = rows(bank(b)[0:PT, :], SHTH, SHTL, cols(t), part, (2 * k, 2 * k + 1), k == 0, k == 1, freed[b], sht_ok[t])
                if t == TT - 1:
                    W.release(part, s)
            W.split()
            i = t % 2
            l = dma("sync", x3l_sem[i], lambda e: e.dma_start(X3L[i][:, 512 * h:512 * h + 512], x3d[t * PT:(t + 1) * PT, sl]), x3l_free[i], x3_stored)
            a = dve(lambda e: e.tensor_tensor(SO[:, t, sl], bank(b)[0:PT, :], SB3[:, sl], ALU.add), s, sb3_ok, xt_dead)
            free(b, 1, a)
            c = dve(lambda e: e.scalar_tensor_tensor(SO[:, t, sl], SO[:, t, sl], scl[:, t:t + 1], X3L[i][:, 512 * h:512 * h + 512], op0=ALU.mult, op1=ALU.add), a, l, scl_ok)
            x3l_free[i] = c
            so_done[t, h] = c

        zt, z = {}, {}
        for x in range(8):
            g = gate(x)
            if x:
                zt[x - 1] = turn_z(x - 1, z[x - 1])
            if x < 2:
                turn_shared(2 * x)
            z[x] = hidden(x, g)
            if x < 2:
                turn_shared(2 * x + 1)
            if x:
                third(x - 1, zt[x - 1])
            if x == 3:
                scl_ok = token_scale()
            if x == 2:
                turn_shared(4)
                columns_ok = token_columns()
            if x in (3, 7):
                for t in range(TT):
                    shared_3(x // 4, t)
        zt[7] = turn_z(7, z[7])
        last = third(7, zt[7])

        em_ok = []
        for h in range(2):
            def weigh(h=h, sl=slice(512 * h, 512 * h + 512)):
                r = dve(lambda e: e.tensor_tensor(ER[:, sl], bank(6 + h), ER[:, sl], ALU.add), last[h], er_ok)
                m = act(lambda e: e.activation(EMH[:, sl], ER[:, sl], ACT.Copy, scale=se[:, 21:22]), r, weight_ok, xt_dead)
                em_ok.append(dve(lambda e: e.scalar_tensor_tensor(EML[:, sl], ER[:, sl], se[:, 21:22], EMH[:, sl], op0=ALU.mult, op1=ALU.subtract), m))
            weigh()
        for t in range(TT):
            for h in range(2):
                def last_rows(t=t, h=h, b=(2 * t + h) % 6, sl=slice(512 * h, 512 * h + 512)):
                    def emit(e):
                        for n, m in enumerate((EMH, EML)):
                            ins = e.matmul(bank(b)[0:PT, :], OHM[:, cols(t)], m[:, sl], start=n == 0, stop=n == 1)
                        return ins
                    s = pe(emit, em_ok[h], columns_ok, freed[b])
                    d = dve(lambda e: e.tensor_tensor(SO[:, t, sl], SO[:, t, sl], bank(b)[0:PT, :], ALU.add), s, so_done[t, h])
                    free(b, 1, d)
                    return d
                d = last_rows()
            dma("sync", x3s[t], lambda e, t=t: e.dma_start(out[t * PT:(t + 1) * PT, :], SO[:, t, :]), d)
        q.emit_all()


def half(np, w):
    k, n = w.shape
    return np.ascontiguousarray(w.reshape(k // 128, 128, n // 512, 512).transpose(2, 1, 0, 3)).reshape(n // 512, 128, k // 128 * 512)


def lay_out(np, I):
    P = {n: I[n] for n in ("x", "L0_gnn_bias", "L0_gnn_b_gate", "L1_gnn_b")}
    e = np.zeros((3, 164 * 128), np.int32)
    e[1], e[2] = 1023, 7
    for i, n in enumerate(("src", "dst", "edge_type_8")):
        e[i, :20000] = I[n]
    P["edges"] = np.ascontiguousarray(e.reshape(3, 164, 128).transpose(1, 0, 2))
    for p in ("L0_mix_", "L1_mix_"):
        for n in "qkvo":
            w = I[f"{p}W{n}"]
            P[f"{p}W{n}"] = half(np, w if p[1] == "0" else w.T)
            P[f"{p}b{n}"] = I[f"{p}b{n}"]
        P[f"{p}bq"] = np.ascontiguousarray(I[f"{p}bq"].reshape(8, 128).T)
    P["L0_gnn_root"] = half(np, I["L0_gnn_root"])
    P["L0_gnn_weight"] = np.stack([half(np, w) for w in I["L0_gnn_weight"]])
    P["L0_gnn_w_gate"] = np.stack([half(np, I["L0_gnn_w_gate"][:1024]), half(np, I["L0_gnn_w_gate"][1024:])])
    P["L1_gnn_W"] = half(np, I["L1_gnn_W"].T)
    for fs in ("k", "qv", "f"):
        nodes = np.zeros((len(fs), 256, 1024), np.float32)
        for i, f in enumerate(fs):
            nodes[i, :255] = I[f"L0_ffn_{f}_nw"]
        P[f"L0_ffn_{fs}_nw"] = np.ascontiguousarray(nodes.reshape(len(fs) * 256, 8, 128).transpose(2, 1, 0)).reshape(128, -1)
    nb = np.zeros((4, 256), np.float32)
    leaf = np.arange(32)
    for i, f in enumerate("kqvf"):
        p = f"L0_ffn_{f}_"
        nb[i, :255] = I[p + "nb"]
        P[p + "w1"] = np.ascontiguousarray(I[p + "w1"].reshape(8, 32, 8, 128, 16).transpose(0, 3, 2, 1, 4)).reshape(8, 128, 4096)
        P[p + "w2"] = np.ascontiguousarray(I[p + "w2"].reshape(8, 4, 128, 1024).transpose(0, 2, 1, 3)).reshape(8, 128, 4096)
        P[p + "b1"], P[p + "b2"] = I[p + "b1"].reshape(8, 512), I[p + "b2"]
        blocks = np.zeros((2, 4, 32, 32, 16), np.float32)
        blocks[:, :, leaf, leaf, :] = I[p + "b1"].reshape(2, 4, 32, 16)
        P[p + "bd"] = blocks.reshape(256, 512)
    P["L0_ffn_nb"] = nb.reshape(1024)
    f = "L1_ffn_"
    P[f + "index"] = np.ascontiguousarray(np.stack([I[f + "index_b"], I[f + "index_t"]], 1))
    for n in ("sw1", "sw2"):
        P[f + n] = half(np, I[f + n].T)[0]
    P[f + "sw3"] = half(np, I[f + "sw3"].T)
    for n in ("ew1", "ew2"):
        P[f + n] = np.stack([half(np, w.T)[0] for w in I[f + n]])
    P[f + "ew3"] = np.stack([half(np, w.T) for w in I[f + "ew3"]])
    for n in ("sb1", "sb2", "sb3", "s_ln_g", "s_ln_b", "eb1", "eb2", "eb3", "sel_ln_g", "sel_ln_b"):
        P[f + n] = I[f + n]
    gates = np.zeros((10, 1024), np.float32)
    gates[0:1], gates[1:9] = I[f + "sg_w"], I[f + "eg_w"]
    P[f + "gates"] = np.ascontiguousarray(gates.reshape(10, 8, 128).transpose(2, 1, 0)).reshape(128, 80)
    b = np.zeros(20, np.float32)
    b[0:1], b[1:9], b[10:18] = I[f + "sg_b"], I[f + "eg_b"], I[f + "exp_bias"]
    P[f + "gate_b"] = b
    return P


def kernel(**inputs):
    import numpy as np
    import concourse.bacc as bacc
    from concourse.bass_utils import run_bass_kernel_spmd

    laid = lay_out(np, {n: np.asarray(a) for n, a in inputs.items()})
    nc = bacc.Bacc("TRN2", target_bir_lowering=False, num_devices=1)
    arrays, A = {}, {}
    for name, a in laid.items():
        a = np.ascontiguousarray(a)
        arrays[f"in_{name}"] = a
        A[name] = nc.dram_tensor(f"in_{name}", a.shape, mybir.dt.from_np(a.dtype), kind="ExternalInput").ap()
    out = nc.dram_tensor("out_0", (N, D), F32, kind="ExternalOutput").ap()
    gps_layers(nc, A, out)
    r = run_bass_kernel_spmd(nc, [arrays], core_ids=[0])
    return r.results[0]["out_0"]
```
